# Optimizing a Trainium2 kernel written in Bass

```python
import numpy as np
import jax
import jax.numpy as jnp

def _softmax(x, axis=-1):
    return jax.nn.softmax(x, axis=axis)

def _gelu(x):
    return jax.nn.gelu(x, approximate=True)

def _silu(x):
    return jax.nn.silu(x)

def _sigmoid(x):
    return jax.nn.sigmoid(x)

def _layernorm(x, axis=-1, eps=1e-05):
    m = jnp.mean(x, axis=axis, keepdims=True)
    v = jnp.var(x, axis=axis, keepdims=True)
    return (x - m) / jnp.sqrt(v + eps)

def _scatter_add(tgt, idx, src, axis=0):
    return tgt.at[idx].add(src)

def _segment_sum(src, seg, n):
    return jax.ops.segment_sum(src, seg, n)
kernel_name = 'mk_recurrent_d1_jaxref_r8_fec977'

def setup_inputs(seed: int=0):
    np.random.seed(seed)
    _w = jnp.asarray

    def _L0_attn_setup():
        import jax, jax.numpy as jnp
        import numpy as np
        NUM_HEADS = 16
        LN_EPS = 1e-05
        key = jax.random.key(seed)
        ks = jax.random.split(key, 5)
        B, S, E = (4, 128, 128)
        x = jax.random.normal(ks[0], (B, S, E), dtype=jnp.float32)
        Wq = jax.random.normal(ks[1], (E, E), dtype=jnp.float32) * E ** (-0.5)
        Wk = jax.random.normal(ks[2], (E, E), dtype=jnp.float32) * E ** (-0.5)
        Wv = jax.random.normal(ks[3], (E, E), dtype=jnp.float32) * E ** (-0.5)
        Wo = jax.random.normal(ks[4], (E, E), dtype=jnp.float32) * E ** (-0.5)
        gamma = jnp.ones((E,), dtype=jnp.float32)
        beta = jnp.zeros((E,), dtype=jnp.float32)
        return {'x': x, 'Wq': Wq, 'Wk': Wk, 'Wv': Wv, 'Wo': Wo, 'gamma': gamma, 'beta': beta}
    _L0_attn_in = _L0_attn_setup()

    def _L0_ffn_setup():
        import jax, jax.numpy as jnp
        import numpy as np
        DIM = 128
        NQ = 16
        NKV = 4
        HD = DIM // NQ
        HID = 256
        E = 8
        B, S = (1, 128)
        EPS = 1e-06

        def rmsnorm(x, w):
            ms = jnp.mean(x * x, axis=-1, keepdims=True)
            return w * (x * jax.lax.rsqrt(ms + EPS))

        def rope_tables(seq_len, head_dim):
            inv_freq = 1.0 / 10000.0 ** (jnp.arange(0, head_dim, 2, dtype=jnp.float32) / head_dim)
            t = jnp.arange(seq_len, dtype=jnp.float32)
            freqs = jnp.einsum('i,j->ij', t, inv_freq)
            return (jnp.cos(freqs), jnp.sin(freqs))

        def apply_rope(x, cos, sin):
            c = cos[None, :, None, :]
            s = sin[None, :, None, :]
            half = x.shape[-1] // 2
            x1, x2 = (x[..., :half], x[..., half:])
            return jnp.concatenate([x1 * c - x2 * s, x1 * s + x2 * c], axis=-1)

        def _forward(x, ln1_w, ln2_w, Wq, bq, Wk, bk, Wv, bv, qn_w, kn_w, Wg, bg, Wo, bo, Wr, br, W1, b1, W2, b2):
            batch, seq, _ = x.shape
            cos, sin = rope_tables(seq, HD)
            h = rmsnorm(x, ln1_w)
            q = (h @ Wq + bq).reshape(batch, seq, NQ, HD)
            k = (h @ Wk + bk).reshape(batch, seq, NKV, HD)
            v = (h @ Wv + bv).reshape(batch, seq, NKV, HD)
            q = rmsnorm(apply_rope(q, cos, sin), qn_w)
            k = rmsnorm(apply_rope(k, cos, sin), kn_w)
            rep = NQ // NKV
            k = jnp.repeat(k, rep, axis=2)
            v = jnp.repeat(v, rep, axis=2)
            scores = jnp.einsum('bthd,bshd->bhts', q, k) / np.sqrt(HD)
            causal = jnp.tril(jnp.ones((seq, seq), dtype=bool))
            scores = jnp.where(causal[None, None], scores, -jnp.inf)
            attn = jax.nn.softmax(scores, axis=-1)
            out = jnp.einsum('bhts,bshd->bthd', attn, v)
            gate = jax.nn.sigmoid(out @ Wg + bg)
            out = (out * gate).reshape(batch, seq, DIM)
            x = x + out @ Wo + bo
            h2 = rmsnorm(x, ln2_w)
            logits = h2 @ Wr + br
            top1 = jnp.argmax(logits, axis=-1).reshape(-1)
            xt = h2.reshape(-1, DIM)
            u = jnp.einsum('td,edf->tef', xt, W1) + b1
            u1, u2 = (u[..., :HID], u[..., HID:])
            act = u1 * jax.nn.sigmoid(u2)
            y_all = jnp.einsum('teh,ehd->ted', act, W2) + b2
            y = jnp.take_along_axis(y_all, top1[:, None, None], axis=1)[:, 0, :]
            return x + y.reshape(batch, seq, DIM)
        key = jax.random.key(seed)
        ks = jax.random.split(key, 20)
        sc = lambda fan_in: 1.0 / np.sqrt(fan_in)
        d = {}
        d['x'] = jax.random.normal(ks[0], (B, S, DIM), dtype=jnp.float32)
        d['ln1_w'] = jnp.ones((DIM,), jnp.float32)
        d['ln2_w'] = jnp.ones((DIM,), jnp.float32)
        d['Wq'] = jax.random.normal(ks[1], (DIM, DIM), jnp.float32) * sc(DIM)
        d['bq'] = jnp.zeros((DIM,), jnp.float32)
        d['Wk'] = jax.random.normal(ks[2], (DIM, HD * NKV), jnp.float32) * sc(DIM)
        d['bk'] = jnp.zeros((HD * NKV,), jnp.float32)
        d['Wv'] = jax.random.normal(ks[3], (DIM, HD * NKV), jnp.float32) * sc(DIM)
        d['bv'] = jnp.zeros((HD * NKV,), jnp.float32)
        d['qn_w'] = jnp.ones((HD,), jnp.float32)
        d['kn_w'] = jnp.ones((HD,), jnp.float32)
        d['Wg'] = jax.random.normal(ks[4], (HD, HD), jnp.float32) * sc(HD)
        d['bg'] = jnp.zeros((HD,), jnp.float32)
        d['Wo'] = jax.random.normal(ks[5], (DIM, DIM), jnp.float32) * sc(DIM)
        d['bo'] = jnp.zeros((DIM,), jnp.float32)
        d['Wr'] = jax.random.normal(ks[6], (DIM, E), jnp.float32) * sc(DIM)
        d['br'] = jnp.zeros((E,), jnp.float32)
        d['W1'] = jax.random.normal(ks[7], (E, DIM, 2 * HID), jnp.float32) * sc(DIM)
        d['b1'] = jnp.zeros((E, 2 * HID), jnp.float32)
        d['W2'] = jax.random.normal(ks[8], (E, HID, DIM), jnp.float32) * sc(HID)
        d['b2'] = jnp.zeros((E, DIM), jnp.float32)
        return d
    _L0_ffn_in = _L0_ffn_setup()
    _d = {'L0_attn_x': _L0_attn_in['x'], 'L0_attn_Wq': _L0_attn_in['Wq'], 'L0_attn_Wk': _L0_attn_in['Wk'], 'L0_attn_Wv': _L0_attn_in['Wv'], 'L0_attn_Wo': _L0_attn_in['Wo'], 'L0_attn_gamma': _L0_attn_in['gamma'], 'L0_attn_beta': _L0_attn_in['beta'], 'L0_ffn_ln1_w': _L0_ffn_in['ln1_w'], 'L0_ffn_ln2_w': _L0_ffn_in['ln2_w'], 'L0_ffn_Wq': _L0_ffn_in['Wq'], 'L0_ffn_bq': _L0_ffn_in['bq'], 'L0_ffn_Wk': _L0_ffn_in['Wk'], 'L0_ffn_bk': _L0_ffn_in['bk'], 'L0_ffn_Wv': _L0_ffn_in['Wv'], 'L0_ffn_bv': _L0_ffn_in['bv'], 'L0_ffn_qn_w': _L0_ffn_in['qn_w'], 'L0_ffn_kn_w': _L0_ffn_in['kn_w'], 'L0_ffn_Wg': _L0_ffn_in['Wg'], 'L0_ffn_bg': _L0_ffn_in['bg'], 'L0_ffn_Wo': _L0_ffn_in['Wo'], 'L0_ffn_bo': _L0_ffn_in['bo'], 'L0_ffn_Wr': _L0_ffn_in['Wr'], 'L0_ffn_br': _L0_ffn_in['br'], 'L0_ffn_W1': _L0_ffn_in['W1'], 'L0_ffn_b1': _L0_ffn_in['b1'], 'L0_ffn_W2': _L0_ffn_in['W2'], 'L0_ffn_b2': _L0_ffn_in['b2']}
    _x0 = _d['L0_attn_x']
    _d['L0_attn_x'] = jax.random.normal(jax.random.fold_in(jax.random.key(seed), 1), (1, 2048, 128), dtype=_x0.dtype)
    del _x0
    return _d

def reference(L0_attn_x, L0_attn_Wq, L0_attn_Wk, L0_attn_Wv, L0_attn_Wo, L0_attn_gamma, L0_attn_beta, L0_ffn_ln1_w, L0_ffn_ln2_w, L0_ffn_Wq, L0_ffn_bq, L0_ffn_Wk, L0_ffn_bk, L0_ffn_Wv, L0_ffn_bv, L0_ffn_qn_w, L0_ffn_kn_w, L0_ffn_Wg, L0_ffn_bg, L0_ffn_Wo, L0_ffn_bo, L0_ffn_Wr, L0_ffn_br, L0_ffn_W1, L0_ffn_b1, L0_ffn_W2, L0_ffn_b2):

    def _L0_attn_ref(x, Wq, Wk, Wv, Wo, gamma, beta):
        import jax, jax.numpy as jnp
        import numpy as np
        NUM_HEADS = 16
        LN_EPS = 1e-05
        B, S, E = x.shape
        H = NUM_HEADS
        D = E // H
        scale = 1.0 / D ** 0.5
        q = x @ Wq.T
        k = x @ Wk.T * scale
        v = x @ Wv.T
        qh = q.reshape(B, S, H, D)
        kh = k.reshape(B, S, H, D)
        qk = jnp.einsum('bthd,bshd->bhts', qh, kh)
        causal = jnp.tril(jnp.ones((S, S), dtype=bool))
        qk = jnp.where(causal, qk, -jnp.inf)
        attn = jax.nn.softmax(qk, axis=-1)
        vh = v.reshape(B, S, D, H)
        qkv = jnp.einsum('bsdh,bhts->bthd', vh, attn)
        qkv = qkv.reshape(B, S, E)
        mu = jnp.mean(qkv, axis=-1, keepdims=True)
        var = jnp.mean(jnp.square(qkv - mu), axis=-1, keepdims=True)
        ln = (qkv - mu) * jax.lax.rsqrt(var + LN_EPS) * gamma + beta
        return ln @ Wo.T

    def _L0_ffn_ref(x, ln1_w, ln2_w, Wq, bq, Wk, bk, Wv, bv, qn_w, kn_w, Wg, bg, Wo, bo, Wr, br, W1, b1, W2, b2):
        import jax, jax.numpy as jnp
        import numpy as np
        DIM = 128
        NQ = 16
        NKV = 4
        HD = DIM // NQ
        HID = 256
        E = 8
        B, S = (1, 128)
        EPS = 1e-06

        def rmsnorm(x, w):
            ms = jnp.mean(x * x, axis=-1, keepdims=True)
            return w * (x * jax.lax.rsqrt(ms + EPS))

        def rope_tables(seq_len, head_dim):
            inv_freq = 1.0 / 10000.0 ** (jnp.arange(0, head_dim, 2, dtype=jnp.float32) / head_dim)
            t = jnp.arange(seq_len, dtype=jnp.float32)
            freqs = jnp.einsum('i,j->ij', t, inv_freq)
            return (jnp.cos(freqs), jnp.sin(freqs))

        def apply_rope(x, cos, sin):
            c = cos[None, :, None, :]
            s = sin[None, :, None, :]
            half = x.shape[-1] // 2
            x1, x2 = (x[..., :half], x[..., half:])
            return jnp.concatenate([x1 * c - x2 * s, x1 * s + x2 * c], axis=-1)

        def _forward(x, ln1_w, ln2_w, Wq, bq, Wk, bk, Wv, bv, qn_w, kn_w, Wg, bg, Wo, bo, Wr, br, W1, b1, W2, b2):
            batch, seq, _ = x.shape
            cos, sin = rope_tables(seq, HD)
            h = rmsnorm(x, ln1_w)
            q = (h @ Wq + bq).reshape(batch, seq, NQ, HD)
            k = (h @ Wk + bk).reshape(batch, seq, NKV, HD)
            v = (h @ Wv + bv).reshape(batch, seq, NKV, HD)
            q = rmsnorm(apply_rope(q, cos, sin), qn_w)
            k = rmsnorm(apply_rope(k, cos, sin), kn_w)
            rep = NQ // NKV
            k = jnp.repeat(k, rep, axis=2)
            v = jnp.repeat(v, rep, axis=2)
            scores = jnp.einsum('bthd,bshd->bhts', q, k) / np.sqrt(HD)
            causal = jnp.tril(jnp.ones((seq, seq), dtype=bool))
            scores = jnp.where(causal[None, None], scores, -jnp.inf)
            attn = jax.nn.softmax(scores, axis=-1)
            out = jnp.einsum('bhts,bshd->bthd', attn, v)
            gate = jax.nn.sigmoid(out @ Wg + bg)
            out = (out * gate).reshape(batch, seq, DIM)
            x = x + out @ Wo + bo
            h2 = rmsnorm(x, ln2_w)
            logits = h2 @ Wr + br
            top1 = jnp.argmax(logits, axis=-1).reshape(-1)
            xt = h2.reshape(-1, DIM)
            u = jnp.einsum('td,edf->tef', xt, W1) + b1
            u1, u2 = (u[..., :HID], u[..., HID:])
            act = u1 * jax.nn.sigmoid(u2)
            y_all = jnp.einsum('teh,ehd->ted', act, W2) + b2
            y = jnp.take_along_axis(y_all, top1[:, None, None], axis=1)[:, 0, :]
            return x + y.reshape(batch, seq, DIM)
        return _forward(x, ln1_w, ln2_w, Wq, bq, Wk, bk, Wv, bv, qn_w, kn_w, Wg, bg, Wo, bo, Wr, br, W1, b1, W2, b2)
    x = L0_attn_x
    xn = _layernorm(x, axis=-1)
    s = _L0_attn_ref(xn, L0_attn_Wq, L0_attn_Wk, L0_attn_Wv, L0_attn_Wo, L0_attn_gamma, L0_attn_beta)
    g = _silu(_L0_ffn_ref(xn, L0_ffn_ln1_w, L0_ffn_ln2_w, L0_ffn_Wq, L0_ffn_bq, L0_ffn_Wk, L0_ffn_bk, L0_ffn_Wv, L0_ffn_bv, L0_ffn_qn_w, L0_ffn_kn_w, L0_ffn_Wg, L0_ffn_bg, L0_ffn_Wo, L0_ffn_bo, L0_ffn_Wr, L0_ffn_br, L0_ffn_W1, L0_ffn_b1, L0_ffn_W2, L0_ffn_b2))
    x = x + s * g
    return x

_drawn_inputs = setup_inputs


def setup_inputs(seed=0):
    import zlib

    import numpy as np

    out = dict(_drawn_inputs(seed))
    spreads = {'L0_attn_gamma': (1.0, 0.2),
     'L0_attn_beta': (0.0, 0.1),
     'L0_ffn_ln1_w': (1.0, 0.2),
     'L0_ffn_ln2_w': (1.0, 0.2),
     'L0_ffn_bq': (0.0, 0.289),
     'L0_ffn_bk': (0.0, 0.449),
     'L0_ffn_bv': (0.0, 0.1),
     'L0_ffn_qn_w': (1.0, 0.2),
     'L0_ffn_kn_w': (1.0, 0.2),
     'L0_ffn_bg': (0.0, 0.8),
     'L0_ffn_bo': (0.0, 0.1),
     'L0_ffn_br': (0.0, 0.1),
     'L0_ffn_b1': (0.0, 0.1),
     'L0_ffn_b2': (0.0, 0.1)}
    factors = {}
    for name, (base, spread) in spreads.items():
        noise = np.random.default_rng([zlib.crc32(name.encode()), seed]).standard_normal(out[name].shape)
        drawn = base * np.exp(spread * noise) if base else spread * noise
        out[name] = jnp.asarray(drawn.astype(out[name].dtype))
    for name, factor in factors.items():
        out[name] = (out[name] * factor).astype(out[name].dtype)
    return out
```

```python
import numpy as np
from contextlib import ExitStack

import concourse.bass as bass
from concourse import mybir

F32 = mybir.dt.float32
BF16 = mybir.dt.bfloat16
ALU = mybir.AluOpType
ACT = mybir.ActivationFunctionType
AX = mybir.AxisListType.X

P = 128
S = 2048
T = S // P
NH, HD = 16, 8
NKV = 4
HG = 4
NG = 2 * NH // HG
CH = 512
NC = S // CH
BPC = CH // P
NE, HID = 8, 256
SCALE = float(HD) ** -0.5
PARTS = 3
STACK = PARTS * PARTS * HD
SHIFT = 96
NEG = -1.0e30

STEPS = [(c, kb) for c in range(NC) for kb in range(BPC * (c + 1))]
NS = len(STEPS)
TILES = 2 * NS
RING = 8
LAG = 1
ITEMS = [(qb, kc) for qb in range(T) for kc in range(qb // BPC + 1)]
UNITS = len(ITEMS) * HG
DIAG = 2 * T
ITEM_FIRST, ITEM_LAST = 6, 35
SHIFT_STEP = ITEM_LAST + 1

R_B1, R_GAMMA, R_BETA, R_LN1, R_LN2, R_BG = 0, 32, 33, 34, 35, 36
NROWS = 37


def items_at(s):
    if not ITEM_FIRST <= s <= ITEM_LAST:
        return []
    n = ITEM_LAST - ITEM_FIRST + 1
    a, b = ((s - ITEM_FIRST) * len(ITEMS) // n, (s - ITEM_FIRST + 1) * len(ITEMS) // n)
    return list(range(a, b))


def diag_index(s):
    return sum(1 for c, kb in STEPS[:s] if kb >= BPC * c)


U_W, U_X, U_P, U_S = 0, 2, 6, 22
NSRC = 16
B_L, B_O, B_S, B_G, B_W, B_H, B_R, B_T, B_END = 0, 4, 8, 12, 16, 20, 24, 25, 29
NW = 22 + NH + (NH + NKV) + NH
EX0, PV0 = 2, RING // 2
NLOAD = PARTS + PARTS * PARTS


def downs(k):
    return k + 1 + k // (2 * NE)


def build(nc, x, aWq, aWk, aWv, aWo, gamma, beta, ln1, ln2, Wq, bq, Wk, bk, Wv, bv, qn, kn, Wg, bg,
          Wo, bo, Wr, br, W1, b1, W2, b2, rope_cos, rope_sin, out):
    with ExitStack() as ctx:
        def sb(name, shape, dt=F32):
            return ctx.enter_context(nc.sbuf_tensor(name, shape, dt))

        def sem(name):
            return ctx.enter_context(nc.semaphore(name))

        XN = sb("XN", [P, T, P])
        XT = sb("XT", [P, S])
        QA = sb("QA", [P, 2, HG, S], BF16)
        KA = sb("KA", [P, 2, HG, S], BF16)
        PR = sb("PR", [P, RING, 2, CH])
        VX = sb("VX", [P, NG, T, HG * HD])
        VA = sb("VA", [P, 2, T, HG, 32])
        AO = sb("AO", [P, NG, T, HG * HD])
        W1S = sb("W1S", [P, NE, 2 * HID])
        W2S = sb("W2S", [P, NE, 2, P])
        WT = sb("WT", [P, 4, P])
        WN = sb("WN", [P, P + 192])
        WQKV = sb("WQKV", [P, 192])
        WO1 = sb("WO1", [P, P])
        WRS = sb("WRS", [P, NE])
        WG = sb("WG", [P, P])
        B2S = sb("B2S", [NE, P])
        ROWS = sb("ROWS", [NROWS, P])
        COLS = sb("COLS", [P, NROWS])
        QKVB = sb("QKVB", [P, 192])
        BOB = sb("BOB", [P, P])
        BRB = sb("BRB", [P, NE])
        QKN = sb("QKN", [P, NH + NKV, HD])
        COS = sb("COS", [P, T, HD // 2])
        SIN = sb("SIN", [P, T, HD // 2])
        ID = sb("ID", [P, P])
        IDB = sb("IDB", [P, P], BF16)
        CM = sb("CM", [P, P], BF16)
        SEL = sb("SEL", [NE, NE, P], BF16)
        RANK = sb("RANK", [P, NE])
        BN = sb("BN", [P, T, 6])
        MV = sb("MV", [P, T, 2])
        ST = sb("ST", [P, 8, T])
        MP = sb("MP", [P, HG * T, NC])
        NM = sb("NM", [P, HG * T])
        NMR = sb("NMR", [P, 2, HG * T], BF16)
        MROW = sb("MROW", [2 * HG * T, P], BF16)
        OT = sb("OT", [P, 2, CH])
        RL = sb("RL", [P, 2, BPC, HG])
        MX = sb("MX", [P, 2, T])

        SP3 = W2S[:, :, :, :].rearrange("p e m n -> p (e m n)")[:, 0:PARTS * CH].bitcast(BF16)\
            .rearrange("p (a i n) -> p a i n", a=2, i=PARTS)
        RES = OT
        prf = PR[:, :, :, :].rearrange("p a b c -> p (a b c)")
        SELF = prf[0:NE, 0:NE * P].rearrange("p (e n) -> p e n", e=NE)
        WIN = prf[:, 1024:1536].rearrange("p (a n) -> p a n", a=4)
        QF = prf[:, 0:4096].rearrange("p (a t n) -> p a t n", a=2, t=T)
        RT = prf[:, 4096:4096 + 2560].rearrange("p (t h d) -> p t h d", t=T, h=NH + NKV)
        RTMP = prf[:, 6656:6656 + 1280].rearrange("p (t h d) -> p t h d", t=T, h=NH + NKV)
        SQF = prf[:, 0:2560].rearrange("p (t h d) -> p t h d", t=T, h=NH + NKV)
        aof = AO[:, :, :, :].rearrange("p g t n -> p (g t n)")
        QKV1 = aof[:, 0:T * 192].rearrange("p (t n) -> p t n", t=T)
        HS = aof[:, T * 192:T * 192 + 3 * T * (NH + NKV)].rearrange("p (a n) -> p a n", a=3)
        qf = QA[:, :, :, :].rearrange("p a h s -> p (a h s)").bitcast(F32)
        kf = KA[:, :, :, :].rearrange("p a h s -> p (a h s)").bitcast(F32)
        vf = VA[:, :, :, :, :].rearrange("p a t h n -> p (a t h n)")
        OHT = vf[0:NE, 0:S]
        OHB = vf[0:NE, S:S + S // 2].bitcast(BF16)
        O1T, GT = qf[:, 0:S], qf[:, S:2 * S]
        X2 = qf[:, 2 * S:3 * S].rearrange("p (t n) -> p t n", t=T)
        H2 = qf[:, 3 * S:4 * S].rearrange("p (t n) -> p t n", t=T)
        LNO = kf[:, 0:S].rearrange("p (t n) -> p t n", t=T)
        XR = LNO
        LG = prf[:, 0:4 * T * NE].rearrange("p (a t e) -> p a t e", a=4, t=T)
        LNT = kf[:, S:2 * S]
        SO = kf[:, 2 * S:3 * S].rearrange("p (t n) -> p t n", t=T)
        YT = kf[:, 3 * S:4 * S]
        O2N = YT.rearrange("p (t n) -> p t n", t=T)

        PS = ctx.enter_context(nc.psum_tensor("PS", [P, 8, CH], F32))
        TB = PS[:, 7, :]
        TBH = PS[:, 7, :].bitcast(BF16)

        QP = nc.dram_tensor("q_parts", [NG, HG, PARTS, HD, S], BF16, kind="Internal").ap()
        KP = nc.dram_tensor("k_parts", [NG, HG, PARTS, HD, S], BF16, kind="Internal").ap()

        s_x = sem("x_loaded")
        s_seen = sem("probabilities_seen_by_pool")
        s_o2 = sem("second_output_regrouped")
        s_xr = sem("x_reloaded")
        s_w = sem("weights_loaded")
        s_moe = sem("moe_weights_loaded")
        s_const = sem("constants_built")
        s_zero = sem("stack_constants_built")
        s_v = sem("vector_chain")
        s_g = sem("pool_chain")
        s_a = sem("scalar_chain")
        s_var = sem("variances_ready")
        s_std = sem("deviations_ready")
        s_xn = sem("xn_ready")
        s_wn = sem("projection_weights_ready")
        s_qf = sem("q_normed")
        s_kf = sem("k_expanded")
        s_vx = sem("values_placed")
        s_ft = sem("front_bank_filled")
        s_fr = sem("front_bank_read")
        s_hi = sem("first_part_ready")
        s_mid = sem("second_part_ready")
        s_lo = sem("third_part_ready")
        s_wr = [sem("parts_written_0"), sem("parts_written_1")]
        s_ld = [sem("stack_loaded_0"), sem("stack_loaded_1")]
        s_va = sem("value_tiles_ready")
        s_sh = sem("shift_rows_loaded")
        s_sc = sem("scores_ready")
        s_ex = sem("probabilities_ready")
        s_mk = sem("probabilities_masked")
        s_pv = sem("value_products_done")
        s_mm = sem("max_scores_ready")
        s_mr = sem("max_scores_read")
        s_oe = sem("outputs_read")
        s_t = sem("transposes_ready")
        s_tr = sem("transposes_read")
        s_ch = sem("maxima_reduced")
        s_rl = sem("denominators_inverted")
        s_wgz = sem("gate_weight_zeroed")
        s_h2 = sem("ffn_tile_normed")
        s_nm = sem("shift_parts_ready")
        s_bt = sem("back_bank_filled")
        s_br = sem("back_bank_read")
        s_ln = sem("ln_operand_ready")
        s_sig = sem("gate_sigmoid_ready")
        s_oh = sem("onehot_ready")
        s_u = sem("expert_up_ready")
        s_us = sem("expert_sigmoid_ready")
        s_ua = sem("expert_act_ready")
        s_mb = sem("expert_mask_ready")
        s_dn = sem("expert_down_done")
        s_yt = sem("y_copied")
        s_yn = sem("y_turned")
        s_f = sem("ffn_out_ready")
        s_fs = sem("ffn_sigmoid_ready")
        s_o = sem("result_ready")
        s_out = sem("result_stored")

        def bcast_rows(v, n):
            return v.rearrange("(a n) -> a n", a=1).broadcast_to([P, n])

        def o_first(t):
            return AO[:, 0:NG // 2, t, :]

        block = ctx.enter_context(nc.Block())

        @block.sync
        def _(sp):
            xv = x[0].rearrange("(t p) n -> p t n", p=P)
            for c in range(4):
                sp.dma_start(XN[:, 4 * c:4 * c + 4, :], xv[:, 4 * c:4 * c + 4, :]).then_inc(s_x, 16)
            for n in range(NSRC):
                a, isk, c = n // 8, (n // 4) % 2, n % 4
                dst = KP if isk else QP
                sp.wait_ge(s_lo, n + 1)
                for i in range(PARTS):
                    sp.dma_start(
                        dst[4 * a:4 * a + 4, :, i, :, c * CH:(c + 1) * CH].rearrange("g h d s -> (g h) d s"),
                        SP3[:, n % 2, i, :]).then_inc(s_wr[n % 2], 16)
            for a in range(2):
                sp.wait_ge(s_wr[a], 16 * PARTS * NSRC // 2)

            def load_stacks(g, b):
                for i in range(PARTS):
                    sp.dma_start(KA[24 * i:24 * i + 24, b, :, :],
                                 KP[bass.ds(g, 1)].rearrange("o h j d s -> (o j d) h s")).then_inc(s_ld[b], 16)
                    for j in range(PARTS):
                        r = 24 * i + 8 * j
                        sp.dma_start(QA[r:r + 8, b, :, :],
                                     QP[bass.ds(g, 1), :, i].rearrange("o h d s -> (o d) h s")).then_inc(s_ld[b], 16)

            def shift_rows(g, b):
                sp.wait_ge(s_tr, 2 if isinstance(g, int) and g == 0 else 5 * g + 1)
                for i in range(2):
                    sp.dma_start(QA[SHIFT + i:SHIFT + i + 1, b, :, :].rearrange("o h (t s) -> o (h t) s", t=T),
                                 MROW[i * HG * T:(i + 1) * HG * T, :]).then_inc(s_sh, 16)

            sp.wait_ge(s_zero, 1)
            load_stacks(0, 0)
            load_stacks(1, 1)
            shift_rows(0, 0)
            sp.dma_start(W1S[:, :, :], W1.rearrange("e d f -> d e f")).then_inc(s_moe, 16)
            sp.dma_start(W2S[:, :, :, :], W2.rearrange("e (m p) d -> p e m d", p=P)).then_inc(s_moe, 16)

            def group(g, b, load, shift):
                if shift:
                    shift_rows(g + 1, 1 - b)
                if load:
                    sp.wait_ge(s_pv, PV0 + NS * (g + 1))
                    load_stacks(g + 2, b)

            with sp.Fori(0, NG // 2 - 1) as i:
                group(2 * i, 0, True, True)
                group(2 * i + 1, 1, True, True)
            group(NG - 2, 0, False, True)

            sp.wait_ge(s_bt, B_L + NC)
            sp.dma_start(XR[:, :, :], xv).then_inc(s_xr, 16)
            ov = out[0].rearrange("(t p) n -> p t n", p=P)
            for c in range(NC):
                sp.wait_ge(s_o, c + 1)
                sp.dma_start(ov[:, 4 * c:4 * c + 4, :], H2[:, 4 * c:4 * c + 4, :]).then_inc(s_out, 16)
            sp.wait_ge(s_out, 16 * NC)

        @block.gpsimd
        def _(gp):
            n = [0]

            def link(ins):
                n[0] += 1
                ins.then_inc(s_g, 1)
                gp.wait_ge(s_g, n[0])

            for m in (ID, IDB, CM):
                link(gp.memset(m[:, :], 0.0))
            for m in (ID, IDB):
                link(gp.affine_select(out=m[:, :], in_=m[:, :], compare_op=ALU.not_equal, fill=1.0, base=0,
                                      pattern=[[-1, P]], channel_multiplier=1))
            link(gp.affine_select(out=CM[:, :], in_=CM[:, :], compare_op=ALU.is_ge, fill=NEG, base=0,
                                  pattern=[[-1, P]], channel_multiplier=1))
            link(gp.memset(SELF[:, :, :], 1.0))
            link(gp.affine_select(out=SELF[:, :, :], in_=SELF[:, :, :], compare_op=ALU.is_equal, fill=0.0, base=0,
                                  pattern=[[-1, NE], [0, P]], channel_multiplier=1))
            link(gp.tensor_copy(SEL[:, :, :], SELF[:, :, :]))
            for e in range(NE):
                link(gp.memset(RANK[:, e:e + 1], float(NE - e)))
            gp.sem_inc(s_const, 1)
            link(gp.memset(QA[:, :, :, :].rearrange("p a h s -> p (a h s)").bitcast(F32), 0.0))
            link(gp.memset(KA[:, :, :, :].rearrange("p a h s -> p (a h s)").bitcast(F32), 0.0))
            link(gp.memset(KA[SHIFT:SHIFT + 2, :, :, :].rearrange("p a h s -> p (a h s)"), 1.0))
            gp.sem_inc(s_zero, 1)
            link(gp.memset(VA[:, :, :, :, :].rearrange("p a t h n -> p (a t h) n"), 0.0))
            link(gp.memset(VA[:, :, :, :, HD:HD + 1].rearrange("p a t h n -> p (a t h) n"), 1.0))

            gp.wait_ge(s_fr, U_S)
            for g in range(NKV):
                v = QKV1[:, :, 160 + g * HD:160 + (g + 1) * HD]
                for hh in range(HG):
                    gp.tensor_copy(VX[:, NKV + g, :, hh * HD:(hh + 1) * HD], v).then_inc(s_vx, 1)
            gp.wait_ge(s_qf, 1)
            for h in range(NH):
                gp.tensor_copy(QF[:, 1, :, h * HD:(h + 1) * HD],
                               RT[:, :, NH + h // HG, :]).then_inc(s_kf, 1)
            gp.wait_ge(s_fr, U_P)
            gp.wait_ge(s_w, 16 * NW)
            for t in range(T):
                gp.tensor_tensor(XN[:, t, :], XN[:, t, :], BOB[:, :], ALU.add).then_inc(s_kf, 1)

            def build_values(g, b):
                gp.tensor_copy(VA[:, b, :, :, 0:HD],
                               VX[:, bass.ds(g, 1), :, :].rearrange("p o t (h d) -> p (o t) h d", h=HG))\
                  .then_inc(s_va, 1)

            gp.wait_ge(s_vx, NH)
            build_values(0, 0)
            build_values(1, 1)

            def group(g, b, load):
                for s, (c, kb) in enumerate(STEPS):
                    if kb < BPC * c:
                        continue
                    for p in range(2):
                        tile = 2 * s + p
                        gp.wait_ge(s_ex, EX0 + TILES * g + tile + 1)
                        v = PR[:, tile % RING, :, 0:P]
                        gp.sem_inc(s_seen, 1)
                        gp.affine_select(out=v, in_=v, compare_op=ALU.is_ge, fill=0.0, base=0,
                                         pattern=[[0, 2], [1, P]], channel_multiplier=-1).then_inc(s_mk, 1)
                if load:
                    gp.wait_ge(s_pv, PV0 + NS * (g + 1))
                    build_values(g + 2, b)

            with gp.Fori(0, NG // 2 - 1) as i:
                group(2 * i, 0, True)
                group(2 * i + 1, 1, True)
            group(NG - 2, 0, False)
            group(NG - 1, 1, False)
            gp.wait_ge(s_tr, 1 + 5 * NG)
            gp.wait_ge(s_pv, PV0 + NS * NG)
            gp.tensor_copy(O2N.rearrange("p t (g n) -> p t g n", g=4),
                           AO[:, NG // 2:NG, :, :].rearrange("p g t n -> p t g n")).then_inc(s_o2, 1)

        @block.scalar
        def _(act):
            for dst, src in ((WIN[:, 0, :], aWq), (WIN[:, 1, :], aWk), (WIN[:, 2, :], aWv), (WIN[:, 3, :], aWo),
                             (WQKV[:, 0:128], Wq), (WQKV[:, 128:160], Wk), (WQKV[:, 160:192], Wv),
                             (ROWS[R_B1:R_B1 + 32, :], b1.rearrange("e (m p) -> (e m) p", p=P)),
                             (ROWS[R_GAMMA:R_GAMMA + 1, :], gamma.rearrange("(a n) -> a n", a=1)),
                             (ROWS[R_BETA:R_BETA + 1, :], beta.rearrange("(a n) -> a n", a=1)),
                             (ROWS[R_LN1:R_LN1 + 1, :], ln1.rearrange("(a n) -> a n", a=1)),
                             (ROWS[R_LN2:R_LN2 + 1, :], ln2.rearrange("(a n) -> a n", a=1)),
                             (QKVB[:, 0:128], bcast_rows(bq, 128)), (QKVB[:, 128:160], bcast_rows(bk, 32)),
                             (QKVB[:, 160:192], bcast_rows(bv, 32)), (BOB[:, :], bcast_rows(bo, 128)),
                             (BRB[:, :], bcast_rows(br, NE)),
                             (COS[:, :, :], rope_cos.rearrange("(t p) n -> p t n", p=P)),
                             (SIN[:, :, :], rope_sin.rearrange("(t p) n -> p t n", p=P)),
                             (WO1[:, :], Wo), (WRS[:, :], Wr), (B2S[:, :], b2)):
                act.dma_start(dst, src).then_inc(s_w, 16)
            for h in range(NH):
                act.dma_start(ROWS[R_BG:R_BG + 1, h * HD:(h + 1) * HD],
                              bg.rearrange("(a n) -> a n", a=1)).then_inc(s_w, 16)
            for h in range(NH + NKV):
                act.dma_start(QKN[:, h, :], bcast_rows(qn if h < NH else kn, HD)).then_inc(s_w, 16)
            act.wait_ge(s_wgz, 1)
            for h in range(NH):
                act.dma_start(WG[h * HD:(h + 1) * HD, h * HD:(h + 1) * HD], Wg).then_inc(s_w, 16)

            act.sem_inc(s_ex, EX0)

            for k in range(2):
                act.wait_ge(s_var, k + 1)
                act.activation(ST[:, 2 * k + 1, :], ST[:, 2 * k, :], ACT.Sqrt).then_inc(s_std, 1)
            def split(n):
                bank, c = (U_S + n) % 8, SCALE if (n // 4) % 2 == 1 else 1.0
                act.wait_ge(s_ft, U_S + n + 1)
                if n >= 2:
                    act.wait_ge(s_wr[n % 2], 16 * PARTS * (n // 2))
                act.activation(SP3[:, n % 2, 0, :], PS[:, bank, :], ACT.Copy, scale=c).then_inc(s_hi, 1)
                act.wait_ge(s_fr, U_S + n + 1)
                act.activation(SP3[:, n % 2, 1, :], RES[:, n % 2, :], ACT.Copy).then_inc(s_mid, 1)

            act.wait_ge(s_var, 3)
            act.activation(HS[:, 1, :], HS[:, 0, :], ACT.Sqrt).then_inc(s_std, 1)
            for n in range(NSRC):
                split(n)

            def group(g):
                for s, (c, kb) in enumerate(STEPS):
                    q0 = max(0, kb - BPC * c) * P
                    for p in range(2):
                        tile = 2 * s + p
                        if p == 0:
                            act.wait_ge(s_pv, NS * g + s + 1)
                        act.wait_ge(s_sc, TILES * g + tile + 1)
                        act.activation(PR[:, tile % RING, :, 0:CH - q0],
                                       PS[:, 2 * p:2 * p + 2, 0:CH - q0], ACT.Exp).then_inc(s_ex, 1)

            with act.Fori(0, NG // 2 - 1) as i:
                group(2 * i)
                group(2 * i + 1)
            group(NG - 2)
            group(NG - 1)

            act.wait_ge(s_var, 4)
            act.activation(ST[:, 5, :], ST[:, 4, :], ACT.Sqrt).then_inc(s_std, 1)
            for c in range(NC):
                act.wait_ge(s_bt, B_G + c + 1)
                act.activation(PR[:, c, 0, :], PS[:, (B_G + c) % 8, :], ACT.Sigmoid,
                               bias=COLS[:, R_BG:R_BG + 1]).then_inc(s_sig, 1)
            act.wait_ge(s_var, 5)
            act.activation(ST[:, 7, :], ST[:, 6, :], ACT.Sqrt).then_inc(s_std, 1)
            act.wait_ge(s_br, B_END)
            for c in range(NC):
                for e in range(NE):
                    for m in range(2):
                        k = (c * NE + e) * 2 + m
                        act.wait_ge(s_u, k + 1)
                        if k >= 2:
                            act.wait_ge(s_ua, 2 * (k - 1))
                        act.activation(PR[:, k % 2, 0, :], PS[:, 2 * (k % 2) + 1, :], ACT.Sigmoid,
                                       bias=COLS[:, R_B1 + 4 * e + 2 + m:R_B1 + 4 * e + 3 + m]).then_inc(s_us, 1)
                act.wait_ge(s_f, c + 1)
                act.activation(H2[:, 4 * c:4 * c + 4, :], X2[:, 4 * c:4 * c + 4, :], ACT.Sigmoid).then_inc(s_fs, 1)

        @block.tensor
        def _(pe):
            def front(u):
                if u >= 8:
                    pe.wait_ge(s_fr, u - 7)
                return PS[:, u % 8, :]

            pe.wait_ge(s_const, 1)
            pe.wait_ge(s_w, 16 * NW)
            bank = front(U_W)
            for k in range(4):
                last = pe.transpose(bank[:, k * P:(k + 1) * P], WIN[:, k, :], ID[:, :])
            last.then_inc(s_ft, 1)
            bank = front(U_W + 1)
            pe.transpose(bank[:, 0:NROWS], ROWS[:, :], ID[0:NROWS, 0:NROWS]).then_inc(s_ft, 1)
            pe.wait_ge(s_xn, T)
            for c in range(NC):
                bank = front(U_X + c)
                for k in range(BPC):
                    last = pe.transpose(bank[:, k * P:(k + 1) * P], XN[:, 4 * c + k, :], ID[:, :])
                last.then_inc(s_ft, 1)
            pe.wait_ge(s_wn, 1)
            pe.wait_ge(s_fr, U_P)
            for t in range(T):
                bank = front(U_P + t)
                pe.matmul(bank[:, 0:P + 192], XT[:, t * P:(t + 1) * P], WN[:, :], start=True, stop=True)\
                  .then_inc(s_ft, 1)
            for n in range(8):
                bank = front(U_S + n)
                pe.matmul(bank, WT[:, n // 4, :], XT[:, (n % 4) * CH:(n % 4 + 1) * CH], start=True, stop=True)\
                  .then_inc(s_ft, 1)
            pe.wait_ge(s_qf, 2)
            for n in range(8, 16):
                if n == 12:
                    pe.wait_ge(s_kf, NH)
                bank = front(U_S + n)
                for k in range(BPC):
                    last = pe.transpose(bank[:, k * P:(k + 1) * P], QF[:, (n - 8) // 4, 4 * (n % 4) + k, :], ID[:, :])
                last.then_inc(s_ft, 1)
            pe.wait_ge(s_fr, U_S + NSRC)

            def max_unit(g, b, item, hh):
                qb, kc = ITEMS[item]
                u = item * HG + hh
                diag = kc == qb // BPC
                w = (qb % BPC + 1) * P if diag else CH
                bank = PS[:, 4 + u % 2, :]
                pe.wait_ge(s_mr, UNITS * g + u + 1)
                last = pe.matmul(bank[:, 0:w], QA[0:SHIFT, b, hh, qb * P:(qb + 1) * P],
                                 KA[0:SHIFT, b, hh, kc * CH:kc * CH + w], start=True, stop=not diag)
                if diag:
                    last = pe.matmul(bank[:, w - P:w], IDB[:, :], CM[:, :], start=False, stop=True)
                last.then_inc(s_mm, 1)

            def shift_turn(g):
                pe.wait_ge(s_nm, g + 1)
                use = 5 * g - 1 if not (isinstance(g, int) and g == 0) else 0
                pe.wait_ge(s_tr, use + 1)
                pe.transpose(TBH[:, 0:P], NMR[:, :, :].rearrange("p a n -> p (a n)"), IDB[:, :]).then_inc(s_t, 1)

            pe.wait_ge(s_ld[0], 16 * NLOAD)
            for item in range(len(ITEMS)):
                for hh in range(HG):
                    max_unit(0, 0, item, hh)
            shift_turn(0)

            def group(g, b, loads, last_group):
                pe.wait_ge(s_sh, 32 * (g + 1))
                pe.wait_ge(s_va, g + 1)

                def scores(s):
                    c, kb = STEPS[s]
                    q0 = max(0, kb - BPC * c) * P
                    for p in range(2):
                        pe.wait_ge(s_ex, TILES * g + 2 * s + p + 1)
                        for i in range(2):
                            last = pe.matmul(PS[:, 2 * p + i, 0:CH - q0],
                                             KA[:, b, 2 * p + i, kb * P:(kb + 1) * P],
                                             QA[:, b, 2 * p + i, c * CH + q0:(c + 1) * CH], start=True, stop=True)
                        last.then_inc(s_sc, 1)

                def values(s):
                    c, kb = STEPS[s]
                    q0 = max(0, kb - BPC * c) * P
                    if kb == 0:
                        pe.wait_ge(s_oe, NC * g + c + 1)
                    if kb >= BPC * c:
                        pe.wait_ge(s_mk, DIAG * g + 2 * diag_index(s + 1))
                    pe.wait_ge(s_ex, EX0 + TILES * g + 2 * s + 2)
                    for hh in range(HG):
                        last = pe.matmul(PS[32 * hh:32 * hh + 32, 6, q0:CH], VA[:, b, kb, hh, :],
                                         PR[:, (2 * s + hh // 2) % RING, hh % 2, 0:CH - q0],
                                         start=kb == 0, stop=kb == BPC * (c + 1) - 1)
                    last.then_inc(s_pv, 1)

                def turn(c):
                    use = 5 * g + 1 + (c if c < 3 else 4)
                    if last_group and c == 3:
                        use = 5 * g + 4
                    pe.wait_ge(s_oe, NC * g + c + 2)
                    pe.wait_ge(s_tr, use + 1)
                    for k in range(BPC):
                        last = pe.transpose(TB[:, k * P:(k + 1) * P], OT[:, c % 2, k * P:(k + 1) * P], ID[:, :])
                    last.then_inc(s_t, 1)

                for s in range(NS + LAG + 1):
                    if s < NS:
                        scores(s)
                        if not last_group:
                            if s == ITEM_FIRST:
                                pe.wait_ge(s_ld[1 - b], 16 * NLOAD * loads)
                            for item in items_at(s):
                                for hh in range(HG):
                                    max_unit(g + 1, 1 - b, item, hh)
                    if LAG <= s < NS + LAG:
                        values(s - LAG)
                    if s > LAG and STEPS[s - LAG - 1][1] == BPC * (STEPS[s - LAG - 1][0] + 1) - 1:
                        turn(STEPS[s - LAG - 1][0])
                    if s == SHIFT_STEP and not last_group:
                        shift_turn(g + 1)

            with pe.Fori(0, NG // 2 - 1) as i:
                group(2 * i, 0, i + 1, False)
                group(2 * i + 1, 1, i + 2, False)
            group(NG - 2, 0, NG // 2, False)
            group(NG - 1, 1, None, True)

            def back(u):
                if u >= 8:
                    pe.wait_ge(s_br, u - 7)
                return PS[:, u % 8, :]

            pe.wait_ge(s_tr, 1 + 5 * NG)
            pe.wait_ge(s_ln, T)
            for c in range(NC):
                bank = back(B_L + c)
                for k in range(BPC):
                    last = pe.transpose(bank[:, k * P:(k + 1) * P], LNO[:, 4 * c + k, :], ID[:, :])
                last.then_inc(s_bt, 1)
            pe.wait_ge(s_o2, 1)
            for c in range(NC):
                bank = back(B_O + c)
                for k in range(BPC):
                    last = pe.transpose(bank[:, k * P:(k + 1) * P], O2N[:, 4 * c + k, :], ID[:, :])
                last.then_inc(s_bt, 1)
            for c in range(NC):
                pe.wait_ge(s_br, B_L + c + 1)
                bank = back(B_S + c)
                for k in range(BPC):
                    t = 4 * c + k
                    last = pe.matmul(bank[:, k * P:(k + 1) * P], LNT[:, t * P:(t + 1) * P], WT[:, 3, :],
                                     start=True, stop=True)
                last.then_inc(s_bt, 1)
            for c in range(NC):
                pe.wait_ge(s_br, B_O + c + 1)
                bank = back(B_G + c)
                pe.matmul(bank, WG[:, :], O1T[:, c * CH:(c + 1) * CH], start=True, stop=True).then_inc(s_bt, 1)
            for c in range(NC):
                pe.wait_ge(s_br, B_G + c + 1)
                bank = back(B_W + c)
                for k in range(BPC):
                    t = 4 * c + k
                    last = pe.matmul(bank[:, k * P:(k + 1) * P], GT[:, t * P:(t + 1) * P], WO1[:, :],
                                     start=True, stop=True)
                last.then_inc(s_bt, 1)
            for c in range(NC):
                pe.wait_ge(s_h2, 4 * (c + 1))
                bank = back(B_H + c)
                for k in range(BPC):
                    last = pe.transpose(bank[:, k * P:(k + 1) * P], H2[:, 4 * c + k, :], ID[:, :])
                last.then_inc(s_bt, 1)
            pe.wait_ge(s_br, B_R)
            bank = back(B_R)
            for t in range(T):
                last = pe.matmul(bank[:, t * NE:(t + 1) * NE], XT[:, t * P:(t + 1) * P], WRS[:, :],
                                 start=True, stop=True)
            last.then_inc(s_bt, 1)
            pe.wait_ge(s_oh, 1)
            for c in range(NC):
                bank = back(B_T + c)
                for k in range(BPC):
                    last = pe.transpose(bank[0:NE, k * P:(k + 1) * P], LG[:, 3, 4 * c + k, :], ID[:, :])
                last.then_inc(s_bt, 1)
            pe.wait_ge(s_br, B_END)
            pe.wait_ge(s_moe, 32)
            units = [(c, e, m) for c in range(NC) for e in range(NE) for m in range(2)]

            def up(k):
                c, e, m = units[k]
                if k >= 2:
                    pe.wait_ge(s_ua, 2 * (k - 1))
                if m == 0:
                    if k >= 4:
                        pe.wait_ge(s_ua, 2 * (k - 2))
                    pe.matmul(PS[:, 4 + (k // 2) % 2, :], SEL[:, e, :], OHB[:, c * CH:(c + 1) * CH],
                              start=True, stop=True).then_inc(s_mb, 1)
                for v in range(2):
                    last = pe.matmul(PS[:, 2 * (k % 2) + v, :], W1S[:, e, v * HID + m * P:v * HID + (m + 1) * P],
                                     XT[:, c * CH:(c + 1) * CH], start=True, stop=True)
                last.then_inc(s_u, 1)

            def down(k):
                c, e, m = units[k]
                pe.wait_ge(s_ua, 2 * (k + 1))
                if e == 0 and m == 0 and c >= 1:
                    pe.wait_ge(s_yt, c)
                last = pe.matmul(PS[:, 6, :], W2S[:, e, m, :], PR[:, 4 + k % 2, 0, :],
                                 start=e == 0 and m == 0, stop=False)
                last.then_inc(s_dn, 1)
                if e == NE - 1 and m == 1:
                    pe.matmul(PS[:, 6, :], B2S[:, :], OHT[:, c * CH:(c + 1) * CH], start=False, stop=True)\
                      .then_inc(s_dn, 1)

            for k in range(len(units) + 1):
                if k < len(units):
                    up(k)
                if k >= 1:
                    down(k - 1)
                    c, e, m = units[k - 1]
                    if e == NE - 1 and m == 1:
                        pe.wait_ge(s_yt, c + 1)
                        if c >= 1:
                            pe.wait_ge(s_f, c)
                        for j in range(BPC):
                            last = pe.transpose(PS[:, 7, j * P:(j + 1) * P],
                                                YT[:, (4 * c + j) * P:(4 * c + j + 1) * P], ID[:, :])
                        last.then_inc(s_yn, 1)

        @block.vector
        def _(dve):
            n = [0]

            def link(ins):
                n[0] += 1
                ins.then_inc(s_v, 1)
                dve.wait_ge(s_v, n[0])

            dve.wait_ge(s_const, 1)
            dve.memset(WG[:, :], 0.0).then_inc(s_wgz, 1)
            link(dve.memset(MP[:, :, :], NEG))
            dve.sem_inc(s_pv, PV0)
            dve.sem_inc(s_mr, 2)
            dve.sem_inc(s_oe, 1)
            dve.sem_inc(s_tr, 1)

            def moments(src):
                for t in range(T):
                    last = dve.bn_stats(BN[:, t, :], src(t))
                link(last)
                for t in range(T):
                    last = dve.bn_aggr(MV[:, t, :], BN[:, t, :])
                link(last)

            dve.wait_ge(s_x, 64)
            moments(lambda t: XN[:, t, :])
            dve.tensor_scalar(ST[:, 0, :], MV[:, :, 1], 1e-5, None, ALU.add).then_inc(s_var, 1)
            dve.wait_ge(s_std, 1)
            link(dve.reciprocal(ST[:, 1, :], ST[:, 1, :]))
            for t in range(T):
                dve.tensor_scalar(XN[:, t, :], XN[:, t, :], MV[:, t, 0:1], ST[:, 1, t:t + 1],
                                  ALU.subtract, ALU.mult).then_inc(s_xn, 1)
            link(dve.tensor_tensor(ST[:, 2, :], ST[:, 1, :], ST[:, 1, :], ALU.mult))
            link(dve.tensor_tensor(ST[:, 2, :], ST[:, 2, :], MV[:, :, 1], ALU.mult))
            dve.tensor_scalar(ST[:, 2, :], ST[:, 2, :], 1e-6, None, ALU.add).then_inc(s_var, 1)
            dve.wait_ge(s_std, 2)
            link(dve.reciprocal(ST[:, 3, :], ST[:, 3, :]))

            dve.wait_ge(s_ft, U_W + 1)
            dve.tensor_copy(WT[:, :, :].rearrange("p a n -> p (a n)"), PS[:, U_W, :]).then_inc(s_fr, 1)
            dve.wait_ge(s_ft, U_W + 2)
            dve.tensor_copy(COLS[:, :], PS[:, U_W + 1, 0:NROWS]).then_inc(s_fr, 1)
            dve.wait_ge(s_fr, 2)
            dve.tensor_copy(WN[:, 0:P], WT[:, 2, :])
            dve.tensor_scalar(WN[:, P:P + 192], WQKV[:, :], COLS[:, R_LN1:R_LN1 + 1], None, ALU.mult)\
               .then_inc(s_wn, 1)
            for c in range(NC):
                dve.wait_ge(s_ft, U_X + c + 1)
                dve.tensor_copy(XT[:, c * CH:(c + 1) * CH], PS[:, (U_X + c) % 8, :]).then_inc(s_fr, 1)
            for t in range(T):
                bank = PS[:, (U_P + t) % 8, :]
                dve.wait_ge(s_ft, U_P + t + 1)
                dve.tensor_copy(VX[:, 0:4, t, :].rearrange("p g (h d) -> p g h d", h=HG),
                                bank[:, 0:P].rearrange("p (d g h) -> p g h d", d=HD, g=4))
                dve.scalar_tensor_tensor(QKV1[:, t, :], bank[:, P:P + 192], ST[:, 3, t:t + 1], QKVB[:, :],
                                         ALU.mult, ALU.add).then_inc(s_fr, 1)
            dve.wait_ge(s_fr, U_S)

            def split(k):
                bank, c = PS[:, (U_S + k) % 8, :], SCALE if (k // 4) % 2 == 1 else 1.0
                dve.wait_ge(s_hi, k + 1)
                dve.scalar_tensor_tensor(RES[:, k % 2, :], bank, c, SP3[:, k % 2, 0, :], ALU.mult, ALU.subtract)\
                   .then_inc(s_fr, 1)
                dve.wait_ge(s_mid, k + 1)
                dve.tensor_tensor(SP3[:, k % 2, 2, :], RES[:, k % 2, :], SP3[:, k % 2, 1, :], ALU.subtract)\
                   .then_inc(s_lo, 1)

            h2 = HD // 2
            qk = QKV1[:, :, 0:160].rearrange("p t (h d) -> p t h d", d=HD)
            x1, x2 = qk[:, :, :, 0:h2], qk[:, :, :, h2:HD]
            cos = COS[:, :, :].unsqueeze(2).broadcast_to([P, T, NH + NKV, h2])
            sin = SIN[:, :, :].unsqueeze(2).broadcast_to([P, T, NH + NKV, h2])
            r1, r2, tmp = RT[:, :, :, 0:h2], RT[:, :, :, h2:HD], RTMP[:, :, :, :]
            link(dve.tensor_tensor(r1, x1, cos, ALU.mult))
            link(dve.tensor_tensor(tmp, x2, sin, ALU.mult))
            link(dve.tensor_tensor(r1, r1, tmp, ALU.subtract))
            link(dve.tensor_tensor(r2, x1, sin, ALU.mult))
            link(dve.tensor_tensor(tmp, x2, cos, ALU.mult))
            link(dve.tensor_tensor(r2, r2, tmp, ALU.add))
            link(dve.tensor_tensor(SQF[:, :, :, :], RT[:, :, :, :], RT[:, :, :, :], ALU.mult))
            hs = HS[:, 0, :].rearrange("p (t h) -> p t h", t=T)
            link(dve.tensor_reduce(hs, SQF[:, :, :, :], AX, ALU.add))
            dve.tensor_scalar(HS[:, 0, :], HS[:, 0, :], 1.0 / HD, 1e-6, ALU.mult, ALU.add).then_inc(s_var, 1)
            dve.wait_ge(s_std, 3)
            link(dve.reciprocal(HS[:, 2, :], HS[:, 1, :]))
            rr = HS[:, 2, :].rearrange("p (t h) -> p t h", t=T).unsqueeze(3).broadcast_to([P, T, NH + NKV, HD])
            link(dve.tensor_tensor(RT[:, :, :, :], RT[:, :, :, :], rr, ALU.mult))
            wk = QKN[:, NH:NH + NKV, :].unsqueeze(1).broadcast_to([P, T, NKV, HD])
            dve.tensor_tensor(RT[:, :, NH:NH + NKV, :], RT[:, :, NH:NH + NKV, :], wk, ALU.mult).then_inc(s_qf, 1)
            wq = QKN[:, 0:NH, :].unsqueeze(1).broadcast_to([P, T, NH, HD])
            dve.tensor_tensor(QF[:, 0, :, :].rearrange("p t (h d) -> p t h d", d=HD), RT[:, :, 0:NH, :], wq,
                              ALU.mult).then_inc(s_qf, 1)
            for k in range(NSRC):
                split(k)

            def max_unit(g, item, hh):
                qb, kc = ITEMS[item]
                u = item * HG + hh
                w = (qb % BPC + 1) * P if kc == qb // BPC else CH
                dve.wait_ge(s_mm, UNITS * g + u + 1)
                dve.reduce_max(MP[:, hh * T + qb, kc:kc + 1], PS[:, 4 + u % 2, 0:w], AX).then_inc(s_mr, 1)

            def shift_parts(g):
                dve.wait_ge(s_mr, 2 + UNITS * (g + 1))
                dve.tensor_reduce(NM[:, :], MP[:, :, :], AX, ALU.max, negate=True).then_inc(s_ch, 1)
                dve.wait_ge(s_ch, 2 * g + 1)
                dve.tensor_copy(NMR[:, 0, :], NM[:, :]).then_inc(s_ch, 1)
                dve.wait_ge(s_ch, 2 * g + 2)
                dve.tensor_tensor(NMR[:, 1, :], NM[:, :], NMR[:, 0, :], ALU.subtract).then_inc(s_nm, 1)

            def shift_read(g):
                use = 5 * g - 1 if not (isinstance(g, int) and g == 0) else 0
                dve.wait_ge(s_t, use + 1)
                if not (isinstance(g, int) and g == 0):
                    dve.wait_ge(s_sh, 32 * g)
                dve.tensor_copy(MROW[:, :], TBH[:, 0:P]).then_inc(s_tr, 1)

            for item in range(len(ITEMS)):
                for hh in range(HG):
                    max_unit(0, item, hh)
            shift_parts(0)
            shift_read(0)

            def group(g, last_group):
                def copy_out(c):
                    end = max(s for s in range(NS) if STEPS[s][0] == c)
                    dve.wait_ge(s_pv, PV0 + NS * g + end + 1)
                    dve.tensor_copy(OT[:, c % 2, :], PS[:, 6, :]).then_inc(s_oe, 1)

                def normalise(c):
                    use = 5 * g + 1 + (c if c < 3 else 4)
                    if last_group and c == 3:
                        use = 5 * g + 4
                    dve.wait_ge(s_t, use + 1)
                    o = TB.rearrange("p (k h n) -> p k h n", k=BPC, h=HG)
                    dve.reciprocal(RL[:, c % 2, :, :], o[:, :, :, HD]).then_inc(s_rl, 1)
                    dve.wait_ge(s_rl, NC * g + c + 1)
                    dve.tensor_tensor(
                        AO[:, bass.ds(g, 1), 4 * c:4 * c + 4, :].rearrange("p o t (h d) -> p (o t) h d", h=HG),
                        o[:, :, :, 0:HD], RL[:, c % 2, :, :].unsqueeze(3).broadcast_to([P, BPC, HG, HD]),
                        ALU.mult).then_inc(s_tr, 1)

                for s in range(NS + LAG + 1):
                    if s < NS and not last_group:
                        for item in items_at(s):
                            for hh in range(HG):
                                max_unit(g + 1, item, hh)
                    if s == SHIFT_STEP - 1 and not last_group:
                        shift_parts(g + 1)
                    if s > LAG and STEPS[s - LAG - 1][1] == BPC * (STEPS[s - LAG - 1][0] + 1) - 1:
                        normalise(STEPS[s - LAG - 1][0])
                    if LAG <= s < NS + LAG:
                        c, kb = STEPS[s - LAG]
                        if kb == BPC * (c + 1) - 1:
                            copy_out(c)
                    if s == SHIFT_STEP and not last_group:
                        shift_read(g + 1)

            with dve.Fori(0, NG // 2 - 1) as i:
                group(2 * i, False)
                group(2 * i + 1, False)
            group(NG - 2, False)
            group(NG - 1, True)

            dve.wait_ge(s_tr, 1 + 5 * NG)
            dve.wait_ge(s_pv, PV0 + NS * NG)
            moments(o_first)
            dve.tensor_scalar(ST[:, 4, :], MV[:, :, 1], 1e-5, None, ALU.add).then_inc(s_var, 1)
            dve.wait_ge(s_std, 4)
            link(dve.reciprocal(ST[:, 5, :], ST[:, 5, :]))
            for t in range(T):
                dve.tensor_scalar(LNO[:, t, :].rearrange("p (g n) -> p g n", g=4), o_first(t), MV[:, t, 0:1],
                                  ST[:, 5, t:t + 1], ALU.subtract, ALU.mult).then_inc(s_ln, 1)
            for c in range(NC):
                dve.wait_ge(s_bt, B_L + c + 1)
                dve.tensor_scalar(LNT[:, c * CH:(c + 1) * CH], PS[:, (B_L + c) % 8, :],
                                  COLS[:, R_GAMMA:R_GAMMA + 1], COLS[:, R_BETA:R_BETA + 1],
                                  ALU.mult, ALU.add).then_inc(s_br, 1)
            for c in range(NC):
                dve.wait_ge(s_bt, B_O + c + 1)
                dve.tensor_copy(O1T[:, c * CH:(c + 1) * CH], PS[:, (B_O + c) % 8, :]).then_inc(s_br, 1)
            for c in range(NC):
                dve.wait_ge(s_bt, B_S + c + 1)
                dve.tensor_copy(SO[:, 4 * c:4 * c + 4, :].rearrange("p t n -> p (t n)"), PS[:, (B_S + c) % 8, :])\
                   .then_inc(s_br, 1)
            for c in range(NC):
                dve.wait_ge(s_sig, c + 1)
                dve.tensor_tensor(GT[:, c * CH:(c + 1) * CH], O1T[:, c * CH:(c + 1) * CH], PR[:, c, 0, :],
                                  ALU.mult).then_inc(s_br, 1)
            for c in range(NC):
                dve.wait_ge(s_bt, B_W + c + 1)
                dve.wait_ge(s_kf, NH + T)
                dve.tensor_tensor(X2[:, 4 * c:4 * c + 4, :].rearrange("p t n -> p (t n)"), PS[:, (B_W + c) % 8, :],
                                  XN[:, 4 * c:4 * c + 4, :].rearrange("p t n -> p (t n)"), ALU.add).then_inc(s_br, 1)
            dve.wait_ge(s_br, B_H)
            for t in range(T):
                last = dve.tensor_tensor(H2[:, t, :], X2[:, t, :], X2[:, t, :], ALU.mult)
            link(last)
            link(dve.tensor_reduce(ST[:, 6, :], H2[:, :, :], AX, ALU.add))
            dve.tensor_scalar(ST[:, 6, :], ST[:, 6, :], 1.0 / P, 1e-6, ALU.mult, ALU.add).then_inc(s_var, 1)
            dve.wait_ge(s_std, 5)
            link(dve.reciprocal(ST[:, 7, :], ST[:, 7, :]))
            for t in range(T):
                dve.tensor_scalar(H2[:, t, :], X2[:, t, :], ST[:, 7, t:t + 1], None, ALU.mult).then_inc(s_h2, 1)
            for c in range(NC):
                dve.wait_ge(s_bt, B_H + c + 1)
                dve.tensor_scalar(XT[:, c * CH:(c + 1) * CH], PS[:, (B_H + c) % 8, :],
                                  COLS[:, R_LN2:R_LN2 + 1], None, ALU.mult).then_inc(s_br, 1)
            dve.wait_ge(s_bt, B_R + 1)
            lg = LG[:, 0, :, :]
            brb = BRB[:, :].unsqueeze(1).broadcast_to([P, T, NE])
            rank = RANK[:, :].unsqueeze(1).broadcast_to([P, T, NE])
            dve.tensor_tensor(lg, PS[:, B_R % 8, 0:T * NE].rearrange("p (t e) -> p t e", t=T), brb, ALU.add)\
               .then_inc(s_br, 1)
            dve.wait_ge(s_br, B_R + 1)
            link(dve.tensor_reduce(MX[:, 0, :], lg, AX, ALU.max))
            mx = MX[:, 0, :].unsqueeze(2).broadcast_to([P, T, NE])
            link(dve.tensor_tensor(LG[:, 1, :, :], lg, mx, ALU.is_equal))
            link(dve.tensor_tensor(LG[:, 2, :, :], LG[:, 1, :, :], rank, ALU.mult))
            link(dve.tensor_reduce(MX[:, 1, :], LG[:, 2, :, :], AX, ALU.max))
            mx1 = MX[:, 1, :].unsqueeze(2).broadcast_to([P, T, NE])
            dve.tensor_tensor(LG[:, 3, :, :], LG[:, 2, :, :], mx1, ALU.is_equal).then_inc(s_oh, 1)
            for c in range(NC):
                dve.wait_ge(s_bt, B_T + c + 1)
                dve.tensor_copy(OHT[:, c * CH:(c + 1) * CH], PS[0:NE, (B_T + c) % 8, :])
                dve.tensor_copy(OHB[:, c * CH:(c + 1) * CH], PS[0:NE, (B_T + c) % 8, :]).then_inc(s_br, 1)

            for c in range(NC):
                for e in range(NE):
                    for m in range(2):
                        k = (c * NE + e) * 2 + m
                        dve.wait_ge(s_us, k + 1)
                        dve.wait_ge(s_u, k + 1)
                        dve.scalar_tensor_tensor(PR[:, 2 + k % 2, 0, :], PS[:, 2 * (k % 2), :],
                                                 COLS[:, R_B1 + 4 * e + m:R_B1 + 4 * e + m + 1], PR[:, k % 2, 0, :],
                                                 ALU.add, ALU.mult).then_inc(s_ua, 1)
                        dve.wait_ge(s_ua, 2 * k + 1)
                        dve.wait_ge(s_mb, k // 2 + 1)
                        if k >= 2:
                            dve.wait_ge(s_dn, downs(k - 2))
                        dve.tensor_tensor(PR[:, 4 + k % 2, 0, :], PR[:, 2 + k % 2, 0, :], PS[:, 4 + (k // 2) % 2, :],
                                          ALU.mult).then_inc(s_ua, 1)
                dve.wait_ge(s_dn, (2 * NE + 1) * (c + 1))
                dve.tensor_copy(YT[:, c * CH:(c + 1) * CH], PS[:, 6, :]).then_inc(s_yt, 1)
                dve.wait_ge(s_yn, c + 1)
                x2 = X2[:, 4 * c:4 * c + 4, :].rearrange("p t n -> p (t n)")
                dve.tensor_tensor(x2, x2, PS[:, 7, :], ALU.add).then_inc(s_f, 1)
                dve.wait_ge(s_fs, c + 1)
                so = SO[:, 4 * c:4 * c + 4, :].rearrange("p t n -> p (t n)")
                hh_ = H2[:, 4 * c:4 * c + 4, :].rearrange("p t n -> p (t n)")
                link(dve.tensor_tensor(hh_, hh_, x2, ALU.mult))
                link(dve.tensor_tensor(hh_, hh_, so, ALU.mult))
                dve.wait_ge(s_xr, 16)
                dve.tensor_tensor(hh_, hh_, XR[:, 4 * c:4 * c + 4, :].rearrange("p t n -> p (t n)"), ALU.add)\
                   .then_inc(s_o, 1)


_INS = ['L0_attn_x', 'L0_attn_Wq', 'L0_attn_Wk', 'L0_attn_Wv', 'L0_attn_Wo', 'L0_attn_gamma', 'L0_attn_beta',
        'L0_ffn_ln1_w', 'L0_ffn_ln2_w', 'L0_ffn_Wq', 'L0_ffn_bq', 'L0_ffn_Wk', 'L0_ffn_bk', 'L0_ffn_Wv',
        'L0_ffn_bv', 'L0_ffn_qn_w', 'L0_ffn_kn_w', 'L0_ffn_Wg', 'L0_ffn_bg', 'L0_ffn_Wo', 'L0_ffn_bo',
        'L0_ffn_Wr', 'L0_ffn_br', 'L0_ffn_W1', 'L0_ffn_b1', 'L0_ffn_W2', 'L0_ffn_b2']


def rope_tables():
    inv = (np.float32(1.0) / np.float32(10000.0) ** (np.arange(0, HD, 2, dtype=np.float32) / np.float32(HD)))
    f = np.arange(S, dtype=np.float32)[:, None] * inv.astype(np.float32)[None, :]
    return np.cos(f).astype(np.float32), np.sin(f).astype(np.float32)


def kernel(**inputs):
    import concourse.bacc as _bacc
    from concourse.bass_utils import run_bass_kernel_spmd as _run

    nc = _bacc.Bacc("TRN2", target_bir_lowering=False, num_devices=1)
    cos, sin = rope_tables()
    named = [(name, np.ascontiguousarray(inputs[name])) for name in _INS] + [("rope_cos", cos), ("rope_sin", sin)]
    arrays, args = {}, []
    for name, a in named:
        arrays[f"in_{name}"] = a
        args.append(nc.dram_tensor(f"in_{name}", a.shape, mybir.dt.from_np(a.dtype), kind="ExternalInput").ap())
    out = nc.dram_tensor("out_0", (1, S, P), F32, kind="ExternalOutput").ap()
    build(nc, *args, out)
    r = _run(nc, [arrays], core_ids=[0])
    return r.results[0]["out_0"]
```

```python
import numpy as np
from contextlib import ExitStack

import concourse.bass as bass
from concourse import mybir

F32 = mybir.dt.float32
BF16 = mybir.dt.bfloat16
I32 = mybir.dt.int32
U32 = mybir.dt.uint32
ALU = mybir.AluOpType
ACT = mybir.ActivationFunctionType
AX = mybir.AxisListType.X

P = 128
S = 2048
T = S // P
NH, HD = 16, 8
NKV = 4
HG = 4
NA = NH // HG
NG = 2 * NA
CH = 512
NC = S // CH
BPC = CH // P
NE, HID = 8, 256
SCALE = float(HD) ** -0.5
PARTS = 3
STACK = PARTS * PARTS * HD
SHIFT = 96
NEG = -1.0e30
BOUND = 80.0

ORDER = list(range(NC))[::-1]
STEPS = [(c, kb) for c in ORDER for kb in range(BPC * (c + 1))]
NS = len(STEPS)
TILES = 2 * NS
RING = 8
LAG = 2
ITEMS = [(qb, kc) for qb in range(BPC, T)[::-1] for kc in range(1, qb // BPC + 1)[::-1]]
ITEMS += [(qb, 0) for qb in range(BPC, T)[::-1]]
LATE_ITEMS = len(ITEMS)
FIRST_NEEDED = next(i for i, (qb, kc) in enumerate(ITEMS) if kc == 0)
ITEMS += [(qb, 0) for qb in range(BPC)]
UNITS = len(ITEMS) * HG
DIAG = 2 * T
EARLY = NS - BPC - 1

SLOT_GROUP = [0, 1, NA, 2, NA + 1, 3, NA + 2, NA + 3]
FFN_BESIDE = "ffn"
PAIRS = NG // 2 - 1
HEAD = 4
LAST_MAX = NS - 6
SHIFT_PARTS, SHIFT_TURN = LAST_MAX + 1, LAST_MAX + 3


def place(i, side):
    return i + (NA - 1) * (1 - side)


def step_width(s):
    c, kb = STEPS[s]
    return CH - max(0, kb - BPC * c) * P


def item_width(i):
    qb, kc = ITEMS[i]
    return (qb % BPC + 1) * P if kc == qb // BPC else CH


def spread(steps):
    total, work = sum(step_width(s) for s in steps), HG * sum(map(item_width, range(len(ITEMS))))
    out, u, done, own = [], 0, 0, 0
    for n, s in enumerate(steps):
        own += step_width(s)
        mine = []
        while u < UNITS and (n == len(steps) - 1 or done * total < own * work):
            mine.append((u // HG, u % HG))
            done += item_width(u // HG)
            u += 1
        out.append(mine)
    return out


PAIR_STEPS = [s for s in range(HEAD, NS)] + [s for s in range(LAST_MAX + 1)]
PAIR_SPREAD = spread(PAIR_STEPS)
SPREAD = {"first": [[]] * HEAD + PAIR_SPREAD[:NS - HEAD],
          "second": PAIR_SPREAD[NS - HEAD:] + [[]] * (NS - LAST_MAX - 1),
          "whole": [[]] * HEAD + spread(range(HEAD, LAST_MAX + 1)) + [[]] * (NS - LAST_MAX - 1),
          "none": [[]] * NS}


def maxima_of(peeled, side):
    return ("whole", "none")[side] if peeled else ("first", "second")[side]


def units_at(kind, s):
    u = SPREAD[kind][s] if s < NS else []
    a = (len(u) + 3) // 4
    b = a + (len(u) + 2) // 4
    return u[:a], u[a:b], u[b:]


def takes_shift(peeled, side):
    return side == (0 if peeled else 1)


def stream(i, peeled, stage):
    for s in range(HEAD, NS):
        stage(i, 0, s, peeled)
    for s in range(NS):
        stage(i, 1, s, peeled)
    for s in range(HEAD):
        if not peeled:
            stage(i, 2, s, peeled)
    for s in range(NS, NS + LAG + 1):
        if peeled:
            stage(i, 1, s, peeled)


def behind(side, s, d):
    return (side, s - d) if s >= d else (side - 1, s - d + NS)


def chunk_end(c):
    return max(s for s in range(NS) if STEPS[s][0] == c)


def ending(s):
    return next((c for c in ORDER if chunk_end(c) == s), None)


def turn_use(i, side, c, peeled):
    k = ORDER.index(c)
    later = takes_shift(peeled, side) and chunk_end(c) + LAG + 1 > SHIFT_TURN
    return (2 * NC + 1) * i + (NC + (1 if peeled else 0)) * side + k + (1 if later else 0)


def shift_use(i, peeled):
    before = sum(1 for c in ORDER if chunk_end(c) + LAG + 1 <= SHIFT_TURN)
    return (2 * NC + 1) * i + (0 if peeled else NC) + before


USES = NC * NG + NA


def diag_index(s):
    return sum(1 for c, kb in STEPS[:s] if kb >= BPC * c)


R_GAMMA, R_BETA, R_LN1, R_LN2, R_BG, R_QN, R_KN = range(7)
NROWS = 7


U_W, U_X, U_A, U_P, U_F = 0, 2, 6, 14, 30
NSRC = 16
SLOTS = 4
FFN_AT = {2: ("C", 0), 4: ("O", 0), 5: ("O", 1), 6: ("G", 0), 7: ("G", 1), 8: ("O", 2), 9: ("W", 0), 10: ("G", 2),
          11: ("O", 3), 12: ("W", 1), 13: ("G", 3), 14: ("W", 2), 15: ("H", 0), 16: ("W", 3), 17: ("H", 1),
          18: ("H", 2), 19: ("H", 3), 20: ("R", 0), 21: ("K", 0)}
FFN_USE = {work: n for n, work in enumerate(FFN_AT.values())}
MOVE_AT = {22: (0, 1, 2), 23: (3,), 28: (4, 5, 6), 29: (7, 8, 9), 30: (10, 11, 12), 31: (13, 14, 15)}

NT = S // P + NE
ROW = P + 1
YRING = 4
SIDE_AT = {-1: ("X", 0), 0: ("X", 1), 3: ("X", 2), 6: ("X", 3), 8: ("L", 0), 9: ("L", 1), 10: ("X", 4),
           11: ("L", 2), 12: ("L", 3), 13: ("S", 0), 14: ("X", 5), 15: ("S", 1), 16: ("S", 2), 17: ("S", 3)}
SIDE_USE = {work: n for n, work in enumerate(SIDE_AT.values())}
EX0, PV0 = 2, RING // 2
NLOAD = 2 * PARTS


def source_use(n):
    return U_A + n if n < NSRC // 2 else U_F + n - NSRC // 2


def reads(u):
    return u + 1 if u < U_X else u + 1 - NC


def build(nc, x, aWq, aWk, aWv, aWo, gamma, beta, ln1, ln2, Wq, bq, Wk, bk, Wv, bv, qn, kn, Wg, bg,
          Wo, bo, Wr, br, W1, b1, W2, b2, rope_cos, rope_sin, out):
    with ExitStack() as ctx:
        def sb(name, shape, dt=F32):
            return ctx.enter_context(nc.sbuf_tensor(name, shape, dt))

        def sem(name):
            return ctx.enter_context(nc.semaphore(name))

        XN = sb("XN", [P, T, P])
        MB = sb("MB", [P, 2, HG, S], BF16)
        QA = sb("QA", [P, 2, HG, S], BF16)
        KA = sb("KA", [P, 2, HG, S], BF16)
        PR = sb("PR", [P, RING, 2, CH])
        VX = sb("VX", [P, NG, T, HG * HD])
        VA = sb("VA", [P, 2, T, HG, 32])
        AO = sb("AO", [P, NG, T, HG * HD])
        WT = sb("WT", [P, 4, P])
        WN = sb("WN", [P, P + 192])
        WQKV = sb("WQKV", [P, 192])
        WO1 = sb("WO1", [P, P])
        WRS = sb("WRS", [P, NE])
        WG = sb("WG", [P, P])
        ROWS = sb("ROWS", [R_QN, P])
        COLS = sb("COLS", [P, NROWS])
        QKVB = sb("QKVB", [P, 192])
        BOB = sb("BOB", [P, P])
        BRB = sb("BRB", [P, NE])
        QKN = sb("QKN", [P, 2, HD])
        COS = sb("COS", [P, T, HD // 2])
        SIN = sb("SIN", [P, T, HD // 2])
        ID = sb("ID", [P, P])
        IDB = sb("IDB", [P, P], BF16)
        CM = sb("CM", [P, P], BF16)
        TRI = sb("TRI", [P, P])
        ONES = sb("ONES", [P, P])
        ZERO = sb("ZERO", [P, ROW])
        J128 = sb("J128", [P, NT])
        TILE = sb("TILE", [P, NT])
        BEFORE = sb("BEFORE", [P, NE, NE])
        OWN = sb("OWN", [PARTS * NE, NE])
        B12 = sb("B12", [PARTS * NE, 5 * P], BF16)
        CNT = sb("CNT", [P, 4, NE])
        TOK = sb("TOK", [P, T])
        SPARE = sb("SPARE", [P, NT])
        POSF = sb("POSF", [P, T])
        POS = sb("POS", [P, T], U32)
        EIDF = sb("EIDF", [P, NT])
        EID = sb("EID", [P, NT], I32)
        YIF = sb("YIF", [P, NT])
        YI = sb("YI", [P, NT], U32)
        RANK = sb("RANK", [P, NE])
        QKM = sb("QKM", [P, 2])
        KNS = sb("KNS", [P, 1])
        MHALF = sb("MHALF", [P, T])
        HBG = sb("HBG", [P, 1])
        QNX = sb("QNX", [1, 2, P])
        BN = sb("BN", [P, T, 6])
        MV = sb("MV", [P, T, 2])
        ST = sb("ST", [P, 8, T])
        MP = sb("MP", [P, HG * T, NC])
        NM = sb("NM", [P, HG * T])
        NMR = sb("NMR", [P, 2, HG * T], BF16)
        MROW = sb("MROW", [2 * HG * T, P], BF16)
        OT = sb("OT", [P, 2, CH])
        RL = sb("RL", [P, 2, BPC, HG])
        MX = sb("MX", [P, 2, T])

        mbf = MB[:, :, :, :].rearrange("p a h s -> p (a h s)").bitcast(F32)
        W1S = mbf[:, 0:4096].rearrange("p (e n) -> p e n", e=NE)
        W2S = mbf[:, 4096:6144].rearrange("p (e m n) -> p e m n", e=NE, m=2)
        XT = mbf[:, 6144:8192]
        XTF = mbf[:, 0:S]
        SP3 = mbf[:, 4096:4096 + SLOTS * PARTS * CH // 2].bitcast(BF16)\
            .rearrange("p (a i n) -> p a i n", a=SLOTS, i=PARTS)
        RES = OT
        prf = PR[:, :, :, :].rearrange("p a b c -> p (a b c)")
        WIN = prf[:, 1024:1536].rearrange("p (a n) -> p a n", a=4)
        QF = prf[:, 0:4096].rearrange("p (a t n) -> p a t n", a=2, t=T)
        RT = prf[:, 5120:5120 + 2560].rearrange("p (t h d) -> p t h d", t=T, h=NH + NKV)
        RTMP = prf[:, 2560:2560 + 2560].rearrange("p (a t h d) -> p a t h d", a=2, t=T, h=NH + NKV)
        SQF = prf[:, 0:2560].rearrange("p (t h d) -> p t h d", t=T, h=NH + NKV)
        aof = AO[:, :, :, :].rearrange("p g t n -> p (g t n)")
        QKV1 = aof[:, 0:T * 192].rearrange("p (t n) -> p t n", t=T)
        HS = aof[:, T * 192:T * 192 + 3 * T * (NH + NKV)].rearrange("p (a n) -> p a n", a=3)
        def quarters(stack, b):
            f = stack[:, b, :, :].rearrange("p h s -> p (h s)").bitcast(F32)
            return f[:, 0:S], f[:, S:2 * S]

        def by_tile(f):
            return f.rearrange("p (t n) -> p t n", t=T)

        OG, O1T = quarters(QA, 0)
        O2N = by_tile(OG)
        qa0 = QA[:, 0, :, :].rearrange("p h s -> p (h s)").bitcast(F32)
        H2 = qa0[:, 0:T * ROW].rearrange("p (t n) -> p t n", t=T)
        XS = qa0[:, 0:NT * ROW].rearrange("p (t n) -> p t n", t=NT)
        X2, RS = map(by_tile, quarters(KA, 0))
        GE = VA[:, 0, :, :, :].rearrange("p t h n -> p (t h n)")
        SQ = by_tile(GE)
        BF = GE[0:NE, 0:5 * P]
        BP = GE[0:NE, 5 * P:5 * P + 5 * P * PARTS // 2].bitcast(BF16).rearrange("p (i n) -> p i n", i=PARTS)
        LG = GE[:, 0:4 * T * NE].rearrange("p (a t e) -> p a t e", a=4, t=T)
        TE = GE[0:PARTS * NE, 4 * T * NE:4 * T * NE + NT * P // 2].bitcast(BF16)\
            .rearrange("p (j n) -> p j n", j=NT)
        EQ = XT[:, 0:NT * NE].rearrange("p (j e) -> p j e", j=NT)
        XG = QA[:, 1, :, :].rearrange("p h s -> p (h s)").bitcast(F32)[:, 0:NT * P]
        LNO_, LNT = quarters(KA, 1)
        LNO = by_tile(LNO_)
        SO = LNO
        XR = XN
        SG = prf[:, 0:2 * HID].rearrange("p (a n) -> p a n", a=2)
        UA = prf[:, 512:512 + 2 * HID].rearrange("p (a n) -> p a n", a=2)
        UT = prf[:, 1024:1024 + 2 * HID].rearrange("p (a n) -> p a n", a=2)
        YS = prf[:, 1536:1536 + YRING * P].rearrange("p (a n) -> p a n", a=YRING)
        YN = by_tile(prf[:, 2048:2048 + S])

        PS = ctx.enter_context(nc.psum_tensor("PS", [P, 8, CH], F32))
        TB = PS[:, 7, :]
        TBH = PS[:, 7, :].bitcast(BF16)

        def parts_tensor(name, tokens):
            return nc.dram_tensor(name, [PARTS, NG, HD, HG, tokens], BF16, kind="Internal").ap()

        QP = {"first": parts_tensor("q_first", CH), "late": parts_tensor("q_late", S - CH)}
        KP = {"first": parts_tensor("k_first", CH), "late": parts_tensor("k_late", S - CH)}
        SH = nc.dram_tensor("shift_rows", [NG, 2, HG, T, P], BF16, kind="Internal").ap()

        XGD = nc.dram_tensor("expert_tokens", [NT * P, ROW], F32, kind="Internal").ap()
        YD = nc.dram_tensor("expert_outputs", [S + NT * P, P], F32, kind="Internal").ap()

        s_x = [sem(f"x_loaded_{c}") for c in range(NC)]
        s_seen = sem("probabilities_seen_by_pool")
        s_o2 = sem("second_output_regrouped")
        s_xr = sem("x_reloaded")
        s_w = sem("projection_weights_loaded")
        s_rw = sem("rope_and_norm_weights_loaded")
        s_wl = sem("later_weights_loaded")
        s_qx = sem("norm_weight_rows_ready")
        s_res = sem("remainder_ready")
        s_r2 = sem("second_halves_rotated")
        s_id = sem("identity_built")
        s_xt = sem("xn_turned")
        s_vc = sem("first_values_placed")
        s_sq = sem("q_and_k_squared")
        s_moe = sem("moe_weights_loaded")
        s_const = sem("constants_built")
        s_zero = sem("stack_constants_built")
        s_v = sem("vector_chain")
        s_g = sem("pool_chain")
        s_a = sem("scalar_chain")
        s_var = sem("variances_ready")
        s_std = sem("deviations_ready")
        s_xn = sem("xn_ready")
        s_wn = sem("projection_weights_ready")
        s_qf = sem("q_normed")
        s_kf = sem("k_expanded")
        s_vx = sem("values_placed")
        s_ft = sem("front_bank_filled")
        s_fr = sem("front_bank_read")
        s_hi = sem("first_part_ready")
        s_mid = sem("second_part_ready")
        s_lo = sem("third_part_ready")
        s_wr = [sem(f"parts_written_{a}") for a in range(SLOTS)]
        s_ld = [sem("stack_loaded_0"), sem("stack_loaded_1")]
        s_late = [sem("later_tokens_loaded_0"), sem("later_tokens_loaded_1")]
        s_ml = sem("max_stacks_late_loaded")
        s_mf = sem("max_stacks_first_loaded")
        s_shw = sem("shift_rows_stored")
        s_cr = sem("constant_shift_ready")
        s_va = sem("value_tiles_ready")
        s_sc = sem("scores_ready")
        s_ex = sem("probabilities_ready")
        s_mk = sem("probabilities_masked")
        s_pv = sem("value_products_done")
        s_mm = sem("max_scores_ready")
        s_mr = sem("max_scores_read")
        s_oe = sem("outputs_read")
        s_t = sem("transposes_ready")
        s_tr = sem("transposes_read")
        s_ch = sem("maxima_reduced")
        s_rl = sem("denominators_inverted")
        s_wgz = sem("gate_weight_zeroed")
        s_h2 = sem("ffn_tile_normed")
        s_nm = sem("shift_parts_ready")
        s_ff = sem("ffn_bank_filled")
        s_fu = sem("ffn_bank_read")
        s_ms = sem("ffn_mean_squares_ready")
        s_rs = sem("ffn_scales_ready")
        s_gt = sem("gated_output_ready")
        s_ng = sem("gate_bias_halved")
        s_bt = sem("back_bank_filled")
        s_br = sem("back_bank_read")
        s_ln = sem("ln_operand_ready")
        s_sig = sem("gate_sigmoid_ready")
        s_oh = sem("onehot_ready")
        s_zd = sem("expert_tokens_zeroed")
        s_bl = sem("expert_biases_loaded")
        s_bp = sem("expert_bias_parts_ready")
        s_bs = sem("expert_bias_parts_stacked")
        s_pos = sem("places_ready")
        s_eid = sem("tile_experts_ready")
        s_mv = sem("tokens_moved")
        s_xs = sem("expert_tokens_loaded")
        s_yi = sem("output_rows_ready")
        s_sf = sem("side_bank_filled")
        s_xe = sem("expert_tokens_turned")
        s_lt = sem("layernorm_turned")
        s_so = sem("first_attention_projected")
        s_u = sem("expert_up_ready")
        s_us = sem("expert_sigmoid_ready")
        s_ua = sem("expert_act_ready")
        s_ut = sem("expert_act_turned")
        s_uc = sem("turned_act_copied")
        s_y = sem("expert_down_done")
        s_ye = sem("expert_output_copied")
        s_ys = [sem(f"expert_output_stored_{a}") for a in range(YRING)]
        s_yl = [sem(f"expert_outputs_loaded_{c}") for c in range(NC)]
        s_f = sem("ffn_out_ready")
        s_fs = sem("ffn_sigmoid_ready")
        s_o = sem("result_ready")
        s_out = sem("result_stored")

        def bcast_rows(v, n):
            return v.rearrange("(a n) -> a n", a=1).broadcast_to([P, n])

        def o_first(t):
            return AO[:, NA:NG, t, :]

        def row(v):
            return v.rearrange("(a n) -> a n", a=1)

        first_weights = [(WIN[:, 0, :], aWq), (WIN[:, 1, :], aWk), (WIN[:, 2, :], aWv), (WIN[:, 3, :], aWo),
                         (ROWS[R_LN1:R_LN1 + 1, :], row(ln1)),
                         (ROWS[R_GAMMA:R_GAMMA + 1, :], row(gamma)), (ROWS[R_BETA:R_BETA + 1, :], row(beta)),
                         (ROWS[R_LN2:R_LN2 + 1, :], row(ln2)),
                         (ROWS[R_BG:R_BG + 1, :], row(bg).broadcast_to([NH, HD])),
                         (QKN[:, 0, :], bcast_rows(qn, HD)), (QKN[:, 1, :], bcast_rows(kn, HD)),
                         (WQKV[:, 0:128], Wq), (WQKV[:, 128:160], Wk), (WQKV[:, 160:192], Wv)]
        rope_weights = [(QKVB[:, 0:128], bcast_rows(bq, 128)), (QKVB[:, 128:160], bcast_rows(bk, 32)),
                        (QKVB[:, 160:192], bcast_rows(bv, 32)),
                        (COS[:, :, :], rope_cos.rearrange("(t p) n -> p t n", p=P)),
                        (SIN[:, :, :], rope_sin.rearrange("(t p) n -> p t n", p=P))]
        later_weights = [(BOB[:, :], bcast_rows(bo, 128)), (BRB[:, :], bcast_rows(br, NE)),
                         (WO1[:, :], Wo), (WRS[:, :], Wr)]

        h2 = HD // 2

        def rope(table):
            return table[:, :, :].unsqueeze(2).broadcast_to([P, T, NH + NKV, h2])

        block = ctx.enter_context(nc.Block())

        @block.sync
        def _(sp):
            xv = x[0].rearrange("(t p) n -> p t n", p=P)
            for c in range(4):
                sp.dma_start(XN[:, 4 * c:4 * c + 4, :], xv[:, 4 * c:4 * c + 4, :]).then_inc(s_x[c], 16)
            sp.wait_ge(s_w, 16 * len(first_weights))
            for dst, src in rope_weights:
                sp.dma_start(dst, src).then_inc(s_rw, 16)
            sp.wait_ge(s_wgz, 1)
            for h in range(NH):
                sp.dma_start(WG[h * HD:(h + 1) * HD, h * HD:(h + 1) * HD], Wg).then_inc(s_wl, 16)
            for dst, src in later_weights:
                sp.dma_start(dst, src).then_inc(s_wl, 16)
            sp.wait_ge(s_cr, 1)
            for g in range(NA):
                sp.dma_start(SH[g].rearrange("i h t s -> (i h t) s"), MROW[:, :]).then_inc(s_shw, 16)
            for n in range(NSRC):
                a, isk, c = n // 8, (n // 4) % 2, n % 4
                dst = (KP if isk else QP)["late" if c else "first"]
                lo = (c - 1) * CH if c else 0
                sp.wait_ge(s_lo, n + 1)
                sp.dma_start(dst[:, NA - NA * a:2 * NA - NA * a, :, :, lo:lo + CH].rearrange("i g d h s -> (g d h) i s"),
                             SP3[:, n % SLOTS, :, :]).then_inc(s_wr[n % SLOTS], 16)
            for a in range(SLOTS):
                sp.wait_ge(s_wr[a], 16 * NSRC // SLOTS)

            def load(q, k, g, piece, landed):
                r, at = PARTS * HD, slice(0, CH) if piece == "first" else slice(CH, S)
                for j in range(PARTS):
                    sp.dma_start(q[r * j:r * (j + 1), :, at],
                                 QP[piece][:, g].rearrange("i d h s -> i d (h s)")).then_inc(landed, 16)
                    sp.dma_start(k[r * j:r * (j + 1), :, at],
                                 KP[piece][j, g].rearrange("d h s -> d (h s)").unsqueeze(0)
                                 .broadcast_to([PARTS, HD, HG * (at.stop - at.start)])).then_inc(landed, 16)

            def load_late(j):
                load(QA[:, j % 2], KA[:, j % 2], SLOT_GROUP[j], "late", s_late[j % 2])

            def load_first(j):
                load(QA[:, j % 2], KA[:, j % 2], SLOT_GROUP[j], "first", s_ld[j % 2])
                if SLOT_GROUP[j] < NA:
                    load_shift(j)

            def load_shift(j):
                sp.dma_start(QA[SHIFT:SHIFT + 2, j % 2, :, :],
                             SH[SLOT_GROUP[j]].rearrange("i h t s -> i h (t s)")).then_inc(s_ld[j % 2], 16)

            def load_max(m, piece, landed):
                load(MB[:, 0], MB[:, 1], NA + m, piece, landed)

            sp.wait_ge(s_shw, 16 * NA)
            sp.wait_ge(s_zero, 1)
            load_late(0)
            load_first(0)
            load_max(0, "late", s_ml)
            load_max(0, "first", s_mf)
            load_late(1)
            load_first(1)
            sp.wait_ge(s_const, 1)
            sp.dma_start(XGD.rearrange("(j p) n -> p j n", p=P), ZERO[:, :].unsqueeze(1).broadcast_to([P, NT, ROW]))\
              .then_inc(s_zd, 16)
            for j in range(NG):
                m = j // 2
                ends_maxima = takes_shift(j >= 2 * PAIRS, j % 2)
                if ends_maxima and m < NA - 1:
                    sp.wait_ge(s_mm, UNITS * m + HG * LATE_ITEMS)
                    load_max(m + 1, "late", s_ml)
                if ends_maxima:
                    sp.wait_ge(s_tr, shift_use(m, m == PAIRS) + 2)
                    sp.dma_start(SH[NA + m].rearrange("i h t s -> (i h t) s"), MROW[:, :]).then_inc(s_shw, 16)
                    sp.wait_ge(s_shw, 16 * (NA + m + 1))
                    load_shift(j + 1)
                if ends_maxima and m < NA - 1:
                    sp.wait_ge(s_mm, UNITS * (m + 1))
                    load_max(m + 1, "first", s_mf)
                if j < NG - 2:
                    sp.wait_ge(s_pv, PV0 + NS * j + EARLY + 1)
                    load_late(j + 2)
                    sp.wait_ge(s_pv, PV0 + NS * (j + 1))
                    load_first(j + 2)
                if j == 2 * PAIRS:
                    sp.wait_ge(s_mm, UNITS * NA)
                    sp.dma_start(W1S, W1.rearrange("e d f -> d e f")).then_inc(s_moe, 16)
                    sp.dma_start(W2S, W2.rearrange("e (m p) d -> p e m d", p=P)).then_inc(s_moe, 16)

            sp.wait_ge(s_pv, PV0 + NS * (NG - 1))
            sp.dma_start(BF[:, 0:4 * P], b1).then_inc(s_bl, 16)
            sp.dma_start(BF[:, 4 * P:5 * P], b2).then_inc(s_bl, 16)
            sp.wait_ge(s_bp, 1)
            for i in range(PARTS):
                sp.dma_start(B12[NE * i:NE * (i + 1), :], BP[:, i, :]).then_inc(s_bs, 16)
            sp.wait_ge(s_fu, FFN_USE["W", NC - 1] + 1)
            sp.dma_start(XR[:, :, :], xv).then_inc(s_xr, 16)
            sp.wait_ge(s_mv, 16 * T)
            sp.dma_start(XS, XGD.rearrange("(j p) n -> p j n", p=P)).then_inc(s_xs, 16)
            for a in range(YRING):
                sp.wait_ge(s_ys[a], 16 * (NT // YRING))
            yv = YD[0:S].rearrange("(t p) n -> p t n", p=P)
            for c in range(NC):
                sp.dma_start(YN[:, 4 * c:4 * c + 4, :], yv[:, 4 * c:4 * c + 4, :]).then_inc(s_yl[c], 16)
            ov = out[0].rearrange("(t p) n -> p t n", p=P)
            for c in range(NC):
                sp.wait_ge(s_o, c + 1)
                sp.dma_start(ov[:, 4 * c:4 * c + 4, :], RS[:, 4 * c:4 * c + 4, :]).then_inc(s_out, 16)
            sp.wait_ge(s_out, 16 * NC)

        @block.gpsimd
        def _(gp):
            n = [0]

            def link(ins):
                n[0] += 1
                ins.then_inc(s_g, 1)
                gp.wait_ge(s_g, n[0])

            link(gp.memset(ID[:, :], 0.0))
            gp.affine_select(out=ID[:, :], in_=ID[:, :], compare_op=ALU.not_equal, fill=1.0, base=0,
                             pattern=[[-1, P]], channel_multiplier=1).then_inc(s_id, 1)
            gp.wait_ge(s_id, 1)
            link(gp.tensor_copy(IDB[:, :], ID[:, :]))
            link(gp.memset(CM[:, :], 0.0))
            link(gp.affine_select(out=CM[:, :], in_=CM[:, :], compare_op=ALU.is_ge, fill=NEG, base=0,
                                  pattern=[[-1, P]], channel_multiplier=1))
            link(gp.memset(TRI[:, :], 1.0))
            link(gp.affine_select(out=TRI[:, :], in_=TRI[:, :], compare_op=ALU.is_gt, fill=0.0, base=0,
                                  pattern=[[1, P]], channel_multiplier=-1))
            link(gp.memset(ONES[:, :], 1.0))
            link(gp.memset(ZERO[:, :], 0.0))
            for j in range(NT):
                link(gp.memset(TILE[:, j:j + 1], float(j)))
                link(gp.memset(J128[:, j:j + 1], float(P * j)))
            link(gp.memset(BEFORE[:, :, :], 1.0))
            link(gp.affine_select(out=BEFORE[:, :, :], in_=BEFORE[:, :, :], compare_op=ALU.is_gt, fill=0.0, base=0,
                                  pattern=[[1, NE], [-1, NE]], channel_multiplier=0))
            link(gp.memset(OWN[:, :], 0.0))
            for i in range(PARTS):
                link(gp.affine_select(out=OWN[:, :], in_=OWN[:, :], compare_op=ALU.not_equal, fill=1.0, base=-NE * i,
                                      pattern=[[-1, NE]], channel_multiplier=1))
            for e in range(NE):
                link(gp.memset(RANK[:, e:e + 1], float(NE - e)))
            link(gp.memset(MHALF[:, :], -0.5))
            gp.sem_inc(s_const, 1)
            link(gp.memset(QA[:, :, :, :].rearrange("p a h s -> p (a h s)").bitcast(F32), 0.0))
            link(gp.memset(KA[:, :, :, :].rearrange("p a h s -> p (a h s)").bitcast(F32), 0.0))
            link(gp.memset(KA[SHIFT:SHIFT + 2, :, :, :].rearrange("p a h s -> p (a h s)"), 1.0))
            gp.sem_inc(s_zero, 1)
            link(gp.memset(VA[:, :, :, :, :].rearrange("p a t h n -> p (a t h) n"), 0.0))
            link(gp.memset(VA[:, :, :, :, HD:HD + 1].rearrange("p a t h n -> p (a t h) n"), 1.0))

            gp.wait_ge(s_fr, reads(U_F - 1))
            qk = QKV1[:, :, 0:160].rearrange("p t (h d) -> p t h d", d=HD)
            r2, tmp = RT[:, :, :, h2:HD], RTMP[:, 1, :, :, :]
            gp.wait_ge(s_rw, 16 * len(rope_weights))
            link(gp.tensor_tensor(r2, qk[:, :, :, 0:h2], rope(SIN), ALU.mult))
            link(gp.tensor_tensor(tmp, qk[:, :, :, h2:HD], rope(COS), ALU.mult))
            gp.tensor_tensor(r2, r2, tmp, ALU.add).then_inc(s_r2, 1)
            gp.wait_ge(s_qf, 1)
            for g in range(NKV):
                gp.tensor_copy(QF[:, 1, :, g * HG * HD:(g + 1) * HG * HD].rearrange("p t (d h) -> p t d h", h=HG),
                               RT[:, :, NH + g, :].unsqueeze(3).broadcast_to([P, T, HD, HG])).then_inc(s_kf, 1)

            for g in range(NKV):
                v = QKV1[:, :, 160 + g * HD:160 + (g + 1) * HD]
                gp.tensor_copy(VX[:, (g + NA - 1) % NA, :, :].rearrange("p t (h d) -> p t h d", h=HG),
                               v.unsqueeze(2).broadcast_to([P, T, HG, HD])).then_inc(s_vx, 1)

            def build_values(at, b):
                gp.tensor_copy(VA[:, b, :, :, 0:HD],
                               VX[:, bass.ds(at, 1), :, :].rearrange("p o t (h d) -> p (o t) h d", h=HG))\
                  .then_inc(s_va, 1)

            gp.wait_ge(s_vx, NKV)
            build_values(place(0, 0), 0)
            build_values(place(0, 1), 1)
            gp.wait_ge(s_xt, NC)
            gp.wait_ge(s_wl, 16 * (len(later_weights) + NH))
            for t in range(T):
                gp.tensor_tensor(XN[:, t, :], XN[:, t, :], BOB[:, :], ALU.add).then_inc(s_kf, 1)
            gp.wait_ge(s_vc, T)

            def slot(i, side, following):
                g = 2 * i + side
                for s, (c, kb) in enumerate(STEPS):
                    if following is FFN_BESIDE:
                        work, k = FFN_AT.get(s - 1, (None, 0))
                        if work == "W":
                            gp.wait_ge(s_ms, k + 1)
                            tiles = slice(BPC * k, BPC * (k + 1))
                            gp.tensor_tensor(ST[:, 7, tiles], ST[:, 6, tiles], MHALF[:, tiles], ALU.pow)\
                              .then_inc(s_rs, 1)
                        for t in MOVE_AT.get(s, ()):
                            if t == 0:
                                gp.wait_ge(s_pos, 1)
                                gp.wait_ge(s_zd, 16)
                                gp.wait_ge(s_h2, T)
                            gp.indirect_dma_start(XGD, bass.IndirectOffsetOnAxis(POS[:, t:t + 1], 0), H2[:, t, :], None)\
                              .then_inc(s_mv, 16)
                    if kb < BPC * c:
                        continue
                    for p in range(2):
                        tile = 2 * s + p
                        gp.wait_ge(s_ex, EX0 + TILES * g + tile + 1)
                        v = PR[:, tile % RING, :, 0:P]
                        gp.sem_inc(s_seen, 1)
                        gp.affine_select(out=v, in_=v, compare_op=ALU.is_ge, fill=0.0, base=0,
                                         pattern=[[0, 2], [1, P]], channel_multiplier=-1).then_inc(s_mk, 1)
                if isinstance(following, int) or following is not FFN_BESIDE and following is not None:
                    gp.wait_ge(s_pv, PV0 + NS * (g + 1))
                    build_values(following, side)

            with gp.Fori(0, PAIRS - 1) as i:
                slot(i, 0, place(i + 1, 0))
                slot(i, 1, place(i + 1, 1))
            slot(PAIRS - 1, 0, NG - 2)
            slot(PAIRS - 1, 1, NG - 1)
            slot(PAIRS, 0, None)
            gp.wait_ge(s_pv, PV0 + NS * (NG - 1))
            gp.wait_ge(s_tr, 1 + turn_use(PAIRS, 0, ORDER[0], True))
            gp.tensor_copy(O2N[:, :, 0:HG * HD], AO[:, NA - 1, :, :]).then_inc(s_o2, 1)
            gp.tensor_copy(O2N[:, :, HG * HD:P].rearrange("p t (g n) -> p t g n", g=NA - 1),
                           AO[:, 0:NA - 1, :, :].rearrange("p g t n -> p t g n")).then_inc(s_o2, 1)
            slot(PAIRS, 1, FFN_BESIDE)
            gp.wait_ge(s_var, 4)
            gp.tensor_tensor(ST[:, 5, :], ST[:, 4, :], MHALF[:, :], ALU.pow).then_inc(s_std, 1)
            gp.wait_ge(s_yi, 1)
            for j in range(NT):
                gp.wait_ge(s_ye, j + 1)
                gp.indirect_dma_start(YD, bass.IndirectOffsetOnAxis(YI[:, j:j + 1], 0), YS[:, j % YRING, :], None)\
                  .then_inc(s_ys[j % YRING], 16)

        @block.scalar
        def _(act):
            for dst, src in first_weights:
                act.dma_start(dst, src).then_inc(s_w, 16)

            act.sem_inc(s_ex, EX0)

            act.wait_ge(s_var, 1)
            act.activation(ST[:, 1, :], ST[:, 0, :], ACT.Sqrt).then_inc(s_std, 1)
            act.wait_ge(s_w, 16 * len(first_weights))
            for a in range(2):
                act.activation(QNX[0:1, a, :].rearrange("p (g d h) -> p g d h", g=NA, d=HD),
                               QKN[0:1, a, :].unsqueeze(1).unsqueeze(3).broadcast_to([1, NA, HD, HG]),
                               ACT.Copy).then_inc(s_qx, 1)
            act.wait_ge(s_var, 2)
            act.activation(ST[:, 3, :], ST[:, 2, :], ACT.Sqrt).then_inc(s_std, 1)
            for c in range(NC):
                act.wait_ge(s_ft, U_X + c + 1)
                act.activation(XTF[:, c * CH:(c + 1) * CH], PS[:, (U_X + c) % 8, :], ACT.Copy).then_inc(s_xt, 1)

            def factor(n):
                return (1.0, SCALE, COLS[:, R_QN:R_QN + 1], KNS[:, 0:1])[n // 4]

            def first_part(n):
                act.wait_ge(s_ft, source_use(n) + 1)
                if n >= SLOTS:
                    act.wait_ge(s_wr[n % SLOTS], 16 * (n // SLOTS))
                act.activation(SP3[:, n % SLOTS, 0, :], PS[:, source_use(n) % 8, :], ACT.Copy, scale=factor(n))\
                   .then_inc(s_hi, 1)

            def second_part(n):
                act.wait_ge(s_res, n + 1)
                act.activation(SP3[:, n % SLOTS, 1, :], RES[:, n % 2, :], ACT.Copy).then_inc(s_mid, 1)

            def split(sources):
                for n in sources:
                    first_part(n)
                    if n > sources[0]:
                        second_part(n - 1)
                second_part(sources[-1])

            split(range(NSRC // 2))
            for t in range(T):
                act.wait_ge(s_ft, U_P + t + 1)
                act.activation(VX[:, NA:NG, t, :].rearrange("p g (h d) -> p g h d", h=HG),
                               PS[:, (U_P + t) % 8, 0:P].rearrange("p (d g h) -> p g h d", d=HD, g=4),
                               ACT.Copy).then_inc(s_vc, 1)
            act.wait_ge(s_const, 1)
            act.wait_ge(s_fr, reads(U_F - 1))
            act.activation(SQF[:, :, :, :], QKV1[:, :, 0:160].rearrange("p t (h d) -> p t h d", d=HD), ACT.Square)\
               .then_inc(s_sq, 1)
            act.wait_ge(s_var, 3)
            act.activation(HS[:, 1, :], HS[:, 0, :], ACT.Sqrt).then_inc(s_std, 1)
            split(range(NSRC // 2, NSRC))

            def slot(g, with_gate):
                for s, (c, kb) in enumerate(STEPS):
                    q0 = max(0, kb - BPC * c) * P
                    for p in range(2):
                        tile = 2 * s + p
                        if p == 0:
                            act.wait_ge(s_pv, NS * g + s + 1)
                        act.wait_ge(s_sc, TILES * g + tile + 1)
                        act.activation(PR[:, tile % RING, :, 0:CH - q0],
                                       PS[:, 2 * p:2 * p + 2, 0:CH - q0], ACT.Exp).then_inc(s_ex, 1)
                    work, k = FFN_AT.get(s - 1, (None, None))
                    if with_gate and work == "G":
                        use = FFN_USE[work, k]
                        act.wait_ge(s_bs, 16 * PARTS)
                        act.wait_ge(s_ng, 1)
                        act.wait_ge(s_ff, use + 1)
                        act.activation(GE[:, k * CH:(k + 1) * CH], PS[:, 4 + use % 2, :], ACT.Tanh,
                                       bias=HBG[:, 0:1], scale=0.5).then_inc(s_sig, 1)

            with act.Fori(0, PAIRS) as i:
                slot(2 * i, False)
                slot(2 * i + 1, False)
            slot(2 * PAIRS, False)
            slot(2 * PAIRS + 1, True)

            def side(j):
                work, k = SIDE_AT.get(j, (None, 0))
                bank = PS[:, 6 + SIDE_USE.get((work, k), 0) % 2, :]
                if work == "X":
                    act.wait_ge(s_sf, SIDE_USE[work, k] + 1)
                    act.activation(XG[:, k * CH:(k + 1) * CH], bank, ACT.Copy, scale=COLS[:, R_LN2:R_LN2 + 1])\
                       .then_inc(s_xe, 1)
                if work == "S":
                    act.wait_ge(s_sf, SIDE_USE[work, k] + 1)
                    act.activation(SO[:, 4 * k:4 * k + 4, :].rearrange("p t n -> p (t n)"), bank, ACT.Copy)\
                       .then_inc(s_so, 1)

            act.wait_ge(s_pv, PV0 + NS * NG)
            side(-1)
            for j in range(NT + 1):
                if j < NT:
                    act.wait_ge(s_u, j + 1)
                    if j >= 2:
                        act.wait_ge(s_ua, j - 1)
                    act.activation(SG[:, j % 2, :], PS[:, j % 2, HID:2 * HID], ACT.Sigmoid).then_inc(s_us, 1)
                side(j)
                if j >= 1:
                    act.wait_ge(s_ut, j)
                    if j >= 3:
                        act.wait_ge(s_y, j - 2)
                    act.activation(UT[:, (j - 1) % 2, :], PS[:, 2 + (j - 1) % 2, 0:2 * P], ACT.Copy).then_inc(s_uc, 1)
            for c in range(NC):
                act.wait_ge(s_f, c + 1)
                act.activation(RS[:, 4 * c:4 * c + 4, :], X2[:, 4 * c:4 * c + 4, :], ACT.Sigmoid).then_inc(s_fs, 1)

        @block.tensor
        def _(pe):
            def front(u):
                if U_X <= u - 8 < U_A:
                    pe.wait_ge(s_xt, u - 8 - U_X + 1)
                elif u >= 8:
                    pe.wait_ge(s_fr, reads(u - 8))
                return PS[:, u % 8, :]

            pe.wait_ge(s_id, 1)
            pe.wait_ge(s_w, 16 * len(first_weights))
            bank = front(U_W)
            for k in range(4):
                last = pe.transpose(bank[:, k * P:(k + 1) * P], WIN[:, k, :], ID[:, :])
            last.then_inc(s_ft, 1)
            pe.wait_ge(s_qx, 2)
            bank = front(U_W + 1)
            for a in range(2):
                pe.transpose(bank[:, R_QN + a:R_QN + a + 1], QNX[0:1, a, :], ID[0:1, 0:1])
            pe.transpose(bank[:, 0:R_QN], ROWS[:, :], ID[0:R_QN, 0:R_QN]).then_inc(s_ft, 1)
            for c in range(NC):
                pe.wait_ge(s_xn, 4 * (c + 1))
                bank = front(U_X + c)
                for k in range(BPC):
                    last = pe.transpose(bank[:, k * P:(k + 1) * P], XN[:, 4 * c + k, :], ID[:, :])
                last.then_inc(s_ft, 1)
            pe.wait_ge(s_wn, 1)
            for n in range(NSRC // 2):
                bank = front(U_A + n)
                pe.wait_ge(s_xt, n % 4 + 1)
                pe.matmul(bank, WT[:, n // 4, :], XTF[:, (n % 4) * CH:(n % 4 + 1) * CH], start=True, stop=True)\
                  .then_inc(s_ft, 1)
            for t in range(T):
                bank = front(U_P + t)
                pe.matmul(bank[:, 0:P + 192], XTF[:, t * P:(t + 1) * P], WN[:, :], start=True, stop=True)\
                  .then_inc(s_ft, 1)
            pe.wait_ge(s_qf, 1 + NA)
            for n in range(NSRC // 2, NSRC):
                if n == 12:
                    pe.wait_ge(s_kf, NKV)
                bank = front(source_use(n))
                for k in range(BPC):
                    last = pe.transpose(bank[:, k * P:(k + 1) * P], QF[:, (n - 8) // 4, 4 * (n % 4) + k, :], ID[:, :])
                last.then_inc(s_ft, 1)
            pe.wait_ge(s_fr, reads(U_F + NSRC // 2 - 1))
            pe.wait_ge(s_const, 1)

            def max_unit(i, item, hh):
                qb, kc = ITEMS[item]
                u = item * HG + hh
                diag = kc == qb // BPC
                w = item_width(item)
                bank = PS[:, 4 + u % 2, :]
                if hh == 0 and item == 0:
                    pe.wait_ge(s_ml, 16 * NLOAD * (i + 1))
                if hh == 0 and item == FIRST_NEEDED:
                    pe.wait_ge(s_mf, 16 * NLOAD * (i + 1))
                pe.wait_ge(s_mr, UNITS * i + u + 1)
                last = pe.matmul(bank[:, 0:w], MB[0:STACK, 0, hh, qb * P:(qb + 1) * P],
                                 MB[0:STACK, 1, hh, kc * CH:kc * CH + w], start=True, stop=not diag)
                if diag:
                    last = pe.matmul(bank[:, w - P:w], IDB[:, :], CM[:, :], start=False, stop=True)
                last.then_inc(s_mm, 1)

            def shift_turn(i, peeled):
                pe.wait_ge(s_nm, i + 1)
                pe.wait_ge(s_tr, shift_use(i, peeled) + 1)
                pe.transpose(TBH[:, 0:P], NMR[:, :, :].rearrange("p a n -> p (a n)"), IDB[:, :]).then_inc(s_t, 1)

            def scores(i, side, s, p):
                c, kb = STEPS[s]
                g, b = 2 * i + side, side % 2
                q0 = max(0, kb - BPC * c) * P
                pe.wait_ge(s_ex, TILES * g + 2 * s + p + 1)
                for k in range(2):
                    last = pe.matmul(PS[:, 2 * p + k, 0:CH - q0],
                                     KA[:, b, 2 * p + k, kb * P:(kb + 1) * P],
                                     QA[:, b, 2 * p + k, c * CH + q0:(c + 1) * CH], start=True, stop=True)
                last.then_inc(s_sc, 1)

            def values(i, side, s):
                c, kb = STEPS[s]
                g, b = 2 * i + side, side % 2
                q0 = max(0, kb - BPC * c) * P
                if kb == 0:
                    pe.wait_ge(s_oe, NC * g + ORDER.index(c) + 1)
                if kb >= BPC * c:
                    pe.wait_ge(s_mk, DIAG * g + 2 * diag_index(s + 1))
                pe.wait_ge(s_ex, EX0 + TILES * g + 2 * s + 2)
                for hh in range(HG):
                    last = pe.matmul(PS[32 * hh:32 * hh + 32, 6, q0:CH], VA[:, b, kb, hh, :],
                                     PR[:, (2 * s + hh // 2) % RING, hh % 2, 0:CH - q0],
                                     start=kb == 0, stop=kb == BPC * (c + 1) - 1)
                last.then_inc(s_pv, 1)

            def turn(i, side, c, peeled):
                g = 2 * i + side
                pe.wait_ge(s_oe, NC * g + ORDER.index(c) + 2)
                pe.wait_ge(s_tr, turn_use(i, side, c, peeled) + 1)
                for k in range(BPC):
                    last = pe.transpose(TB[:, k * P:(k + 1) * P], OT[:, c % 2, k * P:(k + 1) * P], ID[:, :])
                last.then_inc(s_t, 1)

            def stage(i, side, s, peeled):
                if s == 0:
                    pe.wait_ge(s_late[side % 2], 16 * NLOAD * (i + 1 + side // 2))
                    pe.wait_ge(s_ld[side % 2], 16 * (NLOAD + 1) * (i + 1 + side // 2))
                    pe.wait_ge(s_va, 2 * i + side + 1)
                parts = units_at(maxima_of(peeled, side), s) if side < 2 else ((), (), ())
                for p in range(2):
                    if s < NS:
                        scores(i, side, s, p)
                    for item, hh in parts[p]:
                        max_unit(i, item, hh)
                side_v, v = behind(side, s, LAG)
                if v < NS and side_v >= 0:
                    values(i, side_v, v)
                side_t, t = behind(side, s, LAG + 1)
                if ending(t) is not None and side_t >= 0:
                    turn(i, side_t, ending(t), peeled)
                for item, hh in parts[2]:
                    max_unit(i, item, hh)
                if s == SHIFT_TURN and takes_shift(peeled, side):
                    shift_turn(i, peeled)
                if peeled and side == 1:
                    ffn(s)

            def ffn(s):
                if s not in FFN_AT:
                    return
                work, k = FFN_AT[s]
                use = FFN_USE[work, k]
                bank = PS[:, 4 + use % 2, :]
                if work == "C":
                    pe.wait_ge(s_mr, 2 + UNITS * NA)
                    last = pe.matmul(bank[:, 0:1], TRI[:, :], ONES[:, 0:1], start=True, stop=True)
                if use >= 2:
                    pe.wait_ge(s_fu, use - 1)
                if work == "O":
                    pe.wait_ge(s_o2, 2)
                    for j in range(BPC):
                        last = pe.transpose(bank[:, j * P:(j + 1) * P], O2N[:, 4 * k + j, :], ID[:, :])
                if work == "G":
                    pe.wait_ge(s_fu, FFN_USE["O", k] + 1)
                    pe.wait_ge(s_wl, 16 * (len(later_weights) + NH))
                    last = pe.matmul(bank, WG[:, :], O1T[:, k * CH:(k + 1) * CH], start=True, stop=True)
                if work == "W":
                    pe.wait_ge(s_gt, k + 1)
                    for j in range(BPC):
                        t = 4 * k + j
                        last = pe.matmul(bank[:, j * P:(j + 1) * P], O1T[:, t * P:(t + 1) * P], WO1[:, :],
                                         start=True, stop=True)
                if work == "H":
                    pe.wait_ge(s_h2, 4 * (k + 1))
                    for j in range(BPC):
                        last = pe.transpose(bank[:, j * P:(j + 1) * P], H2[:, 4 * k + j, 0:P], ID[:, :])
                if work == "R":
                    pe.wait_ge(s_fu, FFN_USE["H", NC - 1] + 1)
                    for t in range(T):
                        last = pe.matmul(bank[:, t * NE:(t + 1) * NE], XT[:, t * P:(t + 1) * P], WRS[:, :],
                                         start=True, stop=True)
                if work == "K":
                    pe.wait_ge(s_oh, 1)
                    oh = LG[:, 3, :, :]
                    pe.matmul(bank[:, 0:T * NE], TRI[:, :], oh.rearrange("p t e -> p (t e)"), start=True, stop=False)
                    for t in range(T - 1):
                        pe.matmul(bank[:, (t + 1) * NE:T * NE], ONES[:, :],
                                  oh[:, t, :].unsqueeze(1).broadcast_to([P, T - 1 - t, NE]),
                                  start=False, stop=t == T - 2)
                    last = pe.matmul(bank[:, T * NE:2 * T * NE], ONES[:, :], oh.rearrange("p t e -> p (t e)"),
                                     start=True, stop=True)
                last.then_inc(s_ff, 1)

            for s in range(HEAD):
                stage(0, 0, s, False)
            with pe.Fori(0, PAIRS) as i:
                stream(i, False, stage)
            stream(PAIRS, True, stage)

            def side(j):
                if j not in SIDE_AT:
                    return
                work, k = SIDE_AT[j]
                use = SIDE_USE[work, k]
                bank = PS[:, 6 + use % 2, :]
                if use >= 2:
                    before, n = list(SIDE_AT.values())[use - 2]
                    pe.wait_ge({"X": s_xe, "L": s_lt, "S": s_so}[before], n + 1)
                for i in range(BPC):
                    t = BPC * k + i
                    at = bank[:, i * P:(i + 1) * P]
                    if work == "X":
                        last = pe.transpose(at, XS[:, t, 0:P], ID[:, :])
                    if work == "L":
                        pe.wait_ge(s_ln, t + 1)
                        last = pe.transpose(at, LNO[:, t, :], ID[:, :])
                    if work == "S":
                        pe.wait_ge(s_lt, k + 1)
                        last = pe.matmul(at, LNT[:, t * P:(t + 1) * P], WT[:, 3, :], start=True, stop=True)
                last.then_inc(s_sf, 1)

            def up(j):
                e = pe.value_load(EID[0:1, j:j + 1], min_val=0, max_val=NE - 1)
                if j % BPC == 0:
                    pe.wait_ge(s_xe, j // BPC + 1)
                if j >= 2:
                    pe.wait_ge(s_ua, j - 1)
                bank = PS[:, j % 2, :]
                pe.matmul(bank, TE[:, j, :], B12[:, 0:4 * P], start=True, stop=False)
                pe.matmul(bank, XG[:, j * P:(j + 1) * P], W1S[:, bass.ds(e, 1), :].rearrange("p a n -> p (a n)"),
                          start=False, stop=True).then_inc(s_u, 1)
                return e

            def turn_act(j):
                pe.wait_ge(s_ua, j + 1)
                if j >= 2:
                    pe.wait_ge(s_uc, j - 1)
                for m in range(2):
                    last = pe.transpose(PS[:, 2 + j % 2, m * P:(m + 1) * P], UA[:, j % 2, m * P:(m + 1) * P], ID[:, :])
                last.then_inc(s_ut, 1)

            def down(j, e):
                pe.wait_ge(s_uc, j + 1)
                if j >= 2:
                    pe.wait_ge(s_ye, j - 1)
                bank = PS[:, 4 + j % 2, 0:P]
                pe.matmul(bank, TE[:, j, :], B12[:, 4 * P:5 * P], start=True, stop=False)
                for m in range(2):
                    last = pe.matmul(bank, UT[:, j % 2, m * P:(m + 1) * P],
                                     W2S[:, bass.ds(e, 1), m, :].rearrange("p a n -> p (a n)"),
                                     start=False, stop=m == 1)
                last.then_inc(s_y, 1)

            pe.wait_ge(s_tr, 1 + USES)
            pe.wait_ge(s_fu, len(FFN_AT))
            pe.wait_ge(s_xs, 16)
            side(-1)
            pe.wait_ge(s_eid, 1)
            pe.wait_ge(s_bs, 16 * PARTS)
            pe.wait_ge(s_moe, 32)
            experts = []
            for j in range(NT + 2):
                if j < NT:
                    experts.append(up(j))
                side(j)
                if 1 <= j <= NT:
                    turn_act(j - 1)
                if j >= 2:
                    down(j - 2, experts[j - 2])

        @block.vector
        def _(dve):
            n = [0]

            def link(ins):
                n[0] += 1
                ins.then_inc(s_v, 1)
                dve.wait_ge(s_v, n[0])

            dve.memset(WG[:, :], 0.0).then_inc(s_wgz, 1)
            link(dve.memset(MP[:, :, :], NEG))
            dve.sem_inc(s_pv, PV0)
            dve.sem_inc(s_mr, 2)
            dve.sem_inc(s_oe, 1)
            dve.sem_inc(s_tr, 1)

            def moments(src, landed=None):
                for t in range(T):
                    if landed and t % BPC == 0:
                        dve.wait_ge(landed[t // BPC], 16)
                    last = dve.bn_stats(BN[:, t, :], src(t))
                link(last)
                for t in range(T):
                    last = dve.bn_aggr(MV[:, t, :], BN[:, t, :])
                link(last)

            moments(lambda t: XN[:, t, :], s_x)
            dve.tensor_scalar(ST[:, 0, :], MV[:, :, 1], 1e-5, None, ALU.add).then_inc(s_var, 1)
            dve.wait_ge(s_std, 1)
            link(dve.reciprocal(ST[:, 1, :], ST[:, 1, :]))
            for t in range(T):
                dve.tensor_scalar(XN[:, t, :], XN[:, t, :], MV[:, t, 0:1], ST[:, 1, t:t + 1],
                                  ALU.subtract, ALU.mult).then_inc(s_xn, 1)
            link(dve.tensor_tensor(ST[:, 2, :], ST[:, 1, :], ST[:, 1, :], ALU.mult))
            link(dve.tensor_tensor(ST[:, 2, :], ST[:, 2, :], MV[:, :, 1], ALU.mult))
            dve.tensor_scalar(ST[:, 2, :], ST[:, 2, :], 1e-6, None, ALU.add).then_inc(s_var, 1)
            dve.wait_ge(s_std, 2)
            link(dve.reciprocal(ST[:, 3, :], ST[:, 3, :]))

            dve.wait_ge(s_ft, U_W + 1)
            for a in range(2):
                dve.tensor_copy(WT[:, a, :].rearrange("p (g d h) -> p g h d", g=NA, h=HG),
                                PS[:, U_W, a * P:(a + 1) * P].rearrange("p (g h d) -> p g h d", g=NA, h=HG))
            dve.tensor_copy(WT[:, 2:4, :].rearrange("p a n -> p (a n)"), PS[:, U_W, 2 * P:4 * P]).then_inc(s_fr, 1)
            dve.wait_ge(s_ft, U_W + 2)
            dve.tensor_copy(COLS[:, :], PS[:, U_W + 1, 0:NROWS]).then_inc(s_fr, 1)
            dve.wait_ge(s_fr, 2)
            dve.tensor_copy(WN[:, 0:P], WT[:, 2, :])
            dve.tensor_scalar(HBG[:, :], COLS[:, R_BG:R_BG + 1], 0.5, None, ALU.mult).then_inc(s_ng, 1)
            dve.tensor_scalar(KNS[:, :], COLS[:, R_KN:R_KN + 1], SCALE, None, ALU.mult)
            dve.tensor_scalar(WN[:, P:P + 192], WQKV[:, :], COLS[:, R_LN1:R_LN1 + 1], None, ALU.mult)\
               .then_inc(s_wn, 1)

            link(dve.tensor_reduce(QKM[:, :], QKN[:, :, :], AX, ALU.max, apply_absolute_value=True))
            link(dve.tensor_tensor(QKM[:, 0:1], QKM[:, 0:1], QKM[:, 1:2], ALU.mult))
            link(dve.tensor_scalar(QKM[:, 1:2], QKM[:, 0:1], -SCALE * HD, BOUND, ALU.mult, ALU.add))
            link(dve.tensor_scalar(QKM[:, 0:1], QKM[:, 1:2], 0.0, None, ALU.min))
            link(dve.tensor_copy(NMR[:, 0, 0:1], QKM[:, 0:1]))
            link(dve.tensor_tensor(NMR[:, 1, 0:1], QKM[:, 0:1], NMR[:, 0, 0:1], ALU.subtract))
            for i in range(2):
                r = slice(i * HG * T, (i + 1) * HG * T)
                last = dve.tensor_copy(MROW[r, :], NMR[r, i, 0:1].broadcast_to([HG * T, P]))
            last.then_inc(s_cr, 1)

            def factor(n):
                return (1.0, SCALE, COLS[:, R_QN:R_QN + 1], KNS[:, 0:1])[n // 4]

            def remainder(n):
                if n >= 2:
                    dve.wait_ge(s_lo, n - 1)
                dve.wait_ge(s_hi, n + 1)
                dve.scalar_tensor_tensor(RES[:, n % 2, :], PS[:, source_use(n) % 8, :], factor(n),
                                         SP3[:, n % SLOTS, 0, :], ALU.mult, ALU.subtract).then_inc(s_res, 1)

            def third_part(n):
                dve.wait_ge(s_mid, n + 1)
                dve.tensor_tensor(SP3[:, n % SLOTS, 2, :], RES[:, n % 2, :], SP3[:, n % SLOTS, 1, :], ALU.subtract)\
                   .then_inc(s_lo, 1)

            def split(sources):
                for n in sources:
                    remainder(n)
                    if n > sources[0]:
                        third_part(n - 1)
                    dve.wait_ge(s_res, n + 1)
                    dve.sem_inc(s_fr, 1)
                third_part(sources[-1])

            split(range(NSRC // 2))
            dve.wait_ge(s_rw, 16 * len(rope_weights))
            for t in range(T):
                dve.wait_ge(s_vc, t + 1)
                dve.scalar_tensor_tensor(QKV1[:, t, :], PS[:, (U_P + t) % 8, P:P + 192], ST[:, 3, t:t + 1],
                                         QKVB[:, :], ALU.mult, ALU.add).then_inc(s_fr, 1)
            dve.wait_ge(s_fr, reads(U_F - 1))

            qk = QKV1[:, :, 0:160].rearrange("p t (h d) -> p t h d", d=HD)
            r1, tmp = RT[:, :, :, 0:h2], RTMP[:, 0, :, :, :]
            hs = HS[:, 0, :].rearrange("p (t h) -> p t h", t=T)
            link(dve.tensor_tensor(r1, qk[:, :, :, 0:h2], rope(COS), ALU.mult))
            link(dve.tensor_tensor(tmp, qk[:, :, :, h2:HD], rope(SIN), ALU.mult))
            dve.wait_ge(s_sq, 1)
            link(dve.tensor_reduce(hs, SQF[:, :, :, :], AX, ALU.add))
            dve.tensor_scalar(HS[:, 0, :], HS[:, 0, :], 1.0 / HD, 1e-6, ALU.mult, ALU.add).then_inc(s_var, 1)
            link(dve.tensor_tensor(r1, r1, tmp, ALU.subtract))
            dve.wait_ge(s_std, 3)
            link(dve.reciprocal(HS[:, 2, :], HS[:, 1, :]))
            dve.wait_ge(s_r2, 1)
            rr = HS[:, 2, :].rearrange("p (t h) -> p t h", t=T).unsqueeze(3).broadcast_to([P, T, NH + NKV, HD])
            dve.tensor_tensor(RT[:, :, NH:NH + NKV, :], RT[:, :, NH:NH + NKV, :], rr[:, :, NH:NH + NKV, :],
                              ALU.mult).then_inc(s_qf, 1)
            for g in range(NA):
                gh = slice(g * HG, (g + 1) * HG)
                dve.tensor_tensor(QF[:, 0, :, g * HG * HD:(g + 1) * HG * HD].rearrange("p t (d h) -> p t h d", h=HG),
                                  RT[:, :, gh, :], rr[:, :, gh, :], ALU.mult).then_inc(s_qf, 1)
            split(range(NSRC // 2, NSRC))

            def max_unit(i, item, hh):
                qb, kc = ITEMS[item]
                u = item * HG + hh
                w = item_width(item)
                dve.wait_ge(s_mm, UNITS * i + u + 1)
                dve.reduce_max(MP[:, hh * T + qb, kc:kc + 1], PS[:, 4 + u % 2, 0:w], AX).then_inc(s_mr, 1)

            def shift_parts(i):
                dve.wait_ge(s_mr, 2 + UNITS * (i + 1))
                dve.tensor_reduce(NM[:, :], MP[:, :, :], AX, ALU.max, negate=True).then_inc(s_ch, 1)
                dve.wait_ge(s_ch, 2 * i + 1)
                dve.tensor_copy(NMR[:, 0, :], NM[:, :]).then_inc(s_ch, 1)
                dve.wait_ge(s_ch, 2 * i + 2)
                dve.tensor_tensor(NMR[:, 1, :], NM[:, :], NMR[:, 0, :], ALU.subtract).then_inc(s_nm, 1)

            def shift_read(i, peeled):
                dve.wait_ge(s_t, shift_use(i, peeled) + 1)
                dve.wait_ge(s_shw, 16 * (NA + i))
                dve.tensor_copy(MROW[:, :], TBH[:, 0:P]).then_inc(s_tr, 1)

            def copy_out(i, side, c):
                dve.wait_ge(s_pv, PV0 + NS * (2 * i + side) + chunk_end(c) + 1)
                dve.tensor_copy(OT[:, c % 2, :], PS[:, 6, :]).then_inc(s_oe, 1)

            def normalise(i, side, c, peeled):
                dve.wait_ge(s_t, turn_use(i, side, c, peeled) + 1)
                o = TB.rearrange("p (k h n) -> p k h n", k=BPC, h=HG)
                dve.reciprocal(RL[:, c % 2, :, :], o[:, :, :, HD]).then_inc(s_rl, 1)
                dve.wait_ge(s_rl, NC * (2 * i + side) + ORDER.index(c) + 1)
                at = NA + i if peeled and side else place(i, side)
                dve.tensor_tensor(
                    AO[:, bass.ds(at, 1), 4 * c:4 * c + 4, :].rearrange("p o t (h d) -> p (o t) h d", h=HG),
                    o[:, :, :, 0:HD], RL[:, c % 2, :, :].unsqueeze(3).broadcast_to([P, BPC, HG, HD]),
                    ALU.mult).then_inc(s_tr, 1)

            def stage(i, side, s, peeled):
                parts = units_at(maxima_of(peeled, side), s) if side < 2 else ((), (), ())
                for item, hh in (*parts[0], *parts[1]):
                    max_unit(i, item, hh)
                side_v, v = behind(side, s, LAG)
                if ending(v) is not None and side_v >= 0:
                    copy_out(i, side_v, ending(v))
                side_t, t = behind(side, s, LAG + 1)
                if ending(t) is not None and side_t >= 0:
                    normalise(i, side_t, ending(t), peeled)
                for item, hh in parts[2]:
                    max_unit(i, item, hh)
                if s == SHIFT_PARTS and takes_shift(peeled, side):
                    shift_parts(i)
                if s == SHIFT_TURN and takes_shift(peeled, side):
                    shift_read(i, peeled)
                if peeled and side == 1:
                    ffn(s)

            def ffn(s):
                work, k = FFN_AT.get(s, (None, 0))
                use = FFN_USE.get((work, k), 0)
                at, tiles, bank = slice(k * CH, (k + 1) * CH), slice(BPC * k, BPC * (k + 1)), PS[:, 4 + use % 2, :]
                gate, n = FFN_AT.get(s - 1, (None, 0))
                if gate == "G":
                    ge = GE[:, n * CH:(n + 1) * CH]
                    dve.wait_ge(s_sig, n + 1)
                    dve.tensor_scalar(ge, ge, 0.5, 0.5, ALU.mult, ALU.add).then_inc(s_fu, 1)
                if work not in (None, "G"):
                    dve.wait_ge(s_ff, use + 1)
                if work == "O":
                    dve.tensor_copy(O1T[:, at], bank).then_inc(s_fu, 1)
                if gate == "G":
                    o = O1T[:, n * CH:(n + 1) * CH]
                    dve.wait_ge(s_fu, FFN_USE["G", n] + 1)
                    dve.tensor_tensor(o, o, ge, ALU.mult).then_inc(s_gt, 1)
                if work == "C":
                    dve.tensor_scalar(TOK[:, :], J128[:, 0:T], bank[:, 0:1], 1.0, ALU.add, ALU.add)
                    dve.tensor_scalar(SPARE[:, :], J128[:, :], bank[:, 0:1], float(S + 1), ALU.add, ALU.add)\
                       .then_inc(s_fu, 1)
                if s == 3:
                    dve.wait_ge(s_bl, 32)
                    link(dve.tensor_copy(BP[:, 0, :], BF))
                    link(dve.tensor_tensor(BF, BF, BP[:, 0, :], ALU.subtract))
                    link(dve.tensor_copy(BP[:, 1, :], BF))
                    dve.tensor_tensor(BP[:, 2, :], BF, BP[:, 1, :], ALU.subtract).then_inc(s_bp, 1)
                if work == "W":
                    dve.wait_ge(s_kf, NKV + T)
                    dve.tensor_tensor(X2[:, tiles, :].rearrange("p t n -> p (t n)"), bank,
                                      XN[:, tiles, :].rearrange("p t n -> p (t n)"), ALU.add).then_inc(s_fu, 1)
                    dve.wait_ge(s_fu, use + 1)
                    link(dve.tensor_tensor(SQ[:, tiles, :], X2[:, tiles, :], X2[:, tiles, :], ALU.mult))
                    link(dve.tensor_reduce(ST[:, 6, tiles], SQ[:, tiles, :], AX, ALU.add))
                    dve.tensor_scalar(ST[:, 6, tiles], ST[:, 6, tiles], 1.0 / P, 1e-6, ALU.mult, ALU.add)\
                       .then_inc(s_ms, 1)
                if gate == "W":
                    dve.wait_ge(s_rs, n + 1)
                    for t in range(BPC * n, BPC * (n + 1)):
                        dve.tensor_copy(H2[:, t, P:ROW], TOK[:, t:t + 1])
                        dve.tensor_scalar(H2[:, t, 0:P], X2[:, t, :], ST[:, 7, t:t + 1], None, ALU.mult)\
                           .then_inc(s_h2, 1)
                if work == "H":
                    dve.tensor_scalar(XT[:, at], bank, COLS[:, R_LN2:R_LN2 + 1], None, ALU.mult).then_inc(s_fu, 1)
                if work == "R":
                    lg = LG[:, 0, :, :]
                    brb = BRB[:, :].unsqueeze(1).broadcast_to([P, T, NE])
                    rank = RANK[:, :].unsqueeze(1).broadcast_to([P, T, NE])
                    dve.tensor_tensor(lg, bank[:, 0:T * NE].rearrange("p (t e) -> p t e", t=T), brb, ALU.add)\
                       .then_inc(s_fu, 1)
                    dve.wait_ge(s_fu, use + 1)
                    link(dve.tensor_reduce(MX[:, 0, :], lg, AX, ALU.max))
                    mx = MX[:, 0, :].unsqueeze(2).broadcast_to([P, T, NE])
                    link(dve.tensor_tensor(LG[:, 1, :, :], lg, mx, ALU.is_equal))
                    link(dve.tensor_tensor(LG[:, 2, :, :], LG[:, 1, :, :], rank, ALU.mult))
                    link(dve.tensor_reduce(MX[:, 1, :], LG[:, 2, :, :], AX, ALU.max))
                    mx1 = MX[:, 1, :].unsqueeze(2).broadcast_to([P, T, NE])
                    dve.tensor_tensor(LG[:, 3, :, :], LG[:, 2, :, :], mx1, ALU.is_equal).then_inc(s_oh, 1)
                if work == "K":
                    count, tiles_, first, end = (CNT[:, a, :] for a in range(4))
                    link(dve.tensor_reduce(count, bank[:, T * NE:2 * T * NE].rearrange("p (t e) -> p e t", t=T),
                                           AX, ALU.add))
                    more = LG[:, 1, :, :].rearrange("p t e -> p (t e)").rearrange("p (e k) -> p e k", e=NE)
                    link(dve.tensor_tensor(more, count.unsqueeze(2).broadcast_to([P, NE, T]),
                                           J128[:, 0:T].unsqueeze(1).broadcast_to([P, NE, T]), ALU.is_gt))
                    link(dve.tensor_reduce(tiles_, more, AX, ALU.add))
                    before = LG[:, 2, 0:NE, :]
                    link(dve.tensor_tensor(before, tiles_.unsqueeze(1).broadcast_to([P, NE, NE]), BEFORE[:, :, :],
                                           ALU.mult))
                    link(dve.tensor_reduce(first, before, AX, ALU.add))
                    link(dve.tensor_tensor(end, first, tiles_, ALU.add))
                    link(dve.tensor_scalar(first, first, float(P), None, ALU.mult))
                    dve.tensor_tensor(LG[:, 0, :, :], bank[:, 0:T * NE].rearrange("p (t e) -> p t e", t=T),
                                      first.unsqueeze(1).broadcast_to([P, T, NE]), ALU.add).then_inc(s_fu, 1)
                    dve.wait_ge(s_fu, use + 1)
                    link(dve.tensor_tensor(LG[:, 0, :, :], LG[:, 0, :, :], LG[:, 3, :, :], ALU.mult))
                    link(dve.tensor_reduce(POSF[:, :], LG[:, 0, :, :], AX, ALU.add))
                    dve.tensor_copy(POS[:, :], POSF[:, :]).then_inc(s_pos, 1)
                    link(dve.tensor_tensor(EQ, TILE[:, :].unsqueeze(2).broadcast_to([P, NT, NE]),
                                           end.unsqueeze(1).broadcast_to([P, NT, NE]), ALU.is_ge))
                    link(dve.tensor_reduce(EIDF[:, :], EQ, AX, ALU.add))
                    link(dve.tensor_scalar(EIDF[:, :], EIDF[:, :], float(NE - 1), None, ALU.min))
                    link(dve.tensor_copy(EID[:, :], EIDF[:, :]))
                    r = PARTS * NE
                    link(dve.tensor_tensor(EQ[0:r], EIDF[0:r, :].unsqueeze(2).broadcast_to([r, NT, NE]),
                                           TILE[0:r, 0:NE].unsqueeze(1).broadcast_to([r, NT, NE]), ALU.is_equal))
                    link(dve.tensor_tensor(EQ[0:r], EQ[0:r], OWN[:, :].unsqueeze(1).broadcast_to([r, NT, NE]),
                                           ALU.mult))
                    link(dve.tensor_reduce(YIF[0:r, :], EQ[0:r], AX, ALU.add))
                    dve.tensor_copy(TE, YIF[0:r, :].unsqueeze(2).broadcast_to([r, NT, P])).then_inc(s_eid, 1)

            for s in range(HEAD):
                stage(0, 0, s, False)
            with dve.Fori(0, PAIRS) as i:
                stream(i, False, stage)
            stream(PAIRS, True, stage)

            def first_attention(j):
                if 1 <= j <= NC:
                    for t in range(BPC * (j - 1), BPC * j):
                        last = dve.bn_stats(BN[:, t, :], o_first(t))
                    link(last)
                    for t in range(BPC * (j - 1), BPC * j):
                        last = dve.bn_aggr(MV[:, t, :], BN[:, t, :])
                    link(last)
                if j == NC:
                    dve.tensor_scalar(ST[:, 4, :], MV[:, :, 1], 1e-5, None, ALU.add).then_inc(s_var, 1)
                if j == NC + 1:
                    dve.wait_ge(s_std, 4)
                if NC + 1 <= j <= 2 * NC:
                    for t in range(BPC * (j - NC - 1), BPC * (j - NC)):
                        dve.tensor_scalar(LNO[:, t, :].rearrange("p (g n) -> p g n", g=4), o_first(t),
                                          MV[:, t, 0:1], ST[:, 5, t:t + 1], ALU.subtract, ALU.mult).then_inc(s_ln, 1)
                work, k = SIDE_AT.get(j, (None, 0))
                if work == "L":
                    dve.wait_ge(s_sf, SIDE_USE[work, k] + 1)
                    dve.tensor_scalar(LNT[:, k * CH:(k + 1) * CH], PS[:, 6 + SIDE_USE[work, k] % 2, :],
                                      COLS[:, R_GAMMA:R_GAMMA + 1], COLS[:, R_BETA:R_BETA + 1],
                                      ALU.mult, ALU.add).then_inc(s_lt, 1)

            dve.wait_ge(s_tr, 1 + USES)
            dve.wait_ge(s_pv, PV0 + NS * NG)
            dve.wait_ge(s_xs, 16)
            number = XS[:, :, P]
            link(dve.tensor_scalar(YIF[:, :], number, 0.0, None, ALU.is_equal))
            link(dve.tensor_tensor(YIF[:, :], YIF[:, :], SPARE[:, :], ALU.mult))
            link(dve.tensor_tensor(YIF[:, :], YIF[:, :], number, ALU.add))
            link(dve.tensor_scalar(YIF[:, :], YIF[:, :], -1.0, None, ALU.add))
            dve.tensor_copy(YI[:, :], YIF[:, :]).then_inc(s_yi, 1)
            for j in range(NT + 2):
                if j < NT:
                    dve.wait_ge(s_us, j + 1)
                    dve.wait_ge(s_u, j + 1)
                    if j >= 2:
                        dve.wait_ge(s_ut, j - 1)
                    dve.tensor_tensor(UA[:, j % 2, :], PS[:, j % 2, 0:HID], SG[:, j % 2, :], ALU.mult)\
                       .then_inc(s_ua, 1)
                if j >= 2:
                    i = j - 2
                    dve.wait_ge(s_y, i + 1)
                    if i >= YRING:
                        dve.wait_ge(s_ys[i % YRING], 16 * (i // YRING))
                    dve.tensor_copy(YS[:, i % YRING, :], PS[:, 4 + i % 2, 0:P]).then_inc(s_ye, 1)
                first_attention(j)

            dve.wait_ge(s_so, NC)
            dve.wait_ge(s_xr, 16)
            for c in range(NC + 1):
                if c < NC:
                    x2 = X2[:, 4 * c:4 * c + 4, :]
                    dve.wait_ge(s_yl[c], 16)
                    dve.tensor_tensor(x2, x2, YN[:, 4 * c:4 * c + 4, :], ALU.add).then_inc(s_f, 1)
                if c >= 1:
                    tiles = slice(4 * c - 4, 4 * c)
                    rs = RS[:, tiles, :]
                    dve.wait_ge(s_fs, c)
                    link(dve.tensor_tensor(rs, rs, X2[:, tiles, :], ALU.mult))
                    link(dve.tensor_tensor(rs, rs, SO[:, tiles, :], ALU.mult))
                    dve.tensor_tensor(rs, rs, XR[:, tiles, :], ALU.add).then_inc(s_o, 1)


_INS = ['L0_attn_x', 'L0_attn_Wq', 'L0_attn_Wk', 'L0_attn_Wv', 'L0_attn_Wo', 'L0_attn_gamma', 'L0_attn_beta',
        'L0_ffn_ln1_w', 'L0_ffn_ln2_w', 'L0_ffn_Wq', 'L0_ffn_bq', 'L0_ffn_Wk', 'L0_ffn_bk', 'L0_ffn_Wv',
        'L0_ffn_bv', 'L0_ffn_qn_w', 'L0_ffn_kn_w', 'L0_ffn_Wg', 'L0_ffn_bg', 'L0_ffn_Wo', 'L0_ffn_bo',
        'L0_ffn_Wr', 'L0_ffn_br', 'L0_ffn_W1', 'L0_ffn_b1', 'L0_ffn_W2', 'L0_ffn_b2']


def rope_tables():
    inv = (np.float32(1.0) / np.float32(10000.0) ** (np.arange(0, HD, 2, dtype=np.float32) / np.float32(HD)))
    f = np.arange(S, dtype=np.float32)[:, None] * inv.astype(np.float32)[None, :]
    return np.cos(f).astype(np.float32), np.sin(f).astype(np.float32)


def kernel(**inputs):
    import concourse.bacc as _bacc
    from concourse.bass_utils import run_bass_kernel_spmd as _run

    nc = _bacc.Bacc("TRN2", target_bir_lowering=False, num_devices=1)
    cos, sin = rope_tables()
    named = [(name, np.ascontiguousarray(inputs[name])) for name in _INS] + [("rope_cos", cos), ("rope_sin", sin)]
    arrays, args = {}, []
    for name, a in named:
        arrays[f"in_{name}"] = a
        args.append(nc.dram_tensor(f"in_{name}", a.shape, mybir.dt.from_np(a.dtype), kind="ExternalInput").ap())
    out = nc.dram_tensor("out_0", (1, S, P), F32, kind="ExternalOutput").ap()
    build(nc, *args, out)
    r = _run(nc, [arrays], core_ids=[0])
    return r.results[0]["out_0"]
```

```python
import numpy as np
from contextlib import ExitStack

import concourse.bass as bass
from concourse import mybir

F32 = mybir.dt.float32
BF16 = mybir.dt.bfloat16
I32 = mybir.dt.int32
U32 = mybir.dt.uint32
ALU = mybir.AluOpType
ACT = mybir.ActivationFunctionType
AX = mybir.AxisListType.X

P = 128
S = 2048
T = S // P
NH, HD = 16, 8
NKV = 4
HG = 4
NA = NH // HG
NG = 2 * NA
CH = 512
NC = S // CH
BPC = CH // P
NE, HID = 8, 256
SCALE = float(HD) ** -0.5
PARTS = 3
STACK = PARTS * PARTS * HD
SHIFT = 96
NEG = -1.0e30
BOUND = 80.0

ORDER = list(range(NC))[::-1]
STEPS = [(c, kb) for c in ORDER for kb in range(BPC * (c + 1))]
NS = len(STEPS)
TILES = 2 * NS
RING = 8
LAG = 2
ITEMS = [(qb, kc) for qb in range(BPC, T)[::-1] for kc in range(1, qb // BPC + 1)[::-1]]
ITEMS += [(qb, 0) for qb in range(BPC, T)[::-1]]
LATE_ITEMS = len(ITEMS)
FIRST_NEEDED = next(i for i, (qb, kc) in enumerate(ITEMS) if kc == 0)
ITEMS += [(qb, 0) for qb in range(BPC)]
UNITS = len(ITEMS) * HG
DIAG = 2 * T
EARLY = NS - BPC - 1

SLOT_GROUP = [0, 1, NA, 2, NA + 1, 3, NA + 2, NA + 3]
PAIRS = NG // 2 - 1
HEAD = 3
LAST_MAX = NS - 7
SHIFT_PARTS, SHIFT_TURN = LAST_MAX + 1, LAST_MAX + 3


def place(i, side):
    return i + (NA - 1) * (1 - side)


def step_width(s):
    c, kb = STEPS[s]
    return CH - max(0, kb - BPC * c) * P


def item_width(i):
    qb, kc = ITEMS[i]
    return (qb % BPC + 1) * P if kc == qb // BPC else CH


def spread(steps):
    def step_time(s):
        return step_width(s) + 400

    def item_time(i):
        return item_width(i) + 64

    total, work = sum(map(step_time, steps)), HG * sum(map(item_time, range(len(ITEMS))))
    out, u, done, own = [], 0, 0, 0
    for n, s in enumerate(steps):
        own += step_time(s)
        mine = []
        while u < UNITS and (n == len(steps) - 1 or done * total < own * work):
            mine.append((u // HG, u % HG))
            done += item_time(u // HG)
            u += 1
        out.append(mine)
    return out


PAIR_STEPS = [s for s in range(HEAD, NS)] + [s for s in range(LAST_MAX + 1)]
PAIR_SPREAD = spread(PAIR_STEPS)
SPREAD = {"first": [[]] * HEAD + PAIR_SPREAD[:NS - HEAD],
          "second": PAIR_SPREAD[NS - HEAD:] + [[]] * (NS - LAST_MAX - 1),
          "whole": [[]] * HEAD + spread(range(HEAD, LAST_MAX + 1)) + [[]] * (NS - LAST_MAX - 1),
          "none": [[]] * NS}


def maxima_of(peeled, side):
    return ("whole", "none")[side] if peeled else ("first", "second")[side]


def units_at(kind, s):
    u = SPREAD[kind][s] if s < NS else []
    a = (len(u) + 3) // 4
    b = a + (len(u) + 2) // 4
    return u[:a], u[a:b], u[b:]


def takes_shift(peeled, side):
    return side == (0 if peeled else 1)


def stream(i, peeled, stage):
    for s in range(HEAD, NS):
        stage(i, 0, s, peeled)
    for s in range(NS):
        stage(i, 1, s, peeled)
    for s in range(HEAD):
        if not peeled:
            stage(i, 2, s, peeled)
    for s in range(NS, NS + LAG + 1):
        if peeled:
            stage(i, 1, s, peeled)


def behind(side, s, d):
    return (side, s - d) if s >= d else (side - 1, s - d + NS)


def chunk_end(c):
    return max(s for s in range(NS) if STEPS[s][0] == c)


def ending(s):
    return next((c for c in ORDER if chunk_end(c) == s), None)


def turn_use(i, side, c, peeled):
    k = ORDER.index(c)
    later = takes_shift(peeled, side) and chunk_end(c) + LAG + 1 > SHIFT_TURN
    return (2 * NC + 1) * i + (NC + (1 if peeled else 0)) * side + k + (1 if later else 0)


def shift_use(i, peeled):
    before = sum(1 for c in ORDER if chunk_end(c) + LAG + 1 <= SHIFT_TURN)
    return (2 * NC + 1) * i + (0 if peeled else NC) + before


USES = NC * NG + NA


def whole_ring():
    order = []
    for s in range(HEAD, NS):
        a, b, c = ([item * HG + hh for item, hh in part] for part in units_at("whole", s))
        order += a + b
        if s > LAG and ending(s - LAG - 1) is not None:
            order.append(("turn", ending(s - LAG - 1)))
        order += c
        if s == SHIFT_TURN:
            order.append("shift")
    return order


WHOLE_RING = whole_ring()
WHOLE_BANK = {what: (4, 5, 7)[n % 3] for n, what in enumerate(WHOLE_RING)}
LAST_RING_TURN = [what[1] for what in WHOLE_RING if isinstance(what, tuple)][-1]


def unit_bank(u, peeled):
    return WHOLE_BANK[u] if peeled else 4 + u % 2


def turn_bank(what, side, peeled):
    return WHOLE_BANK.get(what, 7) if peeled and side == 0 else 7


def diag_index(s):
    return sum(1 for c, kb in STEPS[:s] if kb >= BPC * c)


R_GAMMA, R_BETA, R_LN1, R_LN2, R_BG, R_QN, R_KN = range(7)
NROWS = 7


U_W, U_X, U_A, U_P, U_F = 0, 2, 6, 14, 30
NSRC = 16
SLOTS = 4
FFN_AT = {2: ("C", 0), 4: ("O", 0), 5: ("O", 1), 6: ("G", 0), 7: ("G", 1), 8: ("O", 2), 9: ("W", 0), 10: ("G", 2),
          11: ("O", 3), 12: ("W", 1), 13: ("G", 3), 14: ("W", 2), 15: ("H", 0), 16: ("W", 3), 17: ("H", 1),
          18: ("H", 2), 19: ("H", 3), 20: ("R", 0), 21: ("N", 0), 22: ("K", 0)}
FFN_USE = {work: n for n, work in enumerate(FFN_AT.values())}
MOVE_AT = {23: (0, 1, 2, 3), 28: (4, 5, 6), 29: (7, 8, 9), 30: (10, 11, 12), 31: (13, 14, 15)}

NT = S // P + NE - 1
ROW = P + 1
YRING = 4
SIDE_AT = {-1: ("X", 0), 0: ("X", 1), 3: ("X", 2), 6: ("X", 3), 8: ("L", 0), 9: ("L", 1), 10: ("X", 4),
           11: ("L", 2), 12: ("L", 3), 13: ("S", 0), 14: ("X", 5), 15: ("S", 1), 16: ("S", 2), 17: ("S", 3)}
SIDE_USE = {work: n for n, work in enumerate(SIDE_AT.values())}
EX0, PV0 = 2, RING // 2
NLOAD = 2 * PARTS


def source(n):
    a, isk, c = n // (2 * NC), (n // NC) % 2, n % NC
    return a, isk, (c + 1) % NC if a and not isk else c


def source_use(n):
    return U_A + n if n < NSRC // 2 else U_F + n - NSRC // 2


def reads(u):
    return u + 1 if u < U_X else u + 1 - NC


def build(nc, x, aWq, aWk, aWv, aWo, gamma, beta, ln1, ln2, Wq, bq, Wk, bk, Wv, bv, qn, kn, Wg, bg,
          Wo, bo, Wr, br, W1, b1, W2, b2, rope_cos, rope_sin, out):
    with ExitStack() as ctx:
        def sb(name, shape, dt=F32):
            return ctx.enter_context(nc.sbuf_tensor(name, shape, dt))

        def sem(name):
            return ctx.enter_context(nc.semaphore(name))

        XN = sb("XN", [P, T, P])
        MB = sb("MB", [P, 2, HG, S], BF16)
        QA = sb("QA", [P, 2, HG, S], BF16)
        KA = sb("KA", [P, 2, HG, S], BF16)
        PR = sb("PR", [P, RING, 2, CH])
        VX = sb("VX", [P, NG, T, HG * HD])
        VA = sb("VA", [P, 2, T, HG, 32])
        AO = sb("AO", [P, NG, T, HG * HD])
        WT = sb("WT", [P, 4, P])
        WN = sb("WN", [P, P + 192])
        WQKV = sb("WQKV", [P, 192])
        WO1 = sb("WO1", [P, P])
        WRS = sb("WRS", [P, NE])
        WG = sb("WG", [P, P])
        ROWS = sb("ROWS", [R_QN, P])
        COLS = sb("COLS", [P, NROWS])
        QKVB = sb("QKVB", [P, 192])
        BOB = sb("BOB", [P, P])
        BRB = sb("BRB", [P, NE])
        QKN = sb("QKN", [P, 2, HD])
        COS = sb("COS", [P, T, HD // 2])
        SIN = sb("SIN", [P, T, HD // 2])
        ID = sb("ID", [P, P])
        IDB = sb("IDB", [P, P], BF16)
        CM = sb("CM", [P, P], BF16)
        TRI = sb("TRI", [P, P])
        EARLIER = sb("EARLIER", [P, (T + 1) * NE])
        ONES = sb("ONES", [P, P])
        ZERO = sb("ZERO", [P, ROW])
        J128 = sb("J128", [P, NT])
        TILE = sb("TILE", [P, NT])
        BEFORE = sb("BEFORE", [P, NE, NE])
        OWN = sb("OWN", [PARTS * NE, NE])
        B12 = sb("B12", [PARTS * NE, 5 * P], BF16)
        CNT = sb("CNT", [P, 4, NE])
        TOK = sb("TOK", [P, T])
        SPARE = sb("SPARE", [P, NT])
        POSF = sb("POSF", [P, T])
        POS = sb("POS", [P, T], U32)
        EIDF = sb("EIDF", [P, NT])
        EID = sb("EID", [P, NT], I32)
        YIF = sb("YIF", [P, NT])
        YI = sb("YI", [P, NT], U32)
        RANK = sb("RANK", [P, NE])
        QKM = sb("QKM", [P, 2])
        KNS = sb("KNS", [P, 1])
        MHALF = sb("MHALF", [P, T])
        HBG = sb("HBG", [P, 1])
        QNX = sb("QNX", [1, 2, P])
        BN = sb("BN", [P, T, 6])
        MV = sb("MV", [P, T, 2])
        ST = sb("ST", [P, 8, T])
        MP = sb("MP", [P, HG * T, NC])
        NM = sb("NM", [P, HG * T])
        NMR = sb("NMR", [P, 2, HG * T], BF16)
        MROW = sb("MROW", [2 * HG * T, P], BF16)
        OT = sb("OT", [P, 2, CH])
        RL = sb("RL", [P, 2, BPC, HG])
        MX = sb("MX", [P, 2, T])

        mbf = MB[:, :, :, :].rearrange("p a h s -> p (a h s)").bitcast(F32)
        W1S = mbf[:, 0:4096].rearrange("p (e n) -> p e n", e=NE)
        W2S = mbf[:, 4096:6144].rearrange("p (e m n) -> p e m n", e=NE, m=2)
        XT = mbf[:, 6144:8192]
        XTF = VA[:, 1, :, :, :].rearrange("p t h n -> p (t h n)")
        SP3 = QA[:, 1, :, :].rearrange("p h s -> p (h s)")[:, 0:SLOTS * PARTS * CH]\
            .rearrange("p (a i n) -> p a i n", a=SLOTS, i=PARTS)
        RES = OT
        prf = PR[:, :, :, :].rearrange("p a b c -> p (a b c)")
        WIN = prf[:, 1024:1536].rearrange("p (a n) -> p a n", a=4)
        QF = prf[:, 0:4096].rearrange("p (a t n) -> p a t n", a=2, t=T)
        RT = prf[:, 5120:5120 + 2560].rearrange("p (t h d) -> p t h d", t=T, h=NH + NKV)
        RTMP = prf[:, 2560:2560 + 2560].rearrange("p (a t h d) -> p a t h d", a=2, t=T, h=NH + NKV)
        SQF = prf[:, 0:2560].rearrange("p (t h d) -> p t h d", t=T, h=NH + NKV)
        aof = AO[:, :, :, :].rearrange("p g t n -> p (g t n)")
        QKV1 = aof[:, 0:T * 192].rearrange("p (t n) -> p t n", t=T)
        HS = aof[:, T * 192:T * 192 + 3 * T * (NH + NKV)].rearrange("p (a n) -> p a n", a=3)
        def quarters(stack, b):
            f = stack[:, b, :, :].rearrange("p h s -> p (h s)").bitcast(F32)
            return f[:, 0:S], f[:, S:2 * S]

        def by_tile(f):
            return f.rearrange("p (t n) -> p t n", t=T)

        OG, O1T = quarters(QA, 0)
        O2N = by_tile(OG)
        qa0 = QA[:, 0, :, :].rearrange("p h s -> p (h s)").bitcast(F32)
        H2 = qa0[:, 0:T * ROW].rearrange("p (t n) -> p t n", t=T)
        XS = qa0[:, 0:NT * ROW].rearrange("p (t n) -> p t n", t=NT)
        X2, RS = map(by_tile, quarters(KA, 0))
        GE = VA[:, 0, :, :, :].rearrange("p t h n -> p (t h n)")
        SQ = by_tile(GE)
        BF = GE[0:NE, 0:5 * P]
        BP = GE[0:NE, 5 * P:5 * P + 5 * P * PARTS // 2].bitcast(BF16).rearrange("p (i n) -> p i n", i=PARTS)
        LG = GE[:, 0:4 * T * NE].rearrange("p (a t e) -> p a t e", a=4, t=T)
        TE = GE[0:PARTS * NE, 4 * T * NE:4 * T * NE + NT * P // 2].bitcast(BF16)\
            .rearrange("p (j n) -> p j n", j=NT)
        CB = XT[:, CH:CH + P]
        EQ = XT[:, 0:NT * NE].rearrange("p (j e) -> p j e", j=NT)
        XG = QA[:, 1, :, :].rearrange("p h s -> p (h s)").bitcast(F32)[:, 0:NT * P]
        LNO_, LNT = quarters(KA, 1)
        LNO = by_tile(LNO_)
        SO = LNO
        XR = XN
        SG = prf[:, 0:2 * HID].rearrange("p (a n) -> p a n", a=2)
        UA = prf[:, 512:512 + 2 * HID].rearrange("p (a n) -> p a n", a=2)
        UT = prf[:, 1024:1024 + 2 * HID].rearrange("p (a n) -> p a n", a=2)
        YS = prf[:, 1536:1536 + YRING * P].rearrange("p (a n) -> p a n", a=YRING)
        YN = by_tile(prf[:, 2048:2048 + S])

        PS = ctx.enter_context(nc.psum_tensor("PS", [P, 8, CH], F32))

        def parts_tensor(name, tokens):
            return nc.dram_tensor(name, [PARTS, NG, HD, HG, tokens], BF16, kind="Internal").ap()

        QP = {"first": parts_tensor("q_first", CH), "late": parts_tensor("q_late", S - CH)}
        KP = {"first": parts_tensor("k_first", CH), "late": parts_tensor("k_late", S - CH)}
        SH = nc.dram_tensor("shift_rows", [NG, 2, HG, T, P], BF16, kind="Internal").ap()

        XGD = nc.dram_tensor("expert_tokens", [NT * P, ROW], F32, kind="Internal").ap()
        YD = nc.dram_tensor("expert_outputs", [S + NT * P, P], F32, kind="Internal").ap()

        s_x = [sem(f"x_loaded_{c}") for c in range(NC)]
        s_seen = sem("probabilities_seen_by_pool")
        s_o2 = sem("second_output_regrouped")
        s_xr = sem("x_reloaded")
        s_w = sem("projection_weights_loaded")
        s_rw = sem("rope_and_norm_weights_loaded")
        s_wl = sem("later_weights_loaded")
        s_qx = sem("norm_weight_rows_ready")
        s_res = sem("remainder_ready")
        s_r2 = sem("second_halves_rotated")
        s_id = sem("identity_built")
        s_xt = sem("xn_turned")
        s_vc = sem("first_values_placed")
        s_sq = sem("q_and_k_squared")
        s_moe = sem("moe_weights_loaded")
        s_const = sem("constants_built")
        s_zero = sem("stack_constants_built")
        s_v = sem("vector_chain")
        s_g = sem("pool_chain")
        s_var = sem("variances_ready")
        s_std = sem("deviations_ready")
        s_xn = sem("xn_ready")
        s_wn = sem("projection_weights_ready")
        s_qf = sem("q_normed")
        s_kf = sem("k_expanded")
        s_xb = sem("xn_biased")
        s_vx = sem("values_placed")
        s_ft = sem("front_bank_filled")
        s_fr = sem("front_bank_read")
        s_hi = sem("first_part_ready")
        s_mid = sem("second_part_ready")
        s_lo = sem("third_part_ready")
        s_wr = [sem(f"parts_written_{a}") for a in range(SLOTS)]
        s_ld = [sem("stack_loaded_0"), sem("stack_loaded_1")]
        s_lq = [sem("later_q_loaded_0"), sem("later_q_loaded_1")]
        s_lk = [sem("later_k_loaded_0"), sem("later_k_loaded_1")]
        s_ml = sem("max_stacks_late_loaded")
        s_mf = sem("max_stacks_first_loaded")
        s_shw = sem("shift_rows_stored")
        s_cr = sem("constant_shift_ready")
        s_va = sem("value_tiles_ready")
        s_sc = sem("scores_ready")
        s_ex = sem("probabilities_ready")
        s_mk = sem("probabilities_masked")
        s_pv = sem("value_products_done")
        s_mm = sem("max_scores_ready")
        s_mr = sem("max_scores_read")
        s_oe = sem("outputs_read")
        s_t = sem("transposes_ready")
        s_tr = sem("transposes_read")
        s_ch = sem("maxima_reduced")
        s_rl = sem("denominators_inverted")
        s_wgz = sem("gate_weight_zeroed")
        s_h2 = sem("ffn_tile_normed")
        s_nm = sem("shift_parts_ready")
        s_ff = sem("ffn_bank_filled")
        s_fu = sem("ffn_bank_read")
        s_ms = sem("ffn_mean_squares_ready")
        s_rs = sem("ffn_scales_ready")
        s_cb = sem("tile_counts_ready")
        s_er = sem("earlier_built")
        s_gt = sem("gated_output_ready")
        s_ng = sem("gate_bias_halved")
        s_ln = sem("ln_operand_ready")
        s_sig = sem("gate_sigmoid_ready")
        s_oh = sem("onehot_ready")
        s_zd = sem("expert_tokens_zeroed")
        s_bl = sem("expert_biases_loaded")
        s_bp = sem("expert_bias_parts_ready")
        s_bs = sem("expert_bias_parts_stacked")
        s_pos = sem("places_ready")
        s_eid = sem("tile_experts_ready")
        s_mv = sem("tokens_moved")
        s_xs = sem("expert_tokens_loaded")
        s_yi = sem("output_rows_ready")
        s_sf = sem("side_bank_filled")
        s_xe = sem("expert_tokens_turned")
        s_lt = sem("layernorm_turned")
        s_so = sem("first_attention_projected")
        s_u = sem("expert_up_ready")
        s_us = sem("expert_sigmoid_ready")
        s_ua = sem("expert_act_ready")
        s_ut = sem("expert_act_turned")
        s_uc = sem("turned_act_copied")
        s_y = sem("expert_down_done")
        s_ye = sem("expert_output_copied")
        s_ys = [sem(f"expert_output_stored_{a}") for a in range(YRING)]
        s_yl = [sem(f"expert_outputs_loaded_{c}") for c in range(NC)]
        s_f = sem("ffn_out_ready")
        s_fm = sem("ffn_out_times_first_attention")
        s_fs = sem("ffn_sigmoid_ready")
        s_o = sem("result_ready")
        s_out = sem("result_stored")

        def bcast_rows(v, n):
            return v.rearrange("(a n) -> a n", a=1).broadcast_to([P, n])

        def o_first(t):
            return AO[:, NA:NG, t, :]

        def row(v):
            return v.rearrange("(a n) -> a n", a=1)

        first_weights = [(WIN[:, 0, :], aWq), (WIN[:, 1, :], aWk), (WIN[:, 2, :], aWv), (WIN[:, 3, :], aWo),
                         (ROWS[R_LN1:R_LN1 + 1, :], row(ln1)),
                         (ROWS[R_GAMMA:R_GAMMA + 1, :], row(gamma)), (ROWS[R_BETA:R_BETA + 1, :], row(beta)),
                         (ROWS[R_LN2:R_LN2 + 1, :], row(ln2)),
                         (ROWS[R_BG:R_BG + 1, :], row(bg).broadcast_to([NH, HD])),
                         (QKN[:, 0, :], bcast_rows(qn, HD)), (QKN[:, 1, :], bcast_rows(kn, HD)),
                         (WQKV[:, 0:128], Wq), (WQKV[:, 128:160], Wk), (WQKV[:, 160:192], Wv)]
        rope_weights = [(QKVB[:, 0:128], bcast_rows(bq, 128)), (QKVB[:, 128:160], bcast_rows(bk, 32)),
                        (QKVB[:, 160:192], bcast_rows(bv, 32)),
                        (COS[:, :, :], rope_cos.rearrange("(t p) n -> p t n", p=P)),
                        (SIN[:, :, :], rope_sin.rearrange("(t p) n -> p t n", p=P))]
        later_weights = [(BOB[:, :], bcast_rows(bo, 128)), (BRB[:, :], bcast_rows(br, NE)),
                         (WO1[:, :], Wo), (WRS[:, :], Wr)]

        h2 = HD // 2

        def rope(table):
            return table[:, :, :].unsqueeze(2).broadcast_to([P, T, NH + NKV, h2])

        block = ctx.enter_context(nc.Block())

        @block.sync
        def _(sp):
            xv = x[0].rearrange("(t p) n -> p t n", p=P)
            for c in range(4):
                sp.dma_start(XN[:, 4 * c:4 * c + 4, :], xv[:, 4 * c:4 * c + 4, :]).then_inc(s_x[c], 16)
            for dst, src in first_weights:
                sp.dma_start(dst, src).then_inc(s_w, 16)
            for dst, src in rope_weights:
                sp.dma_start(dst, src).then_inc(s_rw, 16)
            sp.wait_ge(s_cr, 1)
            for g in range(NA):
                sp.dma_start(SH[g].rearrange("i h t s -> (i h t) s"), MROW[:, :]).then_inc(s_shw, 16)
            def store_parts(n):
                a, isk, c = source(n)
                dst = (KP if isk else QP)["late" if c else "first"]
                lo = (c - 1) * CH if c else 0
                sp.wait_ge(s_lo, n + 1)
                groups = slice(NA - NA * a, 2 * NA - NA * a)
                sp.dma_start(dst[:, groups, :, :, lo:lo + CH].rearrange("i g d h s -> (g d h) i s"),
                             SP3[:, n % SLOTS, :, :]).then_inc(s_wr[n % SLOTS], 16)

            def stored(sources):
                for n in sources:
                    sp.wait_ge(s_wr[n % SLOTS], 16 * (n // SLOTS + 1))

            def tokens(piece):
                return slice(0, CH) if piece == "first" else slice(CH, S)

            r = PARTS * HD

            def load_q(q, g, piece, landed):
                for j in range(PARTS):
                    sp.dma_start(q[r * j:r * (j + 1), :, tokens(piece)],
                                 QP[piece][:, g].rearrange("i d h s -> i d (h s)")).then_inc(landed, 16)

            def load_k(k, g, piece, landed):
                n = HG * (CH if piece == "first" else S - CH)
                for j in range(PARTS):
                    sp.dma_start(k[r * j:r * (j + 1), :, tokens(piece)],
                                 KP[piece][j, g].rearrange("d h s -> d (h s)").unsqueeze(0)
                                 .broadcast_to([PARTS, HD, n])).then_inc(landed, 16)

            def load_late_q(j):
                load_q(QA[:, j % 2], SLOT_GROUP[j], "late", s_lq[j % 2])

            def load_late_k(j):
                load_k(KA[:, j % 2], SLOT_GROUP[j], "late", s_lk[j % 2])

            def load_first(j):
                load_k(KA[:, j % 2], SLOT_GROUP[j], "first", s_ld[j % 2])
                load_q(QA[:, j % 2], SLOT_GROUP[j], "first", s_ld[j % 2])
                if SLOT_GROUP[j] < NA:
                    load_shift(j)

            def load_shift(j):
                sp.dma_start(QA[SHIFT:SHIFT + 2, j % 2, :, :],
                             SH[SLOT_GROUP[j]].rearrange("i h t s -> i h (t s)")).then_inc(s_ld[j % 2], 16)

            def load_max(m, piece, landed):
                load_q(MB[:, 0], NA + m, piece, landed)
                load_k(MB[:, 1], NA + m, piece, landed)

            q0, k0 = NSRC - 2 * NC, NSRC - NC
            for n in range(q0):
                store_parts(n)
            stored(range(q0 - SLOTS, q0))
            load_max(0, "late", s_ml)
            load_max(0, "first", s_mf)
            for n in range(q0, k0 + 1):
                store_parts(n)
            sp.wait_ge(s_zero, 1)
            sp.wait_ge(s_shw, 16 * NA)
            stored(range(q0, q0 + NC - 1))
            load_late_q(0)
            store_parts(k0 + 1)
            stored((q0 + NC - 1, k0))
            load_first(0)
            store_parts(k0 + 2)
            store_parts(k0 + 3)
            stored(range(k0 + 1, NSRC))
            load_late_k(0)
            sp.wait_ge(s_zero, 2)
            load_late_q(1)
            load_late_k(1)
            load_first(1)
            for dst, src in later_weights:
                sp.dma_start(dst, src).then_inc(s_wl, 16)
            sp.wait_ge(s_wgz, 1)
            for h in range(NH):
                sp.dma_start(WG[h * HD:(h + 1) * HD, h * HD:(h + 1) * HD], Wg).then_inc(s_wl, 16)
            sp.wait_ge(s_const, 1)
            sp.dma_start(XGD.rearrange("(j p) n -> p j n", p=P), ZERO[:, :].unsqueeze(1).broadcast_to([P, NT, ROW]))\
              .then_inc(s_zd, 16)
            for j in range(NG):
                m = j // 2
                ends_maxima = takes_shift(j >= 2 * PAIRS, j % 2)
                if ends_maxima and m < NA - 1:
                    sp.wait_ge(s_mm, UNITS * m + HG * LATE_ITEMS)
                    load_max(m + 1, "late", s_ml)
                if ends_maxima:
                    sp.wait_ge(s_tr, shift_use(m, m == PAIRS) + 2)
                    sp.dma_start(SH[NA + m].rearrange("i h t s -> (i h t) s"), MROW[:, :]).then_inc(s_shw, 16)
                    sp.wait_ge(s_shw, 16 * (NA + m + 1))
                    load_shift(j + 1)
                if ends_maxima and m < NA - 1:
                    sp.wait_ge(s_mm, UNITS * (m + 1))
                    load_max(m + 1, "first", s_mf)
                if j < NG - 2:
                    sp.wait_ge(s_pv, PV0 + NS * j + EARLY + 1)
                    load_late_q(j + 2)
                    load_late_k(j + 2)
                    sp.wait_ge(s_pv, PV0 + NS * (j + 1))
                    load_first(j + 2)
                if j == 2 * PAIRS:
                    sp.wait_ge(s_mm, UNITS * NA)
                    sp.dma_start(W1S, W1.rearrange("e d f -> d e f")).then_inc(s_moe, 16)
                    sp.dma_start(W2S, W2.rearrange("e (m p) d -> p e m d", p=P)).then_inc(s_moe, 16)

            sp.wait_ge(s_pv, PV0 + NS * (NG - 1))
            sp.dma_start(BF[:, 0:4 * P], b1).then_inc(s_bl, 16)
            sp.dma_start(BF[:, 4 * P:5 * P], b2).then_inc(s_bl, 16)
            sp.wait_ge(s_bp, 1)
            for i in range(PARTS):
                sp.dma_start(B12[NE * i:NE * (i + 1), :], BP[:, i, :]).then_inc(s_bs, 16)
            sp.wait_ge(s_fu, FFN_USE["W", NC - 1] + 1)
            sp.dma_start(XR[:, :, :], xv).then_inc(s_xr, 16)
            sp.wait_ge(s_mv, 16 * T)
            sp.dma_start(XS, XGD.rearrange("(j p) n -> p j n", p=P)).then_inc(s_xs, 16)
            for a in range(YRING):
                sp.wait_ge(s_ys[a], 16 * ((NT + YRING - 1 - a) // YRING))
            yv = YD[0:S].rearrange("(t p) n -> p t n", p=P)
            for c in range(NC):
                sp.dma_start(YN[:, 4 * c:4 * c + 4, :], yv[:, 4 * c:4 * c + 4, :]).then_inc(s_yl[c], 16)
            ov = out[0].rearrange("(t p) n -> p t n", p=P)
            for c in range(NC):
                sp.wait_ge(s_o, c + 1)
                sp.dma_start(ov[:, 4 * c:4 * c + 4, :], RS[:, 4 * c:4 * c + 4, :]).then_inc(s_out, 16)
            sp.wait_ge(s_out, 16 * NC)

        @block.gpsimd
        def _(gp):
            n = [0]

            def link(ins):
                n[0] += 1
                ins.then_inc(s_g, 1)
                gp.wait_ge(s_g, n[0])

            link(gp.memset(ID[:, :], 0.0))
            gp.affine_select(out=ID[:, :], in_=ID[:, :], compare_op=ALU.not_equal, fill=1.0, base=0,
                             pattern=[[-1, P]], channel_multiplier=1).then_inc(s_id, 1)
            gp.wait_ge(s_id, 1)
            link(gp.tensor_copy(IDB[:, :], ID[:, :]))
            link(gp.memset(CM[:, :], 0.0))
            link(gp.affine_select(out=CM[:, :], in_=CM[:, :], compare_op=ALU.is_ge, fill=NEG, base=0,
                                  pattern=[[-1, P]], channel_multiplier=1))
            link(gp.memset(TRI[:, :], 1.0))
            link(gp.affine_select(out=TRI[:, :], in_=TRI[:, :], compare_op=ALU.is_gt, fill=0.0, base=0,
                                  pattern=[[1, P]], channel_multiplier=-1))
            link(gp.memset(ONES[:, :], 1.0))
            link(gp.memset(ZERO[:, :], 0.0))
            for j in range(NT):
                link(gp.memset(TILE[:, j:j + 1], float(j)))
                link(gp.memset(J128[:, j:j + 1], float(P * j)))
            link(gp.memset(BEFORE[:, :, :], 1.0))
            link(gp.affine_select(out=BEFORE[:, :, :], in_=BEFORE[:, :, :], compare_op=ALU.is_gt, fill=0.0, base=0,
                                  pattern=[[1, NE], [-1, NE]], channel_multiplier=0))
            link(gp.memset(OWN[:, :], 0.0))
            for i in range(PARTS):
                link(gp.affine_select(out=OWN[:, :], in_=OWN[:, :], compare_op=ALU.not_equal, fill=1.0, base=-NE * i,
                                      pattern=[[-1, NE]], channel_multiplier=1))
            for e in range(NE):
                link(gp.memset(RANK[:, e:e + 1], float(NE - e)))
            link(gp.memset(MHALF[:, :], -0.5))
            gp.sem_inc(s_const, 1)
            def clear_stack(stack):
                link(gp.memset(stack.rearrange("p h s -> p (h s)").bitcast(F32), 0.0))

            def clear_values(b):
                link(gp.memset(VA[:, b, :, :, :].rearrange("p t h n -> p (t h) n"), 0.0))
                link(gp.memset(VA[:, b, :, :, HD:HD + 1].rearrange("p t h n -> p (t h) n"), 1.0))

            def place_values(g):
                v = QKV1[:, :, 160 + g * HD:160 + (g + 1) * HD]
                gp.tensor_copy(VX[:, (g + NA - 1) % NA, :, :].rearrange("p t (h d) -> p t h d", h=HG),
                               v.unsqueeze(2).broadcast_to([P, T, HG, HD])).then_inc(s_vx, 1)
                gp.wait_ge(s_vx, g + 1)

            def build_values(at, b):
                gp.tensor_copy(VA[:, b, :, :, 0:HD],
                               VX[:, bass.ds(at, 1), :, :].rearrange("p o t (h d) -> p (o t) h d", h=HG))\
                  .then_inc(s_va, 1)

            clear_stack(QA[:, 0, :, :])
            clear_stack(KA[:, 0, :, :])
            link(gp.memset(KA[SHIFT:SHIFT + 2, 0, :, :].rearrange("p h s -> p (h s)"), 1.0))
            gp.sem_inc(s_zero, 1)
            clear_values(0)

            gp.wait_ge(s_fr, reads(U_F - 1))
            qk = QKV1[:, :, 0:160].rearrange("p t (h d) -> p t h d", d=HD)
            r2, tmp = RT[:, :, :, h2:HD], RTMP[:, 1, :, :, :]
            gp.wait_ge(s_rw, 16 * len(rope_weights))
            link(gp.tensor_tensor(r2, qk[:, :, :, 0:h2], rope(SIN), ALU.mult))
            link(gp.tensor_tensor(tmp, qk[:, :, :, h2:HD], rope(COS), ALU.mult))
            gp.tensor_tensor(r2, r2, tmp, ALU.add).then_inc(s_r2, 1)
            place_values(0)
            build_values(place(0, 0), 0)
            for g in range(1, NKV):
                place_values(g)
            clear_values(1)
            build_values(place(0, 1), 1)
            clear_stack(KA[:, 1, :, :])
            link(gp.memset(KA[SHIFT:SHIFT + 2, 1, :, :].rearrange("p h s -> p (h s)"), 1.0))
            for a in range(SLOTS):
                gp.wait_ge(s_wr[a], 16 * NSRC // SLOTS)
            clear_stack(QA[:, 1, :, :])
            gp.sem_inc(s_zero, 1)
            gp.wait_ge(s_xt, NC)
            gp.wait_ge(s_wl, 16 * (len(later_weights) + NH))
            for t in range(T):
                gp.tensor_tensor(XN[:, t, :], XN[:, t, :], BOB[:, :], ALU.add).then_inc(s_xb, 1)
            gp.wait_ge(s_vc, T)

            def slot(i, side, following, ffn_beside=False):
                g = 2 * i + side
                for s, (c, kb) in enumerate(STEPS):
                    if ffn_beside:
                        work, k = FFN_AT.get(s - 1, (None, 0))
                        if work == "W":
                            gp.wait_ge(s_ms, k + 1)
                            tiles = slice(BPC * k, BPC * (k + 1))
                            gp.tensor_tensor(ST[:, 7, tiles], ST[:, 6, tiles], MHALF[:, tiles], ALU.pow)\
                              .then_inc(s_rs, 1)
                        for t in MOVE_AT.get(s, ()):
                            if t == 0:
                                gp.wait_ge(s_pos, 1)
                                gp.wait_ge(s_zd, 16)
                                gp.wait_ge(s_h2, T)
                            gp.indirect_dma_start(XGD, bass.IndirectOffsetOnAxis(POS[:, t:t + 1], 0),
                                                  H2[:, t, :], None)\
                              .then_inc(s_mv, 16)
                    if kb < BPC * c:
                        continue
                    for p in range(2):
                        tile = 2 * s + p
                        gp.wait_ge(s_ex, EX0 + TILES * g + tile + 1)
                        v = PR[:, tile % RING, :, 0:P]
                        gp.sem_inc(s_seen, 1)
                        gp.affine_select(out=v, in_=v, compare_op=ALU.is_ge, fill=0.0, base=0,
                                         pattern=[[0, 2], [1, P]], channel_multiplier=-1).then_inc(s_mk, 1)
                if following is not None:
                    gp.wait_ge(s_pv, PV0 + NS * (g + 1))
                    build_values(following, side)

            with gp.Fori(0, PAIRS - 1) as i:
                slot(i, 0, place(i + 1, 0))
                slot(i, 1, place(i + 1, 1))
            slot(PAIRS - 1, 0, NG - 2)
            slot(PAIRS - 1, 1, NG - 1)
            link(gp.memset(EARLIER[:, :], 0.0))
            for t in range(1, T + 1):
                link(gp.affine_select(out=EARLIER[:, :], in_=EARLIER[:, :], compare_op=ALU.not_equal, fill=1.0,
                                      base=NE * t, pattern=[[-1, (T + 1) * NE]], channel_multiplier=1))
            gp.sem_inc(s_er, 1)
            slot(PAIRS, 0, None)
            gp.wait_ge(s_pv, PV0 + NS * (NG - 1))
            gp.wait_ge(s_tr, 1 + turn_use(PAIRS, 0, ORDER[0], True))
            gp.tensor_copy(O2N[:, :, 0:HG * HD], AO[:, NA - 1, :, :]).then_inc(s_o2, 1)
            gp.tensor_copy(O2N[:, :, HG * HD:P].rearrange("p t (g n) -> p t g n", g=NA - 1),
                           AO[:, 0:NA - 1, :, :].rearrange("p g t n -> p t g n")).then_inc(s_o2, 1)
            slot(PAIRS, 1, None, ffn_beside=True)
            gp.wait_ge(s_var, 4)
            gp.tensor_tensor(ST[:, 5, :], ST[:, 4, :], MHALF[:, :], ALU.pow).then_inc(s_std, 1)
            gp.wait_ge(s_yi, 1)
            for j in range(NT):
                gp.wait_ge(s_ye, j + 1)
                gp.indirect_dma_start(YD, bass.IndirectOffsetOnAxis(YI[:, j:j + 1], 0), YS[:, j % YRING, :], None)\
                  .then_inc(s_ys[j % YRING], 16)
            gp.wait_ge(s_so, NC)
            for c in range(NC):
                so = SO[:, 4 * c:4 * c + 4, :]
                gp.wait_ge(s_f, c + 1)
                gp.tensor_tensor(so, so, X2[:, 4 * c:4 * c + 4, :], ALU.mult).then_inc(s_fm, 1)

        @block.scalar
        def _(act):
            act.sem_inc(s_ex, EX0)

            act.wait_ge(s_var, 1)
            act.activation(ST[:, 1, :], ST[:, 0, :], ACT.Sqrt).then_inc(s_std, 1)
            act.wait_ge(s_w, 16 * len(first_weights))
            for a in range(2):
                act.activation(QNX[0:1, a, :].rearrange("p (g d h) -> p g d h", g=NA, d=HD),
                               QKN[0:1, a, :].unsqueeze(1).unsqueeze(3).broadcast_to([1, NA, HD, HG]),
                               ACT.Copy).then_inc(s_qx, 1)
            act.wait_ge(s_var, 2)
            act.activation(ST[:, 3, :], ST[:, 2, :], ACT.Sqrt).then_inc(s_std, 1)
            for c in range(NC):
                act.wait_ge(s_ft, U_X + c + 1)
                act.activation(XTF[:, c * CH:(c + 1) * CH], PS[:, (U_X + c) % 8, :], ACT.Copy).then_inc(s_xt, 1)

            def factor(n):
                return (1.0, SCALE, COLS[:, R_QN:R_QN + 1], KNS[:, 0:1])[n // 4]

            def first_part(n):
                act.wait_ge(s_ft, source_use(n) + 1)
                if n >= SLOTS:
                    act.wait_ge(s_wr[n % SLOTS], 16 * (n // SLOTS))
                act.activation(SP3[:, n % SLOTS, 0, :], PS[:, source_use(n) % 8, :], ACT.Copy, scale=factor(n))\
                   .then_inc(s_hi, 1)

            def second_part(n):
                act.wait_ge(s_res, n + 1)
                act.activation(SP3[:, n % SLOTS, 1, :], RES[:, n % 2, :], ACT.Copy).then_inc(s_mid, 1)

            def split(sources):
                for n in sources:
                    first_part(n)
                    if n > sources[0]:
                        second_part(n - 1)
                second_part(sources[-1])

            split(range(NSRC // 2))
            for t in range(T):
                act.wait_ge(s_ft, U_P + t + 1)
                act.activation(VX[:, NA:NG, t, :].rearrange("p g (h d) -> p g h d", h=HG),
                               PS[:, (U_P + t) % 8, 0:P].rearrange("p (d g h) -> p g h d", d=HD, g=4),
                               ACT.Copy).then_inc(s_vc, 1)
            act.wait_ge(s_const, 1)
            act.wait_ge(s_fr, reads(U_F - 1))
            act.activation(SQF[:, :, :, :], QKV1[:, :, 0:160].rearrange("p t (h d) -> p t h d", d=HD), ACT.Square)\
               .then_inc(s_sq, 1)
            act.wait_ge(s_var, 3)
            act.activation(HS[:, 1, :], HS[:, 0, :], ACT.Sqrt).then_inc(s_std, 1)
            act.wait_ge(s_qf, 1)
            for g in range(NKV):
                heads = QF[:, 1, :, g * HG * HD:(g + 1) * HG * HD].rearrange("p t (d h) -> p t d h", h=HG)
                k = RT[:, :, NH + g, :].unsqueeze(3).broadcast_to([P, T, HD, HG])
                act.activation(heads, k, ACT.Copy).then_inc(s_kf, 1)
            split(range(NSRC // 2, NSRC))

            def slot(g, with_gate):
                for s, (c, kb) in enumerate(STEPS):
                    q0 = max(0, kb - BPC * c) * P
                    for p in range(2):
                        tile = 2 * s + p
                        if p == 0:
                            act.wait_ge(s_pv, NS * g + s + 1)
                        act.wait_ge(s_sc, TILES * g + tile + 1)
                        act.activation(PR[:, tile % RING, :, 0:CH - q0],
                                       PS[:, 2 * p:2 * p + 2, 0:CH - q0], ACT.Exp).then_inc(s_ex, 1)
                    work, k = FFN_AT.get(s - 1, (None, None))
                    if with_gate and work == "G":
                        use = FFN_USE[work, k]
                        act.wait_ge(s_bs, 16 * PARTS)
                        act.wait_ge(s_ng, 1)
                        act.wait_ge(s_ff, use + 1)
                        act.activation(GE[:, k * CH:(k + 1) * CH], PS[:, 4 + use % 2, :], ACT.Tanh,
                                       bias=HBG[:, 0:1], scale=0.5).then_inc(s_sig, 1)

            with act.Fori(0, PAIRS) as i:
                slot(2 * i, False)
                slot(2 * i + 1, False)
            slot(2 * PAIRS, False)
            slot(2 * PAIRS + 1, True)

            def side(j):
                work, k = SIDE_AT.get(j, (None, 0))
                bank = PS[:, 6 + SIDE_USE.get((work, k), 0) % 2, :]
                if work == "X":
                    act.wait_ge(s_sf, SIDE_USE[work, k] + 1)
                    n = min(CH, NT * P - k * CH)
                    act.activation(XG[:, k * CH:k * CH + n], bank[:, 0:n], ACT.Copy, scale=COLS[:, R_LN2:R_LN2 + 1])\
                       .then_inc(s_xe, 1)
                if work == "S":
                    act.wait_ge(s_sf, SIDE_USE[work, k] + 1)
                    act.activation(SO[:, 4 * k:4 * k + 4, :].rearrange("p t n -> p (t n)"), bank, ACT.Copy)\
                       .then_inc(s_so, 1)

            act.wait_ge(s_pv, PV0 + NS * NG)
            side(-1)
            for j in range(NT + 1):
                if j < NT:
                    act.wait_ge(s_u, j + 1)
                    if j >= 2:
                        act.wait_ge(s_ua, j - 1)
                    act.activation(SG[:, j % 2, :], PS[:, j % 2, HID:2 * HID], ACT.Sigmoid).then_inc(s_us, 1)
                side(j)
                if j >= 1:
                    act.wait_ge(s_ut, j)
                    if j >= 3:
                        act.wait_ge(s_y, j - 2)
                    act.activation(UT[:, (j - 1) % 2, :], PS[:, 2 + (j - 1) % 2, 0:2 * P], ACT.Copy).then_inc(s_uc, 1)
            for c in range(NC):
                act.wait_ge(s_f, c + 1)
                act.activation(RS[:, 4 * c:4 * c + 4, :], X2[:, 4 * c:4 * c + 4, :], ACT.Sigmoid).then_inc(s_fs, 1)

        @block.tensor
        def _(pe):
            def front(u):
                if U_X <= u - 8 < U_A:
                    pe.wait_ge(s_xt, u - 8 - U_X + 1)
                elif u >= 8:
                    pe.wait_ge(s_fr, reads(u - 8))
                return PS[:, u % 8, :]

            pe.wait_ge(s_id, 1)
            pe.wait_ge(s_w, 16 * len(first_weights))
            bank = front(U_W)
            for k in range(4):
                last = pe.transpose(bank[:, k * P:(k + 1) * P], WIN[:, k, :], ID[:, :])
            last.then_inc(s_ft, 1)
            pe.wait_ge(s_qx, 2)
            bank = front(U_W + 1)
            for a in range(2):
                pe.transpose(bank[:, R_QN + a:R_QN + a + 1], QNX[0:1, a, :], ID[0:1, 0:1])
            pe.transpose(bank[:, 0:R_QN], ROWS[:, :], ID[0:R_QN, 0:R_QN]).then_inc(s_ft, 1)
            for c in range(NC):
                pe.wait_ge(s_xn, 4 * (c + 1))
                bank = front(U_X + c)
                for k in range(BPC):
                    last = pe.transpose(bank[:, k * P:(k + 1) * P], XN[:, 4 * c + k, :], ID[:, :])
                last.then_inc(s_ft, 1)
            pe.wait_ge(s_wn, 1)
            for n in range(NSRC // 2):
                bank = front(U_A + n)
                pe.wait_ge(s_xt, n % 4 + 1)
                pe.matmul(bank, WT[:, n // 4, :], XTF[:, (n % 4) * CH:(n % 4 + 1) * CH], start=True, stop=True)\
                  .then_inc(s_ft, 1)
            for t in range(T):
                bank = front(U_P + t)
                pe.matmul(bank[:, 0:P + 192], XTF[:, t * P:(t + 1) * P], WN[:, :], start=True, stop=True)\
                  .then_inc(s_ft, 1)
            pe.wait_ge(s_qf, 1 + NA)
            for n in range(NSRC // 2, NSRC):
                if n == 12:
                    pe.wait_ge(s_kf, NKV)
                bank = front(source_use(n))
                _, isk, c = source(n)
                for k in range(BPC):
                    last = pe.transpose(bank[:, k * P:(k + 1) * P], QF[:, isk, BPC * c + k, :], ID[:, :])
                last.then_inc(s_ft, 1)
            pe.wait_ge(s_fr, reads(U_F + NSRC // 2 - 1))
            pe.wait_ge(s_const, 1)

            def whole_ring_free(what):
                n = WHOLE_RING.index(what)
                before = WHOLE_RING[n - 3] if n >= 3 else n - 2
                if n == 2:
                    pe.wait_ge(s_tr, 1 + (2 * NC + 1) * PAIRS)
                elif before == "shift":
                    pe.wait_ge(s_tr, 2 + shift_use(PAIRS, True))
                elif isinstance(before, tuple):
                    pe.wait_ge(s_tr, 2 + turn_use(PAIRS, 0, before[1], True))
                else:
                    pe.wait_ge(s_mr, 3 + UNITS * PAIRS + before)

            def max_unit(i, item, hh, peeled):
                qb, kc = ITEMS[item]
                u = item * HG + hh
                diag = kc == qb // BPC
                w = item_width(item)
                bank = PS[:, unit_bank(u, peeled), :]
                if hh == 0 and item == 0:
                    pe.wait_ge(s_ml, 16 * NLOAD * (i + 1))
                if hh == 0 and item == FIRST_NEEDED:
                    pe.wait_ge(s_mf, 16 * NLOAD * (i + 1))
                if peeled:
                    whole_ring_free(u)
                else:
                    pe.wait_ge(s_mr, UNITS * i + u + 1)
                last = pe.matmul(bank[:, 0:w], MB[0:STACK, 0, hh, qb * P:(qb + 1) * P],
                                 MB[0:STACK, 1, hh, kc * CH:kc * CH + w], start=True, stop=not diag)
                if diag:
                    last = pe.matmul(bank[:, w - P:w], IDB[:, :], CM[:, :], start=False, stop=True)
                last.then_inc(s_mm, 1)

            def shift_turn(i, peeled):
                pe.wait_ge(s_nm, i + 1)
                if peeled:
                    whole_ring_free("shift")
                else:
                    pe.wait_ge(s_tr, shift_use(i, peeled) + 1)
                bank = PS[:, turn_bank("shift", 0, peeled), :].bitcast(BF16)
                pe.transpose(bank[:, 0:P], NMR[:, :, :].rearrange("p a n -> p (a n)"), IDB[:, :]).then_inc(s_t, 1)

            def scores(i, side, s, p):
                c, kb = STEPS[s]
                g, b = 2 * i + side, side % 2
                q0 = max(0, kb - BPC * c) * P
                pe.wait_ge(s_ex, TILES * g + 2 * s + p + 1)
                for k in range(2):
                    last = pe.matmul(PS[:, 2 * p + k, 0:CH - q0],
                                     KA[:, b, 2 * p + k, kb * P:(kb + 1) * P],
                                     QA[:, b, 2 * p + k, c * CH + q0:(c + 1) * CH], start=True, stop=True)
                last.then_inc(s_sc, 1)

            def values(i, side, s):
                c, kb = STEPS[s]
                g, b = 2 * i + side, side % 2
                q0 = max(0, kb - BPC * c) * P
                if kb == 0:
                    pe.wait_ge(s_oe, NC * g + ORDER.index(c) + 1)
                if kb >= BPC * c:
                    pe.wait_ge(s_mk, DIAG * g + 2 * diag_index(s + 1))
                pe.wait_ge(s_ex, EX0 + TILES * g + 2 * s + 2)
                for hh in range(HG):
                    last = pe.matmul(PS[32 * hh:32 * hh + 32, 6, q0:CH], VA[:, b, kb, hh, :],
                                     PR[:, (2 * s + hh // 2) % RING, hh % 2, 0:CH - q0],
                                     start=kb == 0, stop=kb == BPC * (c + 1) - 1)
                last.then_inc(s_pv, 1)

            def turn(i, side, c, peeled):
                g = 2 * i + side
                pe.wait_ge(s_oe, NC * g + ORDER.index(c) + 2)
                bank = turn_bank(("turn", c), side, peeled)
                if peeled and side == 0 and ("turn", c) in WHOLE_BANK:
                    whole_ring_free(("turn", c))
                else:
                    pe.wait_ge(s_tr, turn_use(i, side, c, peeled) + 1)
                    if peeled:
                        pe.wait_ge(s_mr, 2 + UNITS * NA)
                for k in range(BPC):
                    last = pe.transpose(PS[:, bank, k * P:(k + 1) * P], OT[:, c % 2, k * P:(k + 1) * P], ID[:, :])
                last.then_inc(s_t, 1)

            def stage(i, side, s, peeled):
                if s == 0:
                    pe.wait_ge(s_lq[side % 2], 16 * PARTS * (i + 1 + side // 2))
                    pe.wait_ge(s_ld[side % 2], 16 * (NLOAD + 1) * (i + 1 + side // 2))
                    pe.wait_ge(s_va, 2 * i + side + 1)
                if s == BPC:
                    pe.wait_ge(s_lk[side % 2], 16 * PARTS * (i + 1 + side // 2))
                parts = units_at(maxima_of(peeled, side), s) if side < 2 else ((), (), ())
                for p in range(2):
                    if s < NS:
                        scores(i, side, s, p)
                    for item, hh in parts[p]:
                        max_unit(i, item, hh, peeled)
                side_v, v = behind(side, s, LAG)
                if v < NS and side_v >= 0:
                    values(i, side_v, v)
                side_t, t = behind(side, s, LAG + 1)
                if ending(t) is not None and side_t >= 0:
                    turn(i, side_t, ending(t), peeled)
                for item, hh in parts[2]:
                    max_unit(i, item, hh, peeled)
                if s == SHIFT_TURN and takes_shift(peeled, side):
                    shift_turn(i, peeled)
                if peeled and side == 1:
                    ffn(s)

            def ffn(s):
                if s not in FFN_AT:
                    return
                work, k = FFN_AT[s]
                use = FFN_USE[work, k]
                bank = PS[:, 4 + use % 2, :]
                if work == "C":
                    pe.wait_ge(s_mr, 2 + UNITS * NA)
                    pe.wait_ge(s_tr, 2 + turn_use(PAIRS, 0, LAST_RING_TURN, True))
                    last = pe.matmul(bank[:, 0:1], TRI[:, :], ONES[:, 0:1], start=True, stop=True)
                if use >= 2:
                    pe.wait_ge(s_fu, use - 1)
                if work == "O":
                    pe.wait_ge(s_o2, 2)
                    for j in range(BPC):
                        last = pe.transpose(bank[:, j * P:(j + 1) * P], O2N[:, 4 * k + j, :], ID[:, :])
                if work == "G":
                    pe.wait_ge(s_fu, FFN_USE["O", k] + 1)
                    pe.wait_ge(s_wl, 16 * (len(later_weights) + NH))
                    last = pe.matmul(bank, WG[:, :], O1T[:, k * CH:(k + 1) * CH], start=True, stop=True)
                if work == "W":
                    pe.wait_ge(s_gt, k + 1)
                    for j in range(BPC):
                        t = 4 * k + j
                        last = pe.matmul(bank[:, j * P:(j + 1) * P], O1T[:, t * P:(t + 1) * P], WO1[:, :],
                                         start=True, stop=True)
                if work == "H":
                    pe.wait_ge(s_h2, 4 * (k + 1))
                    for j in range(BPC):
                        last = pe.transpose(bank[:, j * P:(j + 1) * P], H2[:, 4 * k + j, 0:P], ID[:, :])
                if work == "R":
                    pe.wait_ge(s_fu, FFN_USE["H", NC - 1] + 1)
                    for t in range(T):
                        last = pe.matmul(bank[:, t * NE:(t + 1) * NE], XT[:, t * P:(t + 1) * P], WRS[:, :],
                                         start=True, stop=True)
                if work == "N":
                    pe.wait_ge(s_oh, 1)
                    last = pe.matmul(bank[:, 0:1], LG[:, 3, :, :].rearrange("p t e -> p (t e)"), ONES[:, 0:1],
                                     start=True, stop=True)
                if work == "K":
                    pe.wait_ge(s_er, 1)
                    pe.wait_ge(s_cb, 1)
                    pe.matmul(bank[:, 0:(T + 1) * NE], CB, EARLIER[:, :], start=True, stop=False)
                    last = pe.matmul(bank[:, 0:T * NE], TRI[:, :], LG[:, 3, :, :].rearrange("p t e -> p (t e)"),
                                     start=False, stop=True)
                last.then_inc(s_ff, 1)

            for s in range(HEAD):
                stage(0, 0, s, False)
            with pe.Fori(0, PAIRS) as i:
                stream(i, False, stage)
            stream(PAIRS, True, stage)

            def side(j):
                if j not in SIDE_AT:
                    return
                work, k = SIDE_AT[j]
                use = SIDE_USE[work, k]
                bank = PS[:, 6 + use % 2, :]
                if use == 1:
                    pe.wait_ge(s_tr, 1 + USES)
                if use >= 2:
                    before, n = list(SIDE_AT.values())[use - 2]
                    pe.wait_ge({"X": s_xe, "L": s_lt, "S": s_so}[before], n + 1)
                for i in range(min(BPC, NT - BPC * k)):
                    t = BPC * k + i
                    at = bank[:, i * P:(i + 1) * P]
                    if work == "X":
                        last = pe.transpose(at, XS[:, t, 0:P], ID[:, :])
                    if work == "L":
                        pe.wait_ge(s_ln, t + 1)
                        last = pe.transpose(at, LNO[:, t, :], ID[:, :])
                    if work == "S":
                        pe.wait_ge(s_lt, k + 1)
                        last = pe.matmul(at, LNT[:, t * P:(t + 1) * P], WT[:, 3, :], start=True, stop=True)
                last.then_inc(s_sf, 1)

            def up(j):
                e = pe.value_load(EID[0:1, j:j + 1], min_val=0, max_val=NE - 1)
                if j % BPC == 0:
                    pe.wait_ge(s_xe, j // BPC + 1)
                if j >= 2:
                    pe.wait_ge(s_ua, j - 1)
                bank = PS[:, j % 2, :]
                pe.matmul(bank, TE[:, j, :], B12[:, 0:4 * P], start=True, stop=False)
                pe.matmul(bank, XG[:, j * P:(j + 1) * P], W1S[:, bass.ds(e, 1), :].rearrange("p a n -> p (a n)"),
                          start=False, stop=True).then_inc(s_u, 1)
                return e

            def turn_act(j):
                pe.wait_ge(s_ua, j + 1)
                if j >= 2:
                    pe.wait_ge(s_uc, j - 1)
                for m in range(2):
                    last = pe.transpose(PS[:, 2 + j % 2, m * P:(m + 1) * P], UA[:, j % 2, m * P:(m + 1) * P], ID[:, :])
                last.then_inc(s_ut, 1)

            def down(j, e):
                pe.wait_ge(s_uc, j + 1)
                if j >= 2:
                    pe.wait_ge(s_ye, j - 1)
                bank = PS[:, 4 + j % 2, 0:P]
                pe.matmul(bank, TE[:, j, :], B12[:, 4 * P:5 * P], start=True, stop=False)
                for m in range(2):
                    last = pe.matmul(bank, UT[:, j % 2, m * P:(m + 1) * P],
                                     W2S[:, bass.ds(e, 1), m, :].rearrange("p a n -> p (a n)"),
                                     start=False, stop=m == 1)
                last.then_inc(s_y, 1)

            pe.wait_ge(s_oe, 1 + NC * NG)
            pe.wait_ge(s_fu, len(FFN_AT))
            pe.wait_ge(s_xs, 16)
            side(-1)
            pe.wait_ge(s_eid, 1)
            pe.wait_ge(s_bs, 16 * PARTS)
            pe.wait_ge(s_moe, 32)
            experts = []
            for j in range(NT + 2):
                if j < NT:
                    experts.append(up(j))
                side(j)
                if 1 <= j <= NT:
                    turn_act(j - 1)
                if j >= 2:
                    down(j - 2, experts[j - 2])

        @block.vector
        def _(dve):
            n = [0]

            def link(ins):
                n[0] += 1
                ins.then_inc(s_v, 1)
                dve.wait_ge(s_v, n[0])

            dve.memset(WG[:, :], 0.0).then_inc(s_wgz, 1)
            link(dve.memset(MP[:, :, :], NEG))
            dve.sem_inc(s_pv, PV0)
            dve.sem_inc(s_mr, 2)
            dve.sem_inc(s_oe, 1)
            dve.sem_inc(s_tr, 1)

            def moments(src, landed=None):
                for t in range(T):
                    if landed and t % BPC == 0:
                        dve.wait_ge(landed[t // BPC], 16)
                    last = dve.bn_stats(BN[:, t, :], src(t))
                link(last)
                for t in range(T):
                    last = dve.bn_aggr(MV[:, t, :], BN[:, t, :])
                link(last)

            moments(lambda t: XN[:, t, :], s_x)
            dve.tensor_scalar(ST[:, 0, :], MV[:, :, 1], 1e-5, None, ALU.add).then_inc(s_var, 1)
            dve.wait_ge(s_std, 1)
            link(dve.reciprocal(ST[:, 1, :], ST[:, 1, :]))
            for t in range(T):
                dve.tensor_scalar(XN[:, t, :], XN[:, t, :], MV[:, t, 0:1], ST[:, 1, t:t + 1],
                                  ALU.subtract, ALU.mult).then_inc(s_xn, 1)
            link(dve.tensor_tensor(ST[:, 2, :], ST[:, 1, :], ST[:, 1, :], ALU.mult))
            link(dve.tensor_tensor(ST[:, 2, :], ST[:, 2, :], MV[:, :, 1], ALU.mult))
            dve.tensor_scalar(ST[:, 2, :], ST[:, 2, :], 1e-6, None, ALU.add).then_inc(s_var, 1)
            dve.wait_ge(s_std, 2)
            link(dve.reciprocal(ST[:, 3, :], ST[:, 3, :]))

            dve.wait_ge(s_ft, U_W + 1)
            for a in range(2):
                dve.tensor_copy(WT[:, a, :].rearrange("p (g d h) -> p g h d", g=NA, h=HG),
                                PS[:, U_W, a * P:(a + 1) * P].rearrange("p (g h d) -> p g h d", g=NA, h=HG))
            dve.tensor_copy(WT[:, 2:4, :].rearrange("p a n -> p (a n)"), PS[:, U_W, 2 * P:4 * P]).then_inc(s_fr, 1)
            dve.wait_ge(s_ft, U_W + 2)
            dve.tensor_copy(COLS[:, :], PS[:, U_W + 1, 0:NROWS]).then_inc(s_fr, 1)
            dve.wait_ge(s_fr, 2)
            dve.tensor_copy(WN[:, 0:P], WT[:, 2, :])
            dve.tensor_scalar(HBG[:, :], COLS[:, R_BG:R_BG + 1], 0.5, None, ALU.mult).then_inc(s_ng, 1)
            dve.tensor_scalar(KNS[:, :], COLS[:, R_KN:R_KN + 1], SCALE, None, ALU.mult)
            dve.tensor_scalar(WN[:, P:P + 192], WQKV[:, :], COLS[:, R_LN1:R_LN1 + 1], None, ALU.mult)\
               .then_inc(s_wn, 1)

            link(dve.tensor_reduce(QKM[:, :], QKN[:, :, :], AX, ALU.max, apply_absolute_value=True))
            link(dve.tensor_tensor(QKM[:, 0:1], QKM[:, 0:1], QKM[:, 1:2], ALU.mult))
            link(dve.tensor_scalar(QKM[:, 1:2], QKM[:, 0:1], -SCALE * HD, BOUND, ALU.mult, ALU.add))
            link(dve.tensor_scalar(QKM[:, 0:1], QKM[:, 1:2], 0.0, None, ALU.min))
            link(dve.tensor_copy(NMR[:, 0, 0:1], QKM[:, 0:1]))
            link(dve.tensor_tensor(NMR[:, 1, 0:1], QKM[:, 0:1], NMR[:, 0, 0:1], ALU.subtract))
            for i in range(2):
                r = slice(i * HG * T, (i + 1) * HG * T)
                last = dve.tensor_copy(MROW[r, :], NMR[r, i, 0:1].broadcast_to([HG * T, P]))
            last.then_inc(s_cr, 1)

            def factor(n):
                return (1.0, SCALE, COLS[:, R_QN:R_QN + 1], KNS[:, 0:1])[n // 4]

            def remainder(n):
                if n >= 2:
                    dve.wait_ge(s_lo, n - 1)
                dve.wait_ge(s_hi, n + 1)
                dve.scalar_tensor_tensor(RES[:, n % 2, :], PS[:, source_use(n) % 8, :], factor(n),
                                         SP3[:, n % SLOTS, 0, :], ALU.mult, ALU.subtract).then_inc(s_res, 1)

            def third_part(n):
                dve.wait_ge(s_mid, n + 1)
                dve.tensor_tensor(SP3[:, n % SLOTS, 2, :], RES[:, n % 2, :], SP3[:, n % SLOTS, 1, :], ALU.subtract)\
                   .then_inc(s_lo, 1)

            def split(sources):
                for n in sources:
                    remainder(n)
                    if n > sources[0]:
                        third_part(n - 1)
                    dve.wait_ge(s_res, n + 1)
                    dve.sem_inc(s_fr, 1)
                third_part(sources[-1])

            split(range(NSRC // 2))
            dve.wait_ge(s_rw, 16 * len(rope_weights))
            for t in range(T):
                dve.wait_ge(s_vc, t + 1)
                dve.scalar_tensor_tensor(QKV1[:, t, :], PS[:, (U_P + t) % 8, P:P + 192], ST[:, 3, t:t + 1],
                                         QKVB[:, :], ALU.mult, ALU.add).then_inc(s_fr, 1)
            dve.wait_ge(s_fr, reads(U_F - 1))

            qk = QKV1[:, :, 0:160].rearrange("p t (h d) -> p t h d", d=HD)
            r1, tmp = RT[:, :, :, 0:h2], RTMP[:, 0, :, :, :]
            hs = HS[:, 0, :].rearrange("p (t h) -> p t h", t=T)
            link(dve.tensor_tensor(r1, qk[:, :, :, 0:h2], rope(COS), ALU.mult))
            link(dve.tensor_tensor(tmp, qk[:, :, :, h2:HD], rope(SIN), ALU.mult))
            dve.wait_ge(s_sq, 1)
            link(dve.tensor_reduce(hs, SQF[:, :, :, :], AX, ALU.add))
            dve.tensor_scalar(HS[:, 0, :], HS[:, 0, :], 1.0 / HD, 1e-6, ALU.mult, ALU.add).then_inc(s_var, 1)
            link(dve.tensor_tensor(r1, r1, tmp, ALU.subtract))
            dve.wait_ge(s_std, 3)
            link(dve.reciprocal(HS[:, 2, :], HS[:, 1, :]))
            dve.wait_ge(s_r2, 1)
            rr = HS[:, 2, :].rearrange("p (t h) -> p t h", t=T).unsqueeze(3).broadcast_to([P, T, NH + NKV, HD])
            dve.tensor_tensor(RT[:, :, NH:NH + NKV, :], RT[:, :, NH:NH + NKV, :], rr[:, :, NH:NH + NKV, :],
                              ALU.mult).then_inc(s_qf, 1)
            for g in range(NA):
                gh = slice(g * HG, (g + 1) * HG)
                dve.tensor_tensor(QF[:, 0, :, g * HG * HD:(g + 1) * HG * HD].rearrange("p t (d h) -> p t h d", h=HG),
                                  RT[:, :, gh, :], rr[:, :, gh, :], ALU.mult).then_inc(s_qf, 1)
            split(range(NSRC // 2, NSRC))

            def max_unit(i, item, hh, peeled):
                qb, kc = ITEMS[item]
                u = item * HG + hh
                w = item_width(item)
                dve.wait_ge(s_mm, UNITS * i + u + 1)
                dve.reduce_max(MP[:, hh * T + qb, kc:kc + 1], PS[:, unit_bank(u, peeled), 0:w], AX).then_inc(s_mr, 1)

            def shift_parts(i):
                dve.wait_ge(s_mr, 2 + UNITS * (i + 1))
                dve.tensor_reduce(NM[:, :], MP[:, :, :], AX, ALU.max, negate=True).then_inc(s_ch, 1)
                dve.wait_ge(s_ch, 2 * i + 1)
                dve.tensor_copy(NMR[:, 0, :], NM[:, :]).then_inc(s_ch, 1)
                dve.wait_ge(s_ch, 2 * i + 2)
                dve.tensor_tensor(NMR[:, 1, :], NM[:, :], NMR[:, 0, :], ALU.subtract).then_inc(s_nm, 1)

            def shift_read(i, peeled):
                dve.wait_ge(s_t, shift_use(i, peeled) + 1)
                dve.wait_ge(s_shw, 16 * (NA + i))
                bank = PS[:, turn_bank("shift", 0, peeled), :].bitcast(BF16)
                dve.tensor_copy(MROW[:, :], bank[:, 0:P]).then_inc(s_tr, 1)

            def copy_out(i, side, c):
                dve.wait_ge(s_pv, PV0 + NS * (2 * i + side) + chunk_end(c) + 1)
                dve.tensor_copy(OT[:, c % 2, :], PS[:, 6, :]).then_inc(s_oe, 1)

            def normalise(i, side, c, peeled):
                dve.wait_ge(s_t, turn_use(i, side, c, peeled) + 1)
                bank = PS[:, turn_bank(("turn", c), side, peeled), :]
                o = bank.rearrange("p (k h n) -> p k h n", k=BPC, h=HG)
                dve.reciprocal(RL[:, c % 2, :, :], o[:, :, :, HD]).then_inc(s_rl, 1)
                dve.wait_ge(s_rl, NC * (2 * i + side) + ORDER.index(c) + 1)
                at = NA + i if peeled and side else place(i, side)
                dve.tensor_tensor(
                    AO[:, bass.ds(at, 1), 4 * c:4 * c + 4, :].rearrange("p o t (h d) -> p (o t) h d", h=HG),
                    o[:, :, :, 0:HD], RL[:, c % 2, :, :].unsqueeze(3).broadcast_to([P, BPC, HG, HD]),
                    ALU.mult).then_inc(s_tr, 1)

            def stage(i, side, s, peeled):
                parts = units_at(maxima_of(peeled, side), s) if side < 2 else ((), (), ())
                for item, hh in (*parts[0], *parts[1]):
                    max_unit(i, item, hh, peeled)
                side_v, v = behind(side, s, LAG)
                if ending(v) is not None and side_v >= 0:
                    copy_out(i, side_v, ending(v))
                side_t, t = behind(side, s, LAG + 1)
                if ending(t) is not None and side_t >= 0:
                    normalise(i, side_t, ending(t), peeled)
                for item, hh in parts[2]:
                    max_unit(i, item, hh, peeled)
                if s == SHIFT_PARTS and takes_shift(peeled, side):
                    shift_parts(i)
                if s == SHIFT_TURN and takes_shift(peeled, side):
                    shift_read(i, peeled)
                if peeled and side == 1:
                    ffn(s)

            def ffn(s):
                work, k = FFN_AT.get(s, (None, 0))
                use = FFN_USE.get((work, k), 0)
                at, tiles, bank = slice(k * CH, (k + 1) * CH), slice(BPC * k, BPC * (k + 1)), PS[:, 4 + use % 2, :]
                gate, n = FFN_AT.get(s - 1, (None, 0))
                if gate == "G":
                    ge = GE[:, n * CH:(n + 1) * CH]
                    dve.wait_ge(s_sig, n + 1)
                    dve.tensor_scalar(ge, ge, 0.5, 0.5, ALU.mult, ALU.add).then_inc(s_fu, 1)
                if work not in (None, "G"):
                    dve.wait_ge(s_ff, use + 1)
                if work == "O":
                    dve.tensor_copy(O1T[:, at], bank).then_inc(s_fu, 1)
                if gate == "G":
                    o = O1T[:, n * CH:(n + 1) * CH]
                    dve.wait_ge(s_fu, FFN_USE["G", n] + 1)
                    dve.tensor_tensor(o, o, ge, ALU.mult).then_inc(s_gt, 1)
                if work == "C":
                    dve.tensor_scalar(TOK[:, :], J128[:, 0:T], bank[:, 0:1], 1.0, ALU.add, ALU.add)
                    dve.tensor_scalar(SPARE[:, :], J128[:, :], bank[:, 0:1], float(S + 1), ALU.add, ALU.add)\
                       .then_inc(s_fu, 1)
                if s == 3:
                    dve.wait_ge(s_bl, 32)
                    link(dve.tensor_copy(BP[:, 0, :], BF))
                    link(dve.tensor_tensor(BF, BF, BP[:, 0, :], ALU.subtract))
                    link(dve.tensor_copy(BP[:, 1, :], BF))
                    dve.tensor_tensor(BP[:, 2, :], BF, BP[:, 1, :], ALU.subtract).then_inc(s_bp, 1)
                if work == "W":
                    dve.wait_ge(s_xb, T)
                    dve.tensor_tensor(X2[:, tiles, :].rearrange("p t n -> p (t n)"), bank,
                                      XN[:, tiles, :].rearrange("p t n -> p (t n)"), ALU.add).then_inc(s_fu, 1)
                    dve.wait_ge(s_fu, use + 1)
                    link(dve.tensor_tensor(SQ[:, tiles, :], X2[:, tiles, :], X2[:, tiles, :], ALU.mult))
                    link(dve.tensor_reduce(ST[:, 6, tiles], SQ[:, tiles, :], AX, ALU.add))
                    dve.tensor_scalar(ST[:, 6, tiles], ST[:, 6, tiles], 1.0 / P, 1e-6, ALU.mult, ALU.add)\
                       .then_inc(s_ms, 1)
                if gate == "W":
                    dve.wait_ge(s_rs, n + 1)
                    for t in range(BPC * n, BPC * (n + 1)):
                        dve.tensor_copy(H2[:, t, P:ROW], TOK[:, t:t + 1])
                        dve.tensor_scalar(H2[:, t, 0:P], X2[:, t, :], ST[:, 7, t:t + 1], None, ALU.mult)\
                           .then_inc(s_h2, 1)
                if work == "H":
                    dve.tensor_scalar(XT[:, at], bank, COLS[:, R_LN2:R_LN2 + 1], None, ALU.mult).then_inc(s_fu, 1)
                if work == "R":
                    lg = LG[:, 0, :, :]
                    brb = BRB[:, :].unsqueeze(1).broadcast_to([P, T, NE])
                    rank = RANK[:, :].unsqueeze(1).broadcast_to([P, T, NE])
                    dve.tensor_tensor(lg, bank[:, 0:T * NE].rearrange("p (t e) -> p t e", t=T), brb, ALU.add)\
                       .then_inc(s_fu, 1)
                    dve.wait_ge(s_fu, use + 1)
                    link(dve.tensor_reduce(MX[:, 0, :], lg, AX, ALU.max))
                    mx = MX[:, 0, :].unsqueeze(2).broadcast_to([P, T, NE])
                    link(dve.tensor_tensor(LG[:, 1, :, :], lg, mx, ALU.is_equal))
                    link(dve.tensor_tensor(LG[:, 2, :, :], LG[:, 1, :, :], rank, ALU.mult))
                    link(dve.tensor_reduce(MX[:, 1, :], LG[:, 2, :, :], AX, ALU.max))
                    mx1 = MX[:, 1, :].unsqueeze(2).broadcast_to([P, T, NE])
                    dve.tensor_tensor(LG[:, 3, :, :], LG[:, 2, :, :], mx1, ALU.is_equal).then_inc(s_oh, 1)
                if work == "N":
                    dve.tensor_copy(CB, bank[:, 0:1].broadcast_to([P, P])).then_inc(s_fu, 1)
                    dve.wait_ge(s_fu, use + 1)
                    dve.sem_inc(s_cb, 1)
                if work == "K":
                    count, tiles_, first, end = (CNT[:, a, :] for a in range(4))
                    link(dve.tensor_copy(count, bank[:, T * NE:(T + 1) * NE]))
                    more = LG[:, 1, :, :].rearrange("p t e -> p (t e)").rearrange("p (e k) -> p e k", e=NE)
                    link(dve.tensor_tensor(more, count.unsqueeze(2).broadcast_to([P, NE, T]),
                                           J128[:, 0:T].unsqueeze(1).broadcast_to([P, NE, T]), ALU.is_gt))
                    link(dve.tensor_reduce(tiles_, more, AX, ALU.add))
                    before = LG[:, 2, 0:NE, :]
                    link(dve.tensor_tensor(before, tiles_.unsqueeze(1).broadcast_to([P, NE, NE]), BEFORE[:, :, :],
                                           ALU.mult))
                    link(dve.tensor_reduce(first, before, AX, ALU.add))
                    link(dve.tensor_tensor(end, first, tiles_, ALU.add))
                    link(dve.tensor_scalar(first, first, float(P), None, ALU.mult))
                    dve.tensor_tensor(LG[:, 0, :, :], bank[:, 0:T * NE].rearrange("p (t e) -> p t e", t=T),
                                      first.unsqueeze(1).broadcast_to([P, T, NE]), ALU.add).then_inc(s_fu, 1)
                    dve.wait_ge(s_fu, use + 1)
                    link(dve.tensor_tensor(LG[:, 0, :, :], LG[:, 0, :, :], LG[:, 3, :, :], ALU.mult))
                    link(dve.tensor_reduce(POSF[:, :], LG[:, 0, :, :], AX, ALU.add))
                    dve.tensor_copy(POS[:, :], POSF[:, :]).then_inc(s_pos, 1)
                    link(dve.tensor_tensor(EQ, TILE[:, :].unsqueeze(2).broadcast_to([P, NT, NE]),
                                           end.unsqueeze(1).broadcast_to([P, NT, NE]), ALU.is_ge))
                    link(dve.tensor_reduce(EIDF[:, :], EQ, AX, ALU.add))
                    link(dve.tensor_scalar(EIDF[:, :], EIDF[:, :], float(NE - 1), None, ALU.min))
                    link(dve.tensor_copy(EID[:, :], EIDF[:, :]))
                    r = PARTS * NE
                    link(dve.tensor_tensor(EQ[0:r], EIDF[0:r, :].unsqueeze(2).broadcast_to([r, NT, NE]),
                                           TILE[0:r, 0:NE].unsqueeze(1).broadcast_to([r, NT, NE]), ALU.is_equal))
                    link(dve.tensor_tensor(EQ[0:r], EQ[0:r], OWN[:, :].unsqueeze(1).broadcast_to([r, NT, NE]),
                                           ALU.mult))
                    link(dve.tensor_reduce(YIF[0:r, :], EQ[0:r], AX, ALU.add))
                    dve.tensor_copy(TE, YIF[0:r, :].unsqueeze(2).broadcast_to([r, NT, P])).then_inc(s_eid, 1)

            for s in range(HEAD):
                stage(0, 0, s, False)
            with dve.Fori(0, PAIRS) as i:
                stream(i, False, stage)
            stream(PAIRS, True, stage)

            def first_attention(j):
                if 1 <= j <= NC:
                    for t in range(BPC * (j - 1), BPC * j):
                        last = dve.bn_stats(BN[:, t, :], o_first(t))
                    link(last)
                    for t in range(BPC * (j - 1), BPC * j):
                        last = dve.bn_aggr(MV[:, t, :], BN[:, t, :])
                    link(last)
                if j == NC:
                    dve.tensor_scalar(ST[:, 4, :], MV[:, :, 1], 1e-5, None, ALU.add).then_inc(s_var, 1)
                if j == NC + 1:
                    dve.wait_ge(s_std, 4)
                if NC + 1 <= j <= 2 * NC:
                    for t in range(BPC * (j - NC - 1), BPC * (j - NC)):
                        dve.tensor_scalar(LNO[:, t, :].rearrange("p (g n) -> p g n", g=4), o_first(t),
                                          MV[:, t, 0:1], ST[:, 5, t:t + 1], ALU.subtract, ALU.mult).then_inc(s_ln, 1)
                work, k = SIDE_AT.get(j, (None, 0))
                if work == "L":
                    dve.wait_ge(s_sf, SIDE_USE[work, k] + 1)
                    dve.tensor_scalar(LNT[:, k * CH:(k + 1) * CH], PS[:, 6 + SIDE_USE[work, k] % 2, :],
                                      COLS[:, R_GAMMA:R_GAMMA + 1], COLS[:, R_BETA:R_BETA + 1],
                                      ALU.mult, ALU.add).then_inc(s_lt, 1)

            dve.wait_ge(s_tr, 1 + USES)
            dve.wait_ge(s_pv, PV0 + NS * NG)
            dve.wait_ge(s_xs, 16)
            number = XS[:, :, P]
            link(dve.tensor_scalar(YIF[:, :], number, 0.0, None, ALU.is_equal))
            link(dve.tensor_tensor(YIF[:, :], YIF[:, :], SPARE[:, :], ALU.mult))
            link(dve.tensor_tensor(YIF[:, :], YIF[:, :], number, ALU.add))
            link(dve.tensor_scalar(YIF[:, :], YIF[:, :], -1.0, None, ALU.add))
            dve.tensor_copy(YI[:, :], YIF[:, :]).then_inc(s_yi, 1)
            for j in range(NT + 2):
                if j < NT:
                    dve.wait_ge(s_us, j + 1)
                    dve.wait_ge(s_u, j + 1)
                    if j >= 2:
                        dve.wait_ge(s_ut, j - 1)
                    dve.tensor_tensor(UA[:, j % 2, :], PS[:, j % 2, 0:HID], SG[:, j % 2, :], ALU.mult)\
                       .then_inc(s_ua, 1)
                if j >= 2:
                    i = j - 2
                    dve.wait_ge(s_y, i + 1)
                    if i >= YRING:
                        dve.wait_ge(s_ys[i % YRING], 16 * (i // YRING))
                    dve.tensor_copy(YS[:, i % YRING, :], PS[:, 4 + i % 2, 0:P]).then_inc(s_ye, 1)
                first_attention(j)

            dve.wait_ge(s_xr, 16)
            for c in range(NC + 1):
                if c < NC:
                    x2 = X2[:, 4 * c:4 * c + 4, :]
                    dve.wait_ge(s_yl[c], 16)
                    dve.tensor_tensor(x2, x2, YN[:, 4 * c:4 * c + 4, :], ALU.add).then_inc(s_f, 1)
                if c >= 1:
                    tiles = slice(4 * c - 4, 4 * c)
                    rs = RS[:, tiles, :]
                    dve.wait_ge(s_fs, c)
                    dve.wait_ge(s_fm, c)
                    link(dve.tensor_tensor(rs, rs, SO[:, tiles, :], ALU.mult))
                    dve.tensor_tensor(rs, rs, XR[:, tiles, :], ALU.add).then_inc(s_o, 1)


_INS = ['L0_attn_x', 'L0_attn_Wq', 'L0_attn_Wk', 'L0_attn_Wv', 'L0_attn_Wo', 'L0_attn_gamma', 'L0_attn_beta',
        'L0_ffn_ln1_w', 'L0_ffn_ln2_w', 'L0_ffn_Wq', 'L0_ffn_bq', 'L0_ffn_Wk', 'L0_ffn_bk', 'L0_ffn_Wv',
        'L0_ffn_bv', 'L0_ffn_qn_w', 'L0_ffn_kn_w', 'L0_ffn_Wg', 'L0_ffn_bg', 'L0_ffn_Wo', 'L0_ffn_bo',
        'L0_ffn_Wr', 'L0_ffn_br', 'L0_ffn_W1', 'L0_ffn_b1', 'L0_ffn_W2', 'L0_ffn_b2']


def rope_tables():
    inv = (np.float32(1.0) / np.float32(10000.0) ** (np.arange(0, HD, 2, dtype=np.float32) / np.float32(HD)))
    f = np.arange(S, dtype=np.float32)[:, None] * inv.astype(np.float32)[None, :]
    return np.cos(f).astype(np.float32), np.sin(f).astype(np.float32)


def kernel(**inputs):
    import concourse.bacc as _bacc
    from concourse.bass_utils import run_bass_kernel_spmd as _run

    nc = _bacc.Bacc("TRN2", target_bir_lowering=False, num_devices=1)
    cos, sin = rope_tables()
    named = [(name, np.ascontiguousarray(inputs[name])) for name in _INS] + [("rope_cos", cos), ("rope_sin", sin)]
    arrays, args = {}, []
    for name, a in named:
        arrays[f"in_{name}"] = a
        args.append(nc.dram_tensor(f"in_{name}", a.shape, mybir.dt.from_np(a.dtype), kind="ExternalInput").ap())
    out = nc.dram_tensor("out_0", (1, S, P), F32, kind="ExternalOutput").ap()
    build(nc, *args, out)
    r = _run(nc, [arrays], core_ids=[0])
    return r.results[0]["out_0"]
```
